# Optimizing a Trainium2 kernel written in Bass

```python
import numpy as np
import jax
import jax.numpy as jnp

def _softmax(x, axis=-1):
    return jax.nn.softmax(x, axis=axis)

def _gelu(x):
    return jax.nn.gelu(x, approximate=True)

def _silu(x):
    return jax.nn.silu(x)

def _sigmoid(x):
    return jax.nn.sigmoid(x)

def _layernorm(x, axis=-1, eps=1e-05):
    m = jnp.mean(x, axis=axis, keepdims=True)
    v = jnp.var(x, axis=axis, keepdims=True)
    return (x - m) / jnp.sqrt(v + eps)

def _scatter_add(tgt, idx, src, axis=0):
    return tgt.at[idx].add(src)

def _segment_sum(src, seg, n):
    return jax.ops.segment_sum(src, seg, n)
kernel_name = 'mk_gps_d1_gnn_r8_bff0fb'

def setup_inputs(seed: int=0):
    np.random.seed(seed)
    _w = jnp.asarray

    def _rec_inputs():
        import jax
        import jax.numpy as jnp
        _gk = jax.random.key(seed)
        x = -0.0001126 + 1 * jax.random.normal(jax.random.fold_in(_gk, 1), (6250, 256), jnp.float32)
        src = jax.random.randint(jax.random.fold_in(_gk, 2), (200000,), 0, 6250, jnp.int32)
        dst = jax.random.randint(jax.random.fold_in(_gk, 3), (200000,), 0, 6250, jnp.int32)
        _o = jnp.argsort(dst, stable=True)
        src = src[_o]
        dst = dst[_o]
        return (x, src, dst)
    x, src, dst = _rec_inputs()

    def _L0_gnn_setup():
        import jax, jax.numpy as jnp
        import numpy as np
        N, IN_CH, HID, HEADS, OUT_CH, E = (3750, 256, 128, 4, 256, 60000)
        NEG_SLOPE = 0.2

        def gat_conv(x, W, a_src, a_dst, bias, src, dst, heads, out_ch, concat):
            n = x.shape[0]
            h = (x @ W).reshape(n, heads, out_ch)
            al_s = jnp.einsum('nhc,hc->nh', h, a_src)
            al_d = jnp.einsum('nhc,hc->nh', h, a_dst)
            logits = jax.nn.leaky_relu(al_s[src] + al_d[dst], NEG_SLOPE)
            m = jax.lax.stop_gradient(jax.ops.segment_max(logits, dst, num_segments=n))
            e = jnp.exp(logits - m[dst])
            denom = jax.ops.segment_sum(e, dst, num_segments=n)
            alpha = e / denom[dst]
            msg = h[src] * alpha[:, :, None]
            out = jax.ops.segment_sum(msg, dst, num_segments=n)
            out = out.reshape(n, heads * out_ch) if concat else out.mean(axis=1)
            return out + bias
        key = jax.random.key(seed)
        ks = jax.random.split(key, 12)
        s = lambda fin: 1.0 / np.sqrt(fin)
        return {'x': jax.random.normal(ks[0], (N, IN_CH), jnp.float32), 'edge_index': jax.random.randint(ks[1], (2, E), 0, N, jnp.int32), 'W1': jax.random.normal(ks[2], (IN_CH, HEADS * HID), jnp.float32) * s(IN_CH), 'a_src1': jax.random.normal(ks[3], (HEADS, HID), jnp.float32) * s(HID), 'a_dst1': jax.random.normal(ks[4], (HEADS, HID), jnp.float32) * s(HID), 'b1': jnp.zeros((HEADS * HID,), jnp.float32), 'prelu_w': jnp.asarray(0.25, jnp.float32), 'W2': jax.random.normal(ks[5], (HEADS * HID, OUT_CH), jnp.float32) * s(HEADS * HID), 'a_src2': jax.random.normal(ks[6], (1, OUT_CH), jnp.float32) * s(OUT_CH), 'a_dst2': jax.random.normal(ks[7], (1, OUT_CH), jnp.float32) * s(OUT_CH), 'b2': jnp.zeros((OUT_CH,), jnp.float32)}
    _L0_gnn_all = _L0_gnn_setup()
    _L0_gnn_in = {k: v for k, v in _L0_gnn_all.items() if k in ('W1', 'a_src1', 'a_dst1', 'b1', 'prelu_w', 'W2', 'a_src2', 'a_dst2', 'b2')}
    del _L0_gnn_all

    def _L0_mix_setup():
        import jax, jax.numpy as jnp
        import numpy as np
        import math
        EMBED = 256
        HEADS = 4
        HEAD_DIM = EMBED // HEADS
        OUT_DIM = 256
        LN_EPS = 1e-05

        def _qkv_init(key):
            spread = math.sqrt(3.0 / EMBED)
            gain, delta = (0.01, 0.01)
            w = jax.random.uniform(key, (EMBED, EMBED), minval=-spread, maxval=spread) * gain
            return w + delta * jnp.eye(EMBED, dtype=w.dtype)

        def _layer_norm(x, g, b):
            mu = jnp.mean(x, axis=-1, keepdims=True)
            var = jnp.mean(jnp.square(x - mu), axis=-1, keepdims=True)
            return (x - mu) * jax.lax.rsqrt(var + LN_EPS) * g + b

        def _split_heads(x, B, S):
            return x.reshape(B, S, HEADS, HEAD_DIM).transpose(0, 2, 1, 3)
        key = jax.random.key(seed)
        ks = jax.random.split(key, 6)
        seq = jax.random.normal(ks[0], (4, 1024, EMBED), dtype=jnp.float32)
        wq = _qkv_init(ks[1])
        wk = _qkv_init(ks[2])
        wv = _qkv_init(ks[3])
        bound = 1.0 / math.sqrt(EMBED)
        wo = jax.random.uniform(ks[4], (OUT_DIM, EMBED), minval=-bound, maxval=bound)
        bo = jax.random.uniform(ks[5], (OUT_DIM,), minval=-bound, maxval=bound)
        ln_k_g = jnp.ones((HEAD_DIM,), jnp.float32)
        ln_k_b = jnp.zeros((HEAD_DIM,), jnp.float32)
        ln_v_g = jnp.ones((HEAD_DIM,), jnp.float32)
        ln_v_b = jnp.zeros((HEAD_DIM,), jnp.float32)
        return {'seq': seq, 'wq': wq, 'wk': wk, 'wv': wv, 'wo': wo, 'bo': bo, 'ln_k_g': ln_k_g, 'ln_k_b': ln_k_b, 'ln_v_g': ln_v_g, 'ln_v_b': ln_v_b}
    _L0_mix_all = _L0_mix_setup()
    _L0_mix_in = {k: v for k, v in _L0_mix_all.items() if k in ('wq', 'wk', 'wv', 'wo', 'bo', 'ln_k_g', 'ln_k_b', 'ln_v_g', 'ln_v_b')}
    del _L0_mix_all

    def _L0_ffn_setup():
        import jax, jax.numpy as jnp
        import numpy as np
        TOP_K = 2
        key = jax.random.key(seed)
        ks = jax.random.split(key, 4)
        B, L, D, H, E = (8, 512, 256, 1024, 8)
        s = 0.02
        return {'x': jax.random.normal(ks[0], (B, L, D), jnp.float32), 'Wg': jax.random.normal(ks[1], (D, E), jnp.float32) * s, 'bg': jnp.zeros((E,), jnp.float32), 'W1': jax.random.normal(ks[2], (E, D, H), jnp.float32) * s, 'b1': jnp.zeros((E, H), jnp.float32), 'W2': jax.random.normal(ks[3], (E, H, D), jnp.float32) * s, 'b2': jnp.zeros((E, D), jnp.float32)}
    _L0_ffn_all = _L0_ffn_setup()
    _L0_ffn_in = {k: v for k, v in _L0_ffn_all.items() if k in ('Wg', 'bg', 'W1', 'b1', 'W2', 'b2')}
    del _L0_ffn_all
    return {'x': x, 'src': src, 'dst': dst, 'L0_gnn_W1': _L0_gnn_in['W1'], 'L0_gnn_a_src1': _L0_gnn_in['a_src1'], 'L0_gnn_a_dst1': _L0_gnn_in['a_dst1'], 'L0_gnn_b1': _L0_gnn_in['b1'], 'L0_gnn_prelu_w': _L0_gnn_in['prelu_w'], 'L0_gnn_W2': _L0_gnn_in['W2'], 'L0_gnn_a_src2': _L0_gnn_in['a_src2'], 'L0_gnn_a_dst2': _L0_gnn_in['a_dst2'], 'L0_gnn_b2': _L0_gnn_in['b2'], 'L0_mix_wq': _L0_mix_in['wq'], 'L0_mix_wk': _L0_mix_in['wk'], 'L0_mix_wv': _L0_mix_in['wv'], 'L0_mix_wo': _L0_mix_in['wo'], 'L0_mix_bo': _L0_mix_in['bo'], 'L0_mix_ln_k_g': _L0_mix_in['ln_k_g'], 'L0_mix_ln_k_b': _L0_mix_in['ln_k_b'], 'L0_mix_ln_v_g': _L0_mix_in['ln_v_g'], 'L0_mix_ln_v_b': _L0_mix_in['ln_v_b'], 'L0_ffn_Wg': _L0_ffn_in['Wg'], 'L0_ffn_bg': _L0_ffn_in['bg'], 'L0_ffn_W1': _L0_ffn_in['W1'], 'L0_ffn_b1': _L0_ffn_in['b1'], 'L0_ffn_W2': _L0_ffn_in['W2'], 'L0_ffn_b2': _L0_ffn_in['b2']}

def reference(x, src, dst, L0_gnn_W1, L0_gnn_a_src1, L0_gnn_a_dst1, L0_gnn_b1, L0_gnn_prelu_w, L0_gnn_W2, L0_gnn_a_src2, L0_gnn_a_dst2, L0_gnn_b2, L0_mix_wq, L0_mix_wk, L0_mix_wv, L0_mix_wo, L0_mix_bo, L0_mix_ln_k_g, L0_mix_ln_k_b, L0_mix_ln_v_g, L0_mix_ln_v_b, L0_ffn_Wg, L0_ffn_bg, L0_ffn_W1, L0_ffn_b1, L0_ffn_W2, L0_ffn_b2):
    import jax
    import jax.numpy as jnp

    def _L0_gnn_ref(x, edge_index, W1, a_src1, a_dst1, b1, prelu_w, W2, a_src2, a_dst2, b2):
        import jax, jax.numpy as jnp
        import numpy as np
        N, IN_CH, HID, HEADS, OUT_CH, E = (3750, 256, 128, 4, 256, 60000)
        NEG_SLOPE = 0.2

        def gat_conv(x, W, a_src, a_dst, bias, src, dst, heads, out_ch, concat):
            n = x.shape[0]
            h = (x @ W).reshape(n, heads, out_ch)
            al_s = jnp.einsum('nhc,hc->nh', h, a_src)
            al_d = jnp.einsum('nhc,hc->nh', h, a_dst)
            logits = jax.nn.leaky_relu(al_s[src] + al_d[dst], NEG_SLOPE)
            m = jax.lax.stop_gradient(jax.ops.segment_max(logits, dst, num_segments=n))
            e = jnp.exp(logits - m[dst])
            denom = jax.ops.segment_sum(e, dst, num_segments=n)
            alpha = e / denom[dst]
            msg = h[src] * alpha[:, :, None]
            out = jax.ops.segment_sum(msg, dst, num_segments=n)
            out = out.reshape(n, heads * out_ch) if concat else out.mean(axis=1)
            return out + bias
        n = x.shape[0]
        loop = jnp.arange(n, dtype=edge_index.dtype)
        src = jnp.concatenate([edge_index[0], loop])
        dst = jnp.concatenate([edge_index[1], loop])
        h = gat_conv(x, W1, a_src1, a_dst1, b1, src, dst, HEADS, HID, concat=True)
        h = jnp.where(h >= 0, h, prelu_w * h)
        z = gat_conv(h, W2, a_src2, a_dst2, b2, src, dst, 1, OUT_CH, concat=False)
        return z

    def _L0_mix_ref(seq, wq, wk, wv, wo, bo, ln_k_g, ln_k_b, ln_v_g, ln_v_b):
        import jax, jax.numpy as jnp
        import numpy as np
        import math
        EMBED = 256
        HEADS = 4
        HEAD_DIM = EMBED // HEADS
        OUT_DIM = 256
        LN_EPS = 1e-05

        def _qkv_init(key):
            spread = math.sqrt(3.0 / EMBED)
            gain, delta = (0.01, 0.01)
            w = jax.random.uniform(key, (EMBED, EMBED), minval=-spread, maxval=spread) * gain
            return w + delta * jnp.eye(EMBED, dtype=w.dtype)

        def _layer_norm(x, g, b):
            mu = jnp.mean(x, axis=-1, keepdims=True)
            var = jnp.mean(jnp.square(x - mu), axis=-1, keepdims=True)
            return (x - mu) * jax.lax.rsqrt(var + LN_EPS) * g + b

        def _split_heads(x, B, S):
            return x.reshape(B, S, HEADS, HEAD_DIM).transpose(0, 2, 1, 3)
        B, S, _ = seq.shape
        q = _split_heads(seq @ wq.T, B, S)
        k = _split_heads(seq @ wk.T, B, S)
        v = _split_heads(seq @ wv.T, B, S)
        k = _layer_norm(k, ln_k_g, ln_k_b)
        v = _layer_norm(v, ln_v_g, ln_v_b)
        kv = jnp.einsum('bhsd,bhse->bhde', k, v) / S
        ga = jnp.einsum('bhsd,bhde->bhse', q, kv)
        ga = ga.transpose(0, 2, 1, 3).reshape(B, S, EMBED)
        return ga @ wo.T + bo

    def _L0_ffn_ref(x, Wg, bg, W1, b1, W2, b2):
        import jax, jax.numpy as jnp
        import numpy as np
        TOP_K = 2
        B, L, D = x.shape
        E = W1.shape[0]
        xf = x.reshape(-1, D)
        gate_logits = xf @ Wg + bg
        top_w, top_i = jax.lax.top_k(gate_logits, TOP_K)
        top_w = jax.nn.softmax(top_w, axis=-1)
        w_dense = jnp.sum(jax.nn.one_hot(top_i, E, dtype=xf.dtype) * top_w[..., None], axis=1)
        out = jnp.zeros_like(xf)
        for e in range(E):
            h = jax.nn.gelu(xf @ W1[e] + b1[e], approximate=False)
            out = out + w_dense[:, e:e + 1] * (h @ W2[e] + b2[e])
        return out.reshape(B, L, D)
    edge_index = jnp.stack([src, dst])
    xn = _layernorm(x, axis=-1)
    x = x + _L0_gnn_ref(xn, edge_index, L0_gnn_W1, L0_gnn_a_src1, L0_gnn_a_dst1, L0_gnn_b1, L0_gnn_prelu_w, L0_gnn_W2, L0_gnn_a_src2, L0_gnn_a_dst2, L0_gnn_b2) + _L0_mix_ref(xn[None], L0_mix_wq, L0_mix_wk, L0_mix_wv, L0_mix_wo, L0_mix_bo, L0_mix_ln_k_g, L0_mix_ln_k_b, L0_mix_ln_v_g, L0_mix_ln_v_b)[0]
    x = x + _L0_ffn_ref(_layernorm(x, axis=-1)[None], L0_ffn_Wg, L0_ffn_bg, L0_ffn_W1, L0_ffn_b1, L0_ffn_W2, L0_ffn_b2)[0]
    return x

_drawn_inputs = setup_inputs


def setup_inputs(seed=0):
    import zlib

    import numpy as np

    out = dict(_drawn_inputs(seed))
    spreads = {'L0_gnn_b1': (0.0, 0.1),
     'L0_gnn_b2': (0.0, 0.1),
     'L0_mix_ln_k_g': (1.0, 0.6),
     'L0_mix_ln_k_b': (0.0, 0.8),
     'L0_mix_ln_v_g': (1.0, 0.6),
     'L0_mix_ln_v_b': (0.0, 0.8),
     'L0_ffn_bg': (0.0, 0.283),
     'L0_ffn_b1': (0.0, 0.308),
     'L0_ffn_b2': (0.0, 0.1)}
    factors = {'L0_gnn_a_dst1': 24.208,
     'L0_gnn_a_src2': 21.594,
     'L0_gnn_a_dst2': 64.0,
     'L0_mix_wq': 6.863,
     'L0_mix_wk': 7.263,
     'L0_mix_wv': 7.437,
     'L0_mix_wo': 6.791,
     'L0_mix_bo': 3.206}
    for name, (base, spread) in spreads.items():
        noise = np.random.default_rng([zlib.crc32(name.encode()), seed]).standard_normal(out[name].shape)
        drawn = base * np.exp(spread * noise) if base else spread * noise
        out[name] = jnp.asarray(drawn.astype(out[name].dtype))
    for name, factor in factors.items():
        out[name] = (out[name] * factor).astype(out[name].dtype)
    return out
```

```python
from contextlib import ExitStack

import concourse.bass as bass
from concourse import mybir

ALU = mybir.AluOpType
ACT = mybir.ActivationFunctionType
F32 = mybir.dt.float32
I32 = mybir.dt.int32
AX_X = mybir.AxisListType.X

P = 128
N = 6250
D = 256
DK = D // P
NT = -(-N // P)
NP = NT * P
LAST = N - (NT - 1) * P
U = 7
TRIPS = NT // U
assert TRIPS * U == NT
EDGES = 200000
C = -(-EDGES // P)
EP = C * P
HEADS1 = 4
F1 = 512
MIX_HEADS = 8
HD = 64
EPS = 1e-5
SLOPE = 0.2
BIG = 1e30
W = 64
NW = NP // W
STEPS = C + NW - 1
SJ = -(-STEPS // P)
SP = SJ * P
G = 8
OUT_OF_RANGE = 1 << 20
NEXP = 8
HID = 1024
TT = (2 * N + NEXP * (P - 1)) // P
SLOTS = TT * P


class Memory:

    program = None

    def __init__(self, nc, ctx, stage):
        self.nc, self.ctx, self.stage = nc, ctx, stage
        self.sems = []
        self.starts = []
        Memory.program = Memory.program or ctx

    def sb(self, name, shape, dt=F32):
        return self.ctx.enter_context(self.nc.sbuf_tensor(f"{self.stage}_{name}", shape, dt))

    def ps(self, name, shape, dt=F32):
        return self.ctx.enter_context(self.nc.psum_tensor(f"{self.stage}_{name}", shape, dt))

    def swdge_sem(self, name):
        self.sems.append(self.program.enter_context(self.nc.semaphore(f"{self.stage}_{name}")))
        return self.sems[-1]

    def sem(self, name, starts=0):
        self.sems.append(self.ctx.enter_context(self.nc.semaphore(f"{self.stage}_{name}")))
        self.starts.append((self.sems[-1], starts))
        return self.sems[-1]

    def clear_semaphores(self):
        with self.nc.Block() as block:

            @block.sync
            def _(sp):
                for sem in self.sems:
                    sp.sem_clear(sem)
                for sem, starts in self.starts:
                    if starts:
                        sp.sem_inc(sem, starts)


def after(engine, sem, n):
    engine.wait_ge(sem, n + 1)


def spread(ap, axis, n):
    shape = list(ap.shape)
    return ap.unsqueeze(axis).to_broadcast(shape[:axis] + [n] + shape[axis:])


def constants(nc, k):
    with nc.Block() as block:

        @block.gpsimd
        def _(pool):
            nc.gpsimd.memset(k["ident"][:, :], 0.0)
            nc.gpsimd.memset(k["ones"][:, :], 1.0)
            nc.gpsimd.iota(k["node_i"][:, :], [[P, NT]], base=0, channel_multiplier=1)
            nc.gpsimd.iota(k["count_i"][:, :], [[1, P]], base=0, channel_multiplier=0)
            pool.drain()
            nc.gpsimd.affine_select(out=k["ident"][:, :], in_=k["ident"][:, :], compare_op=ALU.not_equal, fill=1.0,
                                    base=0, pattern=[[-1, P]], channel_multiplier=1)
            nc.gpsimd.tensor_copy(k["node"][:, :], k["node_i"][:, :])
            nc.gpsimd.tensor_copy(k["count"][:, :], k["count_i"][:, :])


def node_pass(nc, k, d):
    with ExitStack() as ctx:
        m = Memory(nc, ctx, "node")
        x = m.sb("x", [P, NT, D])
        w1 = m.sb("w1", [P, DK, F1])
        avec = m.sb("avec", [P, 2 * HEADS1, P])
        aprod = m.sb("aprod", [P, HEADS1, P])
        wa = m.sb("wa", [P, DK, 2 * HEADS1])
        wkv = m.sb("wkv", [P, DK, MIX_HEADS, HD])
        wkv_mean = m.sb("wkv_mean", [P, DK * MIX_HEADS])
        wq = m.sb("wq", [P, DK, D])
        wo = m.sb("wo", [P, DK, D])
        gains = m.sb("gains", [P, 2, HD])
        shifts = m.sb("shifts", [P, 2, HD])
        rbias = m.sb("rbias", [P, 2, D])
        valid = m.sb("valid", [P, NT])
        stats = m.sb("stats", [P, NT, 6])
        mean = m.sb("mean", [P, NT])
        half = m.sb("half", [P, NT])
        var = m.sb("var", [P, NT])
        rstd = m.sb("rstd", [P, NT])
        eps = m.sb("eps", [P, 1])
        xn = m.sb("xn", [P, U, D])
        xT = m.sb("xT", [P, 2, DK, P])
        h_out = m.sb("h_out", [P, U, F1])
        square = m.sb("square", [P, 2, F1])
        ssum = m.sb("ssum", [P, 2, MIX_HEADS])
        sroot = m.sb("sroot", [P, 2, MIX_HEADS])
        srec = m.sb("srec", [P, 2, MIX_HEADS])
        kvn = m.sb("kvn", [P, 2, F1])
        kvg = m.sb("kvg", [P, 2, F1])
        kv = m.sb("kv", [P, U, F1])
        zero = m.sb("zero", [P, D])
        kvT = m.sb("kvT", [P, 2, P])
        kvo = m.sb("kvo", [P, 2, D])
        mix = m.sb("mix", [P, DK, D])
        xin = m.sb("xin", [P, U, D])
        base = m.sb("base", [P, U, D])
        pT = m.ps("pT", [P, 2, 512])
        pH = m.ps("pH", [P, 2, F1])
        pKV = m.ps("pKV", [P, 2, F1])
        pA = m.ps("pA", [P, 512])
        pS = m.ps("pS", [P, 4, P])
        loaded = m.sem("loaded")
        weights_in = m.sem("weights_in")
        weights_ready = m.sem("weights_ready")
        stats_done = m.sem("stats_done")
        root_done = m.sem("root_done")
        normed = m.sem("normed")
        turned = m.sem("turned")
        turned_out = m.sem("turned_out")
        multiplied = m.sem("multiplied")
        h_copied = m.sem("h_copied", starts=1)
        squared = m.sem("squared")
        summed = m.sem("summed", starts=1)
        rooted = m.sem("rooted")
        a_copied = m.sem("a_copied", starts=1)
        kv_normed = m.sem("kv_normed", starts=1)
        kv_scaled = m.sem("kv_scaled", starts=1)
        k_ready = m.sem("k_ready")
        v_ready = m.sem("v_ready")
        kv_used = m.sem("kv_used", starts=1)
        h_stored = m.sem("h_stored")
        h_free = m.sem("h_free", starts=1)
        mix_step = m.sem("mix_step")
        mix_copied = m.sem("mix_copied")
        x_in = m.sem("x_in")
        normed2 = m.sem("normed2")
        turned2 = m.sem("turned2")
        turned2_out = m.sem("turned2_out")
        mixed = m.sem("mixed")
        base_ready = m.sem("base_ready", starts=1)
        base_stored = m.sem("base_stored")
        base_free = m.sem("base_free", starts=1)
        WLOADS = 14

        m.clear_semaphores()
        with nc.Block() as block:

            @block.sync
            def _(sp):
                for c in range(0, NT, 10):
                    hi = min(c + 10, NT)
                    sp.dma_start(x[:, c:hi, :], d["x"].rearrange("(t p) c -> p t c", p=P)[:, c:hi, :]).then_inc(loaded, 16)
                with sp.Fori(0, TRIPS) as i:
                    after(sp, h_copied, (i + 1) * U)
                    sp.dma_start(d["h1"].rearrange("(t p) c -> p t c", p=P)[:, bass.ds(i * U, U), :],
                                 h_out[:, :, :]).then_inc(h_stored, 16)
                    sp.wait_ge(h_stored, 16 * (i + 1))
                    sp.sem_inc(h_free, 1)
                with sp.Fori(0, TRIPS) as i:
                    after(sp, base_ready, i * U)
                    sp.dma_start(xin[:, :, :], d["x"].rearrange("(t p) c -> p t c", p=P)[:, bass.ds(i * U, U), :]).then_inc(x_in, 16)
                    after(sp, base_ready, (i + 1) * U)
                    sp.dma_start(d["base"].rearrange("(t p) c -> p t c", p=P)[:, bass.ds(i * U, U), :],
                                 base[:, :, :]).then_inc(base_stored, 16)
                    sp.wait_ge(base_stored, 16 * (i + 1))
                    sp.sem_inc(base_free, 1)
                sp.wait_ge(h_stored, 16 * TRIPS)
                sp.wait_ge(base_stored, 16 * TRIPS)

            @block.scalar
            def _(act):
                loads = [
                    (w1[:, :, :], d["w1"].rearrange("(k p) f -> p k f", p=P)),
                    (avec[:, 0:HEADS1, :], d["a_src1"].partition_broadcast(P)),
                    (avec[:, HEADS1:, :], d["a_dst1"].partition_broadcast(P)),
                    (wkv[:, :, 0:4, :], d["wk_t"].rearrange("(k p) (h e) -> p k h e", p=P, e=HD)),
                    (wkv[:, :, 4:8, :], d["wv_t"].rearrange("(k p) (h e) -> p k h e", p=P, e=HD)),
                    (wq[:, :, :], d["wq"].rearrange("(k p) i -> p k i", p=P)),
                    (wo[:, :, :], d["wo_t"].rearrange("(k p) o -> p k o", p=P)),
                    (gains[:, 0, :], d["ln_k_g"].partition_broadcast(P)),
                    (gains[:, 1, :], d["ln_v_g"].partition_broadcast(P)),
                    (shifts[:, 0, :], d["ln_k_b"].partition_broadcast(P)),
                    (shifts[:, 1, :], d["ln_v_b"].partition_broadcast(P)),
                    (rbias[:, 0, :], d["bo"].partition_broadcast(P)),
                    (rbias[:, 1, :], d["b2"].partition_broadcast(P)),
                    (valid[:, :], d["valid"]),
                ]
                assert len(loads) == WLOADS
                for to, of in loads:
                    act.dma_start(to, of).then_inc(weights_in, 16)
                act.wait_ge(stats_done, 1)
                nc.scalar.activation(half[:, :], var[:, :], ACT.Sqrt, bias=eps[:, 0:1]).then_inc(root_done, 1)


                def copy_turned(t, j, done, copied):
                    act.wait_ge(done, t + 1)
                    nc.scalar.copy(xT[:, j % 2, :, :].rearrange("p k n -> p (k n)"), pT[:, j % 2, 0:D]).then_inc(copied, 1)

                with act.Fori(0, TRIPS) as i:
                    copy_turned(i * U, 0, turned, turned_out)
                    for j in range(U):
                        t = i * U + j
                        if j + 1 < U:
                            copy_turned(t + 1, j + 1, turned, turned_out)
                        act.wait_ge(multiplied, t + 1)
                        act.wait_ge(h_free, i + 1)
                        nc.scalar.copy(h_out[:, j, :], pH[:, j % 2, :]).then_inc(h_copied, 1)
                        after(act, summed, t)
                        nc.scalar.activation(square[:, j % 2, :], pKV[:, j % 2, :], ACT.Square).then_inc(squared, 1)
                        after(act, summed, t + 1)
                        nc.scalar.activation(sroot[:, j % 2, :], ssum[:, j % 2, :], ACT.Sqrt, bias=eps[:, 0:1],
                                             scale=1.0 / HD).then_inc(rooted, 1)
                with act.Fori(0, TRIPS) as i:
                    for j in range(U):
                        copy_turned(i * U + j, j, turned2, turned2_out)

            @block.vector
            def _(dve):
                dve.wait_ge(loaded, 16 * 5)
                with dve.Fori(0, NT) as t:
                    nc.vector.bn_stats(stats[:, t, :], x[:, t, :])
                nc.vector.memset(eps[:, :], EPS)
                nc.vector.memset(zero[:, :], 0.0)
                nc.vector.memset(kvT[:, :, :], 0.0)
                dve.drain()
                nc.vector.tensor_tensor(mean[:, :], stats[:, :, 1], stats[:, :, 4], ALU.add)
                nc.vector.tensor_tensor(half[:, :], stats[:, :, 1], stats[:, :, 4], ALU.subtract)
                nc.vector.tensor_tensor(var[:, :], stats[:, :, 2], stats[:, :, 5], ALU.add)
                dve.drain()
                nc.vector.tensor_scalar(mean[:, :], mean[:, :], 0.5, None, ALU.mult)
                nc.vector.tensor_tensor(half[:, :], half[:, :], half[:, :], ALU.mult)
                nc.vector.tensor_scalar(var[:, :], var[:, :], 1.0 / D, None, ALU.mult)
                dve.drain()
                nc.vector.scalar_tensor_tensor(out=var[:, :], in0=half[:, :], scalar=0.25, in1=var[:, :],
                                               op0=ALU.mult, op1=ALU.add).then_inc(stats_done, 1)
                dve.wait_ge(weights_in, 16 * WLOADS)
                for kk in range(DK):
                    for s in range(2):
                        nc.vector.tensor_tensor(aprod[:, :, :], w1[:, kk, :].rearrange("p (h f) -> p h f", f=P),
                                                avec[:, s * HEADS1:(s + 1) * HEADS1, :], ALU.mult)
                        dve.drain()
                        nc.vector.tensor_reduce(wa[:, kk, s * HEADS1:(s + 1) * HEADS1], aprod[:, :, :], AX_X, ALU.add)
                        dve.drain()
                wkv_v = wkv[:, :, :, :].rearrange("p k h e -> p (k h) e")
                nc.vector.tensor_reduce(wkv_mean[:, :], wkv_v, AX_X, ALU.add)
                dve.drain()
                nc.vector.tensor_scalar(wkv_mean[:, :], wkv_mean[:, :], 1.0 / HD, None, ALU.mult)
                dve.drain()
                nc.vector.tensor_tensor(wkv_v, wkv_v, spread(wkv_mean[:, :], 2, HD), ALU.subtract)
                nc.vector.tensor_tensor(rbias[:, 0, :], rbias[:, 0, :], rbias[:, 1, :], ALU.add)
                dve.drain()
                dve.sem_inc(weights_ready, 1)
                dve.wait_ge(root_done, 1)
                nc.vector.reciprocal(rstd[:, :], half[:, :])
                nc.vector.tensor_scalar(var[:, :], var[:, :], EPS, None, ALU.add)
                dve.drain()
                nc.vector.tensor_tensor(half[:, :], rstd[:, :], rstd[:, :], ALU.mult)
                dve.drain()
                nc.vector.tensor_tensor(half[:, :], half[:, :], var[:, :], ALU.mult)
                dve.drain()
                nc.vector.tensor_scalar(half[:, :], half[:, :], -0.5, 1.5, ALU.mult, ALU.add)
                dve.drain()
                nc.vector.tensor_tensor(rstd[:, :], rstd[:, :], half[:, :], ALU.mult)
                dve.drain()

                def norm(t, j, of, done):
                    nc.vector.tensor_scalar(xn[:, j, :], of, mean[:, bass.ds(t, 1)], rstd[:, bass.ds(t, 1)],
                                            ALU.subtract, ALU.mult).then_inc(done, 1)

                with dve.Fori(0, TRIPS) as i:
                    for j in range(U):
                        norm(i * U + j, j, x[:, i * U + j, :], normed)
                    for j in range(U):
                        t = i * U + j
                        b = j % 2
                        dve.wait_ge(squared, t + 1)
                        nc.vector.tensor_reduce(ssum[:, b, :], square[:, b, :].rearrange("p (h e) -> p h e", e=HD),
                                                AX_X, ALU.add).then_inc(summed, 1)
                        nc.vector.tensor_copy(k["attn1"][:, t, :], pA[:, 0:2 * HEADS1]).then_inc(a_copied, 1)
                        dve.wait_ge(rooted, t + 1)
                        nc.vector.reciprocal(srec[:, b, :], sroot[:, b, :])
                        dve.drain()
                        after(dve, kv_scaled, t)
                        nc.vector.tensor_tensor(kvn[:, b, :].rearrange("p (h e) -> p h e", e=HD),
                                                pKV[:, b, :].rearrange("p (h e) -> p h e", e=HD),
                                                spread(srec[:, b, :], 2, HD), ALU.mult).then_inc(kv_normed, 1)
                        after(dve, kv_scaled, t + 1)
                        nc.vector.scalar_tensor_tensor(
                            out=kv[:, j, D:].rearrange("p (h e) -> p h e", e=HD),
                            in0=spread(shifts[:, 1, :], 1, 4), scalar=valid[:, bass.ds(t, 1)],
                            in1=kvg[:, b, D:].rearrange("p (h e) -> p h e", e=HD),
                            op0=ALU.mult, op1=ALU.add).then_inc(v_ready, 1)
                dve.wait_ge(mix_step, 1)
                for q in range(2):
                    for s in range(2):
                        r = slice(s * HD, (s + 1) * HD)
                        nc.vector.tensor_scalar(kvT[r, q, r], pS[r, q, r], 1.0 / N, None, ALU.mult)
                dve.drain()
                dve.sem_inc(mix_copied, 1)
                for q in range(2):
                    dve.wait_ge(mix_step, 2 + q)
                    nc.vector.tensor_copy(kvo[:, q, :], pH[:, q, 0:D]).then_inc(mix_copied, 1)
                for q in range(2):
                    dve.wait_ge(mix_step, 4 + q)
                    nc.vector.tensor_copy(mix[:, q, :], pKV[:, q, 0:D]).then_inc(mix_copied, 1)
                with dve.Fori(0, TRIPS) as i:
                    dve.wait_ge(x_in, 16 * (i + 1))
                    for j in range(U):
                        norm(i * U + j, j, xin[:, j, :], normed2)
                    dve.drain()
                    nc.vector.tensor_tensor(xin[:, :, :], xin[:, :, :], spread(rbias[:, 0, :], 1, U), ALU.add)
                    dve.drain()
                    for j in range(U):
                        dve.wait_ge(mixed, i * U + j + 1)
                        dve.wait_ge(base_free, i + 1)
                        nc.vector.tensor_tensor(base[:, j, :], pH[:, j % 2, 0:D], xin[:, j, :], ALU.add).then_inc(base_ready, 1)

            @block.gpsimd
            def _(pool):
                pool.wait_ge(weights_ready, 1)
                with pool.Fori(0, TRIPS) as i:
                    for j in range(U):
                        t = i * U + j
                        after(pool, kv_normed, t + 1)
                        for s in range(2):
                            last = nc.gpsimd.tensor_tensor(
                                kvg[:, j % 2, s * D:(s + 1) * D].rearrange("p (h e) -> p h e", e=HD),
                                kvn[:, j % 2, s * D:(s + 1) * D].rearrange("p (h e) -> p h e", e=HD),
                                spread(gains[:, s, :], 1, 4), ALU.mult)
                        last.then_inc(kv_scaled, 1)
                        after(pool, kv_scaled, t + 1)
                        after(pool, kv_used, i)
                        nc.gpsimd.tensor_tensor(kv[:, j, 0:D].rearrange("p (h e) -> p h e", e=HD),
                                                kvg[:, j % 2, 0:D].rearrange("p (h e) -> p h e", e=HD),
                                                spread(shifts[:, 0, :], 1, 4), ALU.add).then_inc(k_ready, 1)

            @block.tensor
            def _(pe):
                pe.wait_ge(weights_ready, 1)
                nc.tensor.matmul(pS[:, 0:2, :].rearrange("p q n -> p (q n)"), zero[:, 0:P], zero[:, :], start=True, stop=False,
                                 skip_group_check=True)

                def turn(t, j, ready, done):
                    pe.wait_ge(ready, t + 1)
                    for kk in range(DK):
                        last = nc.tensor.transpose(pT[:, j % 2, kk * P:(kk + 1) * P], xn[:, j, kk * P:(kk + 1) * P],
                                                   k["ident"][:, :])
                    last.then_inc(done, 1)

                with pe.Fori(0, TRIPS) as i:
                    turn(i * U, 0, normed, turned)
                    for j in range(U):
                        t = i * U + j
                        b = j % 2
                        if j + 1 < U:
                            turn(t + 1, j + 1, normed, turned)
                        pe.wait_ge(turned_out, t + 1)
                        if j >= 2:
                            after(pe, h_copied, t - 1)
                            after(pe, kv_normed, t - 1)
                        else:
                            after(pe, h_copied, i * U)
                            after(pe, kv_normed, i * U)
                        for kk in range(DK):
                            nc.tensor.matmul(pH[:, b, :], xT[:, b, kk, :], w1[:, kk, :], start=(kk == 0), stop=(kk == 1))
                        for kk in range(DK):
                            nc.tensor.matmul(pKV[:, b, :], xT[:, b, kk, :], wkv[:, kk, :, :].rearrange("p h e -> p (h e)"),
                                             start=(kk == 0), stop=(kk == 1))
                        after(pe, a_copied, t)
                        for kk in range(DK):
                            last = nc.tensor.matmul(pA[:, 0:2 * HEADS1], xT[:, b, kk, :], wa[:, kk, :],
                                                    start=(kk == 0), stop=(kk == 1))
                        last.then_inc(multiplied, 1)
                    for j in range(U):
                        pe.wait_ge(k_ready, i * U + j + 1)
                        pe.wait_ge(v_ready, i * U + j + 1)
                        for q in range(2):
                            last = nc.tensor.matmul(pS[:, q, :], kv[:, j, D + q * P:D + (q + 1) * P],
                                                    kv[:, j, q * P:(q + 1) * P], start=False, stop=False,
                                                    skip_group_check=True)
                    last.then_inc(kv_used, 1)
                nc.tensor.matmul(pS[:, 0:2, :].rearrange("p q n -> p (q n)"), zero[:, 0:P], zero[:, :], start=False, stop=True,
                                 skip_group_check=True).then_inc(mix_step, 1)
                pe.wait_ge(mix_copied, 1)
                for q in range(2):
                    nc.tensor.matmul(pH[:, q, 0:D], kvT[:, q, :], wo[:, q, :], start=True, stop=True).then_inc(mix_step, 1)
                pe.wait_ge(mix_copied, 3)
                for c in range(DK):
                    for q in range(2):
                        last = nc.tensor.matmul(pKV[:, c, 0:D], wq[:, q, c * P:(c + 1) * P], kvo[:, q, :],
                                                start=(q == 0), stop=(q == 1))
                    last.then_inc(mix_step, 1)
                pe.wait_ge(mix_copied, 5)
                with pe.Fori(0, TRIPS) as i:
                    for j in range(U):
                        t = i * U + j
                        if j >= 2:
                            pe.wait_ge(turned2_out, t - 1)
                        turn(t, j, normed2, turned2)
                        pe.wait_ge(turned2_out, t + 1)
                        if j >= 2:
                            after(pe, base_ready, t - 1)
                        else:
                            after(pe, base_ready, i * U)
                        for kk in range(DK):
                            last = nc.tensor.matmul(pH[:, j % 2, 0:D], xT[:, j % 2, kk, :], mix[:, kk, :],
                                                    start=(kk == 0), stop=(kk == 1))
                        last.then_inc(mixed, 1)


def edge_pass(nc, k, d):
    with ExitStack() as ctx:
        m = Memory(nc, ctx, "edge")
        first_i = m.sb("first_i", [1, C], I32)
        first_f = m.sb("first_f", [1, C])
        firsts = m.sb("firsts", [P, C])
        leq = m.sb("leq", [P, C])
        tiles_leq = m.sb("tiles_leq", [P, NT])
        tile_i = m.sb("tile_i", [P, NT], I32)
        run_i = m.sb("run_i", [P, NT, P], I32)
        run_f = m.sb("run_f", [P, NT, P])
        rowend = m.sb("rowend", [P, NT])
        rowstart = m.sb("rowstart", [P, NT])
        tmp = m.sb("tmp", [P, NT])
        follow = m.sb("follow", [P, P])
        carry = m.sb("carry", [P, P])
        pick = m.sb("pick", [P, 2, P])
        bound_i = m.sb("bound_i", [P, 2, NT], I32)
        bound = m.sb("bound", [P, 2 * NT])
        window_i = m.sb("window_i", [P, 2 * NT], I32)
        window = m.sb("window", [P, 2 * NT])
        leq_w = m.sb("leq_w", [P, 2 * NT])
        at_window = m.sb("at_window", [P, SJ])
        etile = m.sb("etile", [P, SJ])
        over = m.sb("over", [P, SJ])
        lift = m.sb("lift", [P, SJ])
        offset_i = m.sb("offset_i", [P, SJ], I32)
        offset_f = m.sb("offset_f", [P, SJ])
        off_t = m.sb("off_t", [SJ, P], I32)
        src_i = m.sb("src_i", [P, SJ, P], I32)
        dst_i = m.sb("dst_i", [P, SJ, P], I32)
        src_f = m.sb("src_f", [P, SJ, P])
        dst_f = m.sb("dst_f", [P, SJ, P])
        pB = m.ps("pB", [P, 4, 512])
        pT = m.ps("pT", [P, 2, 4, P])
        pR = m.ps("pR", [P, 512])
        pO = m.ps("pO", [P, 512])
        first_in = m.sem("first_in")
        first_ready = m.sem("first_ready")
        firsts_out = m.sem("firsts_out")
        tiles_ready = m.sem("tiles_ready")
        runs_in = m.swdge_sem("runs_in")
        masks_ready = m.sem("masks_ready")
        ends_ready = m.sem("ends_ready")
        starts_out = m.sem("starts_out")
        walk_ready = m.sem("walk_ready")
        rows_in = m.swdge_sem("rows_in")
        rows_ready = m.sem("rows_ready")
        turned = m.sem("turned")
        copied = m.sem("copied")
        offsets_turned = m.sem("offsets_turned")
        offsets_ready = m.sem("offsets_ready")
        offsets_out = m.sem("offsets_out")
        offsets_in = m.sem("offsets_in")
        QUADS = -(-2 * SJ // 4)

        m.clear_semaphores()
        with nc.Block() as block:

            @block.sync
            def _(sp):
                sp.dma_start(first_i[:, :], d["dst"].rearrange("(c e) -> e c", e=P)[0:1, :],
                             allow_slow_non_contiguous=True).then_inc(first_in, 16)
                sp.wait_ge(offsets_ready, 1)
                sp.dma_start(d["offsets"].rearrange("(j p) -> j p", p=P), off_t[:, :]).then_inc(offsets_out, 16)
                sp.wait_ge(offsets_out, 16)
                sp.dma_start(k["offset"][:, :], d["offsets"].unsqueeze(0)).then_inc(offsets_in, 16)
                sp.wait_ge(offsets_in, 16)

            @block.gpsimd
            def _(pool):
                nc.gpsimd.memset(follow[:, :], 0.0)
                nc.gpsimd.memset(carry[:, :], 0.0)
                nc.gpsimd.memset(pick[:, :, :], 0.0)
                nc.gpsimd.iota(window_i[:, 0:NT], [[2, NT]], base=1, channel_multiplier=0)
                nc.gpsimd.iota(window_i[:, NT:2 * NT], [[2, NT]], base=2, channel_multiplier=0)
                pool.drain()
                nc.gpsimd.affine_select(out=follow[:, :], in_=follow[:, :], compare_op=ALU.not_equal, fill=1.0,
                                        base=1, pattern=[[-1, P]], channel_multiplier=1)
                nc.gpsimd.affine_select(out=carry[:, :], in_=carry[:, :], compare_op=ALU.not_equal, fill=1.0,
                                        base=1 - P, pattern=[[-P, P]], channel_multiplier=1)
                for s in range(2):
                    nc.gpsimd.affine_select(out=pick[:, s, :], in_=pick[:, s, :], compare_op=ALU.not_equal, fill=1.0,
                                            base=1 - W * (s + 1), pattern=[[0, P]], channel_multiplier=1)
                nc.gpsimd.tensor_copy(window[:, :], window_i[:, :])
                pool.drain()
                pool.sem_inc(masks_ready, 1)
                pool.wait_ge(tiles_ready, 1)
                for t in range(NT):
                    pool.indirect_dma_start(run_i[:, t, :], None, d["dst"].rearrange("(c e) -> c e", e=P),
                                            bass.IndirectOffsetOnAxis(ap=tile_i[:, t:t + 1], axis=0)).then_inc(runs_in, 16)
                pool.wait_ge(walk_ready, 1)
                for j in range(SJ):
                    for to, of in ((src_i, d["src"]), (dst_i, d["dst"])):
                        pool.indirect_dma_start(to[:, j, :], None, of.rearrange("(c e) -> c e", e=P),
                                                bass.IndirectOffsetOnAxis(ap=k["etile_i"][:, j:j + 1], axis=0)).then_inc(rows_in, 16)

            @block.vector
            def _(dve):
                dve.wait_ge(first_in, 16)
                nc.vector.tensor_copy(first_f[:, :], first_i[:, :]).then_inc(first_ready, 1)
                dve.wait_ge(firsts_out, 1)
                nc.vector.tensor_copy(firsts[:, :], pB[:, :, :].rearrange("p a b -> p (a b)")[:, 0:C])
                dve.drain()
                with dve.Fori(0, NT) as t:
                    nc.vector.tensor_scalar(leq[:, :], firsts[:, :], k["node"][:, bass.ds(t, 1)], 0.0, ALU.is_le, ALU.add,
                                            accum_out=tiles_leq[:, bass.ds(t, 1)])
                    dve.drain()
                nc.vector.tensor_scalar(tiles_leq[:, :], tiles_leq[:, :], -1.0, 0.0, ALU.add, ALU.max)
                dve.drain()
                nc.vector.tensor_copy(tile_i[:, :], tiles_leq[:, :]).then_inc(tiles_ready, 1)
                dve.wait_ge(runs_in, 16 * NT)
                nc.vector.tensor_tensor(run_f[:, :, :], run_i[:, :, :], spread(k["node"][:, :], 2, P), ALU.is_le)
                dve.drain()
                nc.vector.tensor_reduce(rowend[:, :], run_f[:, :, :], AX_X, ALU.add)
                dve.drain()
                nc.vector.scalar_tensor_tensor(out=rowend[:, :], in0=tiles_leq[:, :], scalar=float(P), in1=rowend[:, :],
                                               op0=ALU.mult, op1=ALU.add).then_inc(ends_ready, 1)
                dve.wait_ge(starts_out, 1)
                nc.vector.tensor_copy(rowstart[:, :], pR[:, 0:NT])
                nc.vector.tensor_copy(bound_i[:, :, :], pO[:, 0:2 * NT].rearrange("p (s t) -> p s t", s=2))
                dve.drain()
                nc.vector.tensor_tensor(k["no_edges"][:, :], rowstart[:, :], rowend[:, :], ALU.is_equal)
                nc.vector.tensor_scalar(tmp[:, :], rowend[:, :], -1.0, 0.0, ALU.add, ALU.max)
                nc.vector.tensor_scalar(bound_i[:, :, :], bound_i[:, :, :], 7, None, ALU.arith_shift_right)
                dve.drain()
                nc.vector.tensor_copy(k["last_i"][:, :], tmp[:, :])
                nc.vector.scalar_tensor_tensor(out=rowstart[:, :], in0=k["no_edges"][:, :], scalar=float(OUT_OF_RANGE),
                                               in1=rowstart[:, :], op0=ALU.mult, op1=ALU.add)
                nc.vector.tensor_tensor(bound[:, :], bound_i[:, :, :].rearrange("p s t -> p (s t)"), window[:, :], ALU.add)
                dve.drain()
                nc.vector.tensor_copy(k["start_i"][:, :], rowstart[:, :])
                for j in range(SJ):
                    nc.vector.tensor_scalar(leq_w[:, 0:NW - 1], bound[:, 0:NW - 1], k["node"][:, j:j + 1], 0.0, ALU.is_le,
                                            ALU.add, accum_out=at_window[:, j:j + 1])
                    dve.drain()
                nc.vector.tensor_tensor(etile[:, :], k["node"][:, 0:SJ], at_window[:, :], ALU.subtract)
                nc.vector.tensor_scalar(offset_f[:, :], at_window[:, :], float(W), None, ALU.mult)
                dve.drain()
                nc.vector.tensor_scalar(over[:, :], etile[:, :], float(C - 1), float(OUT_OF_RANGE), ALU.is_gt, ALU.mult)
                nc.vector.tensor_scalar(etile[:, :], etile[:, :], float(C - 1), None, ALU.min)
                dve.drain()
                nc.vector.tensor_tensor(lift[:, :], offset_f[:, :], over[:, :], ALU.subtract)
                nc.vector.tensor_copy(k["etile_i"][:, :], etile[:, :])
                dve.drain()
                dve.sem_inc(walk_ready, 1)
                dve.wait_ge(offsets_turned, 1)
                nc.vector.tensor_copy(off_t[:, :], pR[0:SJ, 0:P]).then_inc(offsets_ready, 1)
                dve.wait_ge(rows_in, 2 * 16 * SJ)
                nc.vector.tensor_copy(src_f[:, :, :], src_i[:, :, :])
                nc.vector.tensor_tensor(dst_f[:, :, :], dst_i[:, :, :], spread(lift[:, :], 2, P), ALU.subtract)
                dve.drain()
                dve.sem_inc(rows_ready, 1)
                for a in range(QUADS):
                    dve.wait_ge(turned, a + 1)
                    for q in range(4 * a, min(4 * a + 4, 2 * SJ)):
                        to = k["src_step"] if q < SJ else k["place"]
                        j = q % SJ
                        last = nc.vector.tensor_copy(to[:, j * P:(j + 1) * P], pT[:, a % 2, q % 4, :])
                    last.then_inc(copied, 1)

            @block.tensor
            def _(pe):
                pe.wait_ge(first_ready, 1)
                for a in range(4):
                    w = min(512, C - 512 * a)
                    last = nc.tensor.matmul(pB[:, a, 0:w], k["ones"][0:1, :], first_f[:, 512 * a:512 * a + w], start=True, stop=True)
                last.then_inc(firsts_out, 1)
                pe.wait_ge(masks_ready, 1)
                pe.wait_ge(ends_ready, 1)
                nc.tensor.matmul(pR[:, 0:NT], follow[:, :], rowend[:, :], start=True, stop=False, skip_group_check=True)
                nc.tensor.matmul(pR[:, 1:NT], carry[:, :], rowend[:, 0:NT - 1], start=False, stop=True, skip_group_check=True)
                for s in range(2):
                    last = nc.tensor.matmul(pO[:, s * NT:(s + 1) * NT], pick[:, s, :], rowend[:, :], start=True, stop=True)
                last.then_inc(starts_out, 1)
                pe.wait_ge(walk_ready, 1)
                nc.tensor.transpose(pR[0:SJ, 0:P], offset_f[:, :], k["ident"][:, :]).then_inc(offsets_turned, 1)
                pe.wait_ge(rows_ready, 1)
                for a in range(QUADS):
                    if a >= 2:
                        pe.wait_ge(copied, a - 1)
                    for q in range(4 * a, min(4 * a + 4, 2 * SJ)):
                        of = src_f if q < SJ else dst_f
                        last = nc.tensor.transpose(pT[:, a % 2, q % 4, :], of[:, q % SJ, :], k["ident"][:, :])
                    last.then_inc(turned, 1)


def attention_pass(nc, k, d, layer, H, attn):
    with ExitStack() as ctx:
        m = Memory(nc, ctx, f"attn{layer}")
        GTRIPS = C // (2 * G)
        TAIL = [min(G, max(C % (2 * G) - half * G, 0)) for half in range(2)]
        src_row = m.sb("src_row", [P, C + 2 * G], I32)
        dst_row = m.sb("dst_row", [P, C], I32)
        dst_before = m.sb("dst_before", [P, C], I32)
        same = m.sb("same", [P, C])
        reset = m.sb("reset", [P, C])
        zero = m.sb("zero", [P, C])
        first_scan = m.sb("first_scan", [P, C])
        index = m.sb("index", [P, 2, G], I32)
        landing = m.sb("landing", [P, 2, G, H])
        term = m.sb("term", [P, C, H])
        scan = m.sb("scan", [P, C, H])
        target = m.sb("target", [P, C, 2 * H])
        node_in = m.sb("node_in", [P, NT, H])
        node_out = m.sb("node_out", [P, NT, 2 * H])
        logit = m.sb("logit", [P, NT, H])
        peak = m.sb("peak", [P, NT, H])
        through = m.sb("through", [P, 1])
        flags = m.sb("flags", [P, 2, 2 * H])
        ends = m.sb("ends", [P, 2 * H])
        row_flags = m.sb("row_flags", [2 * H, P])
        row_ends = m.sb("row_ends", [2 * H, P])
        row_scan = m.sb("row_scan", [2 * H, P + 1])
        carried = m.sb("carried", [P, 2 * H])
        pF = m.ps("pF", [P, 512])
        pE = m.ps("pE", [P, 512])
        pK = m.ps("pK", [P, 512])
        terms_stored = m.sem("terms_stored")
        rows_in = m.sem("rows_in")
        zero_ready = m.sem("zero_ready")
        zeros_stored = m.sem("zeros_stored")
        index_ready = m.sem("index_ready")
        index_seen = m.sem("index_seen")
        gathered = [m.swdge_sem("gathered0"), m.swdge_sem("gathered1")]
        carry_in = m.sem("carry_in")
        carry_turned = m.sem("carry_turned")
        carry_scanned = m.sem("carry_scanned")
        carry_back = m.sem("carry_back")
        peaks_ready = m.sem("peaks_ready")
        peaks_stored = m.sem("peaks_stored")
        node_peaks_in = m.swdge_sem("node_peaks_in")
        self_ready = m.sem("self_ready")
        self_done = m.sem("self_done")
        node_ready = m.sem("node_ready")
        node_scattered = m.swdge_sem("node_scattered")
        target_in = m.sem("target_in")
        logits_ready = m.sem("logits_ready")
        weights_ready = m.sem("weights_ready")
        weights_stored = m.sem("weights_stored")
        sums_ready = m.sem("sums_ready")
        sums_stored = m.sem("sums_stored")
        node_sums_in = m.swdge_sem("node_sums_in")
        SCANS = [(H, True), (2 * H, False), (H, False)]

        def flat(ap):
            return ap.rearrange("p c h -> p (c h)")

        def dram_rows(ap):
            return ap.rearrange("(p c) h -> p (c h)", p=P)

        m.clear_semaphores()
        with nc.Block() as block:

            @block.sync
            def _(sp):
                sp.dma_start(d["terms"][H].rearrange("(t p) h -> p t h", p=P), attn[:, :, 0:H],
                             allow_slow_non_contiguous=True).then_inc(terms_stored, 16)
                sp.dma_start(src_row[:, 0:C], d["src"].rearrange("(p c) -> p c", p=P)).then_inc(rows_in, 16)
                sp.dma_start(dst_row[:, :], d["dst"].rearrange("(p c) -> p c", p=P)).then_inc(rows_in, 16)
                sp.dma_start(dst_before[:, :], d["dst_ext"][0:EP].rearrange("(p c) -> p c", p=P)).then_inc(rows_in, 16)
                sp.wait_ge(zero_ready, 1)
                for a in range(2 * H):
                    sp.dma_start(dram_rows(d["spread"][H])[:, a * C:(a + 1) * C], zero[:, :]).then_inc(zeros_stored, 16)
                sp.wait_ge(peaks_ready, 1)
                sp.dma_start(dram_rows(d["scanned"][H]), flat(scan[:, :, :])).then_inc(peaks_stored, 16)
                sp.wait_ge(node_scattered, 16 * NT)
                sp.dma_start(flat(target[:, :, :]), dram_rows(d["spread"][H])).then_inc(target_in, 16)
                sp.wait_ge(weights_ready, 1)
                sp.dma_start(dram_rows(d["weights"][H]), flat(term[:, :, :])).then_inc(weights_stored, 16)
                sp.wait_ge(sums_ready, 1)
                sp.dma_start(dram_rows(d["sums"][H]), flat(scan[:, :, :])).then_inc(sums_stored, 16)
                sp.wait_ge(weights_stored, 16)
                sp.wait_ge(sums_stored, 16)

            @block.scalar
            def _(act):
                act.wait_ge(self_ready, 1)
                nc.scalar.activation(k["self_weight"][:, :, 0:H], logit[:, :, :], ACT.Exp).then_inc(self_done, 1)
                act.wait_ge(logits_ready, 1)
                nc.scalar.activation(flat(term[:, :, :]), flat(term[:, :, :]), ACT.Exp).then_inc(weights_ready, 1)

            @block.gpsimd
            def _(pool):
                def gather_terms(i, half, n):
                    pool.wait_ge(index_ready, 2 * i + half + 1)
                    pool.sem_inc(index_seen, 1)
                    pool.wait_ge(terms_stored, 16)
                    for a in range(n):
                        pool.indirect_dma_start(landing[:, half, a, :], None, d["terms"][H],
                                                bass.IndirectOffsetOnAxis(ap=index[:, half, a:a + 1], axis=0)
                                                ).then_inc(gathered[half], 16)

                def gather_last(table, done):
                    for t in range(NT):
                        pool.indirect_dma_start(node_in[:, t, :], None, table,
                                                bass.IndirectOffsetOnAxis(ap=k["last_i"][:, t:t + 1], axis=0)).then_inc(done, 16)

                with pool.Fori(0, GTRIPS) as i:
                    for half in range(2):
                        gather_terms(i, half, G)
                for half in range(2):
                    gather_terms(GTRIPS, half, TAIL[half])
                pool.wait_ge(peaks_stored, 16)
                gather_last(d["scanned"][H], node_peaks_in)
                pool.wait_ge(node_ready, 1)
                pool.wait_ge(zeros_stored, 16 * 2 * H)
                for t in range(NT):
                    pool.indirect_dma_start(d["spread"][H], bass.IndirectOffsetOnAxis(ap=k["start_i"][:, t:t + 1], axis=0),
                                            node_out[:, t, :], None, bounds_check=EP - 1, oob_is_err=False
                                            ).then_inc(node_scattered, 16)
                pool.wait_ge(sums_stored, 16)
                gather_last(d["sums"][H], node_sums_in)

            @block.tensor
            def _(pe):
                for r, (n, _) in enumerate(SCANS):
                    pe.wait_ge(carry_in, r + 1)
                    nc.tensor.transpose(pF[0:n, 0:P], flags[:, 1 if r == 0 else 0, 0:n], k["ident"][:, :])
                    nc.tensor.transpose(pE[0:n, 0:P], ends[:, 0:n], k["ident"][:, :]).then_inc(carry_turned, 1)
                    pe.wait_ge(carry_scanned, r + 1)
                    nc.tensor.transpose(pK[:, 0:n], row_scan[0:n, 0:P], k["ident"][0:n, 0:n]).then_inc(carry_back, 1)

            @block.vector
            def _(dve):
                nc.vector.memset(zero[:, :], 0.0)
                nc.vector.memset(src_row[:, C:], 0)
                dve.drain()
                dve.sem_inc(zero_ready, 1)
                dve.wait_ge(rows_in, 48)
                for half in range(2):
                    nc.vector.tensor_copy(index[:, half, :], src_row[:, half * G:(half + 1) * G]).then_inc(index_ready, 1)
                nc.vector.tensor_tensor(same[:, :], dst_row[:, :], dst_before[:, :], ALU.is_equal)
                dve.drain()
                nc.vector.tensor_scalar(reset[:, :], same[:, :], -1.0, BIG, ALU.add, ALU.mult)
                nc.vector.tensor_reduce(through[:, :], same[:, :], AX_X, ALU.min)
                dve.drain()
                nc.vector.tensor_copy(flags[:, 0, :], through[:, 0:1].to_broadcast([P, 2 * H]))
                nc.vector.tensor_scalar(flags[:, 1, :], through[:, 0:1].to_broadcast([P, 2 * H]), -1.0, BIG, ALU.add, ALU.mult)

                with dve.Fori(0, GTRIPS) as i:
                    for half in range(2):
                        first = (2 * i + half) * G
                        dve.wait_ge(gathered[half], (i + 1) * (G * 16))
                        nc.vector.tensor_copy(term[:, bass.ds(first, G), :], landing[:, half, :, :])
                        nc.vector.tensor_copy(index[:, half, :], src_row[:, bass.ds(first + 2 * G, G)])
                        dve.drain()
                        dve.sem_inc(index_ready, 1)
                for half in range(2):
                    n = TAIL[half]
                    if n:
                        dve.wait_ge(gathered[half], (GTRIPS * G + n) * 16)
                        first = (2 * GTRIPS + half) * G
                        nc.vector.tensor_copy(term[:, first:first + n, :], landing[:, half, 0:n, :])
                dve.drain()

                def run_scan(r, of, to):
                    n, peak_scan = SCANS[r]
                    mark, op0, op1, empty = (reset, ALU.add, ALU.max, -BIG) if peak_scan else (same, ALU.mult, ALU.add, 0.0)
                    for h in range(n):
                        nc.vector.tensor_tensor_scan(first_scan[:, :], mark[:, :], of(h), empty, op0, op1)
                        dve.drain()
                        nc.vector.tensor_copy(ends[:, h:h + 1], first_scan[:, C - 1:C])
                        dve.drain()
                    dve.sem_inc(carry_in, 1)
                    dve.wait_ge(carry_turned, r + 1)
                    nc.vector.tensor_copy(row_flags[0:n, :], pF[0:n, 0:P])
                    nc.vector.tensor_copy(row_ends[0:n, :], pE[0:n, 0:P])
                    nc.vector.memset(row_scan[0:n, 0:1], empty)
                    dve.drain()
                    nc.vector.tensor_tensor_scan(row_scan[0:n, 1:P + 1], row_flags[0:n, :], row_ends[0:n, :], empty, op0, op1)
                    dve.drain()
                    dve.sem_inc(carry_scanned, 1)
                    dve.wait_ge(carry_back, r + 1)
                    nc.vector.tensor_copy(carried[:, 0:n], pK[:, 0:n])
                    dve.drain()
                    for h in range(n):
                        nc.vector.tensor_tensor_scan(to(h), mark[:, :], of(h), carried[:, h:h + 1], op0, op1)
                    dve.drain()

                def leaky(ap):
                    nc.vector.scalar_tensor_tensor(out=ap, in0=ap, scalar=SLOPE, in1=ap, op0=ALU.mult, op1=ALU.max)
                    dve.drain()

                run_scan(0, lambda h: term[:, :, h], lambda h: scan[:, :, h])
                dve.sem_inc(peaks_ready, 1)
                dve.wait_ge(node_peaks_in, 16 * NT)
                nc.vector.scalar_tensor_tensor(out=peak[:, :, :], in0=spread(k["no_edges"][:, :], 2, H), scalar=-BIG,
                                               in1=node_in[:, :, :], op0=ALU.mult, op1=ALU.add)
                nc.vector.tensor_tensor(logit[:, :, :], attn[:, :, 0:H], attn[:, :, H:2 * H], ALU.add)
                dve.drain()
                nc.vector.tensor_tensor(peak[:, :, :], peak[:, :, :], attn[:, :, 0:H], ALU.max)
                dve.drain()
                nc.vector.tensor_tensor(peak[:, :, :], peak[:, :, :], attn[:, :, H:2 * H], ALU.add)
                dve.drain()
                leaky(logit[:, :, :])
                leaky(peak[:, :, :])
                nc.vector.tensor_tensor(logit[:, :, :], logit[:, :, :], peak[:, :, :], ALU.subtract).then_inc(self_ready, 1)
                nc.vector.tensor_copy(node_out[:, :, 0:H], attn[:, :, H:2 * H])
                nc.vector.tensor_copy(node_out[:, :, H:2 * H], peak[:, :, :])
                dve.drain()
                dve.sem_inc(node_ready, 1)
                dve.wait_ge(target_in, 16)
                run_scan(1, lambda h: target[:, :, h], lambda h: target[:, :, h])
                nc.vector.tensor_tensor(term[:, :, :], term[:, :, :], target[:, :, 0:H], ALU.add)
                dve.drain()
                leaky(term[:, :, :])
                nc.vector.tensor_tensor(term[:, :, :], term[:, :, :], target[:, :, H:2 * H], ALU.subtract).then_inc(logits_ready, 1)
                dve.wait_ge(weights_ready, 1)
                run_scan(2, lambda h: term[:, :, h], lambda h: scan[:, :, h])
                dve.sem_inc(sums_ready, 1)
                dve.wait_ge(node_sums_in, 16 * NT)
                nc.vector.tensor_scalar(logit[:, :, 0], k["no_edges"][:, :], -1.0, 1.0, ALU.mult, ALU.add)
                dve.drain()
                nc.vector.tensor_tensor(node_in[:, :, :], node_in[:, :, :], spread(logit[:, :, 0], 2, H), ALU.mult)
                dve.drain()
                nc.vector.tensor_tensor(node_in[:, :, :], node_in[:, :, :], k["self_weight"][:, :, 0:H], ALU.add)
                dve.drain()
                nc.vector.reciprocal(k["rdenom"][:, :, 0:H], node_in[:, :, :])



def weight_table(nc, k, d, layer, H):
    with ExitStack() as ctx:
        m = Memory(nc, ctx, f"table{layer}")
        rows = m.sb("rows", [P, SJ, P * H])
        turned = m.sb("turned", [P, 2, P, H])
        pT = m.ps("pT", [P, 2, 4, P])
        rows_in = m.swdge_sem("rows_in")
        done = m.sem("done")
        copied = m.sem("copied")
        stored = [m.sem("stored0"), m.sem("stored1")]

        def psum(j, h):
            return pT[:, j % 2, h, :]

        m.clear_semaphores()
        with nc.Block() as block:

            @block.gpsimd
            def _(pool):
                for j in range(SJ):
                    pool.indirect_dma_start(rows[:, j, :], None, d["weights"][H].rearrange("(c e) h -> c (e h)", e=P),
                                            bass.IndirectOffsetOnAxis(ap=k["etile_i"][:, j:j + 1], axis=0)).then_inc(rows_in, 16)

            @block.tensor
            def _(pe):
                pe.wait_ge(rows_in, 16 * SJ)
                for j in range(SJ):
                    if j >= 2:
                        pe.wait_ge(copied, j - 1)
                    for h in range(H):
                        last = nc.tensor.transpose(psum(j, h), rows[:, j, :].rearrange("p (e h) -> p h e", h=H)[:, h, :],
                                                   k["ident"][:, :])
                    last.then_inc(done, 1)

            @block.vector
            def _(dve):
                for j in range(SJ):
                    dve.wait_ge(done, j + 1)
                    if j >= 2:
                        dve.wait_ge(stored[j % 2], 16 * (j // 2))
                    for h in range(H):
                        last = nc.vector.tensor_copy(turned[:, j % 2, :, h], psum(j, h))
                    last.then_inc(copied, 1)

            @block.sync
            def _(sp):
                for j in range(SJ):
                    sp.wait_ge(copied, j + 1)
                    sp.dma_start(d["step_weights"][H][:, j * P * H:(j + 1) * P * H],
                                 turned[:, j % 2, :, :].rearrange("p s h -> p (s h)")).then_inc(stored[j % 2], 16)
                sp.wait_ge(stored[0], 16 * (-(-SJ // 2)))
                sp.wait_ge(stored[1], 16 * (SJ // 2))


def self_messages(nc, k, d, layer, H, F, acc, table):
    NB = F // P
    with ExitStack() as ctx:
        m = Memory(nc, ctx, f"self{layer}")
        rows = m.sb("rows", [P, U, F])
        diag = m.sb("diag", [P, 2, H, P])
        pM = m.ps("pM", [P, 2, 512])
        rows_in = m.sem("rows_in")
        diag_ready = m.sem("diag_ready")
        multiplied = m.sem("multiplied", starts=1)
        copied = m.sem("copied", starts=1)
        m.clear_semaphores()
        with nc.Block() as block:

            @block.sync
            def _(sp):
                with sp.Fori(0, TRIPS) as i:
                    after(sp, multiplied, i * U)
                    sp.dma_start(rows[:, :, :], table.rearrange("(t p) c -> p t c", p=P)[:, bass.ds(i * U, U), :]).then_inc(rows_in, 16)

            @block.vector
            def _(dve):
                with dve.Fori(0, TRIPS) as i:
                    for j in range(U):
                        t = i * U + j
                        after(dve, multiplied, i * U + max(j - 1, 0))
                        nc.vector.tensor_tensor(diag[:, j % 2, :, :], spread(k["ident"][:, :], 1, H),
                                                spread(k["self_weight"][:, t, 0:H], 2, P), ALU.mult).then_inc(diag_ready, 1)

            @block.tensor
            def _(pe):
                with pe.Fori(0, TRIPS) as i:
                    pe.wait_ge(rows_in, 16 * (i + 1))
                    for j in range(U):
                        t = i * U + j
                        pe.wait_ge(diag_ready, t + 1)
                        after(pe, copied, i * U + max(j - 1, 0))
                        for b in range(NB):
                            last = nc.tensor.matmul(pM[:, j % 2, b * P:(b + 1) * P], rows[:, j, b * P:(b + 1) * P],
                                                    diag[:, j % 2, b % H, :], start=True, stop=True)
                        last.then_inc(multiplied, 1)

            @block.scalar
            def _(act):
                with act.Fori(0, TRIPS) as i:
                    for j in range(U):
                        t = i * U + j
                        after(act, multiplied, t + 1)
                        nc.scalar.copy(acc[:, 0:NB, bass.ds(t * P, P)],
                                       pM[:, j % 2, 0:F].rearrange("p (b n) -> p b n", n=P)).then_inc(copied, 1)


def message_pass(nc, k, d, layer, H, F, acc, table):
    NB = F // P
    HALVES = SP // G
    with ExitStack() as ctx:
        m = Memory(nc, ctx, f"walk{layer}")
        index = m.sb("index", [P, 2, G], I32)
        rows = m.sb("rows", [P, 2, G, F])
        stepw = m.sb("stepw", [P, 2, G * H])
        hit = m.sb("hit", [P, 2, G, W])
        placed = m.sb("placed", [P, 2, G, H, W])
        pM = m.ps("pM", [P, G, 512])
        index_ready = m.sem("index_ready")
        index_seen = m.sem("index_seen")
        rows_in = [m.swdge_sem(f"rows_in{a}") for a in range(2 * G)]
        stepw_in = [m.sem("stepw_in0"), m.sem("stepw_in1")]
        placed_ready = m.sem("placed_ready")
        multiplied = m.sem("multiplied", starts=2 * G)
        added = m.sem("added", starts=G)

        m.clear_semaphores()
        with nc.Block() as block:

            @block.sync
            def _(sp):
                def load(q, half):
                    sp.dma_start(stepw[:, half, :], d["step_weights"][H][:, bass.ds(q * (G * H), G * H)]).then_inc(stepw_in[half], 16)

                for half in range(2):
                    load(half, half)
                with sp.Fori(1, HALVES // 2) as i:
                    for half in range(2):
                        sp.wait_ge(placed_ready, 2 * i + half - 1)
                        load(2 * i + half, half)

            @block.gpsimd
            def _(pool):
                with pool.Fori(0, HALVES // 2) as i:
                    for half in range(2):
                        pool.wait_ge(index_ready, 2 * i + half + 1)
                        pool.sem_inc(index_seen, 1)
                        for a in range(G):
                            pool.indirect_dma_start(rows[:, half, a, :], None, table,
                                                    bass.IndirectOffsetOnAxis(ap=index[:, half, a:a + 1], axis=0)
                                                    ).then_inc(rows_in[half * G + a], 16)

            @block.tensor
            def _(pe):
                with pe.Fori(0, HALVES // 2) as i:
                    for half in range(2):
                        q = 2 * i + half
                        pe.wait_ge(placed_ready, q + 1)
                        for a in range(G):
                            pe.wait_ge(rows_in[half * G + a], 16 * (i + 1))
                            pe.wait_ge(added, q * G + a + 1)
                            for b in range(NB):
                                last = nc.tensor.matmul(pM[:, a, b * W:(b + 1) * W], rows[:, half, a, b * P:(b + 1) * P],
                                                        placed[:, half, a, b % H, :], start=True, stop=True)
                            last.then_inc(multiplied, 1)

            @block.vector
            def _(dve):

                def prepare(q, half, trip):
                    dve.wait_ge(multiplied, q * G + G)
                    nc.vector.tensor_copy(index[:, half, :], k["src_step"][:, bass.ds(q * G, G)]).then_inc(index_ready, 1)
                    nc.vector.tensor_tensor(hit[:, half, :, :], spread(k["count"][:, 0:W], 1, G),
                                            spread(k["place"][:, bass.ds(q * G, G)], 2, W), ALU.is_equal)
                    dve.drain()
                    dve.wait_ge(stepw_in[half], 16 * trip)
                    nc.vector.tensor_tensor(placed[:, half, :, :, :].rearrange("p g h w -> p g h w"),
                                            spread(hit[:, half, :, :], 2, H),
                                            spread(stepw[:, half, :].rearrange("p (g h) -> p g h", h=H), 3, W),
                                            ALU.mult).then_inc(placed_ready, 1)

                def add(q, half):
                    for a in range(G):
                        node = dve.value_load(k["offset"][0:1, bass.ds(q * G + a, 1)], min_val=0, max_val=NP - W)
                        dve.wait_ge(multiplied, q * G + a + 1 + 2 * G)
                        to = acc[:, 0:NB, bass.ds(node, W)]
                        nc.vector.tensor_tensor(to, pM[:, a, 0:NB * W].rearrange("p (b w) -> p b w", w=W), to, ALU.add)
                        dve.drain()
                        dve.sem_inc(added, 1)

                prepare(0, 0, 1)
                with dve.Fori(0, HALVES // 2 - 1) as i:
                    prepare(2 * i + 1, 1, i + 1)
                    add(2 * i, 0)
                    prepare(2 * i + 2, 0, i + 2)
                    add(2 * i + 1, 1)
                i = HALVES // 2 - 1
                prepare(2 * i + 1, 1, i + 1)
                add(2 * i, 0)
                add(2 * i + 1, 1)


def finish_layer1(nc, k, d, acc):
    NB = F1 // P
    with ExitStack() as ctx:
        m = Memory(nc, ctx, "finish1")
        w2 = m.sb("w2", [P, NB, D])
        avec = m.sb("avec", [P, 2, D])
        aprod = m.sb("aprod", [P, NB, D])
        wa = m.sb("wa", [P, NB, 2])
        bias = m.sb("bias", [P, NB])
        slope = m.sb("slope", [P, 1])
        diag = m.sb("diag", [P, 2, HEADS1, P])
        norm = m.sb("norm", [P, 2, NB, P])
        pos = m.sb("pos", [P, 2, NB, P])
        neg = m.sb("neg", [P, 2, NB, P])
        z = m.sb("z", [P, 2, NB, P])
        h_out = m.sb("h_out", [P, U, D])
        pR = m.ps("pR", [P, 2, 512])
        pH = m.ps("pH", [P, 2, 512])
        pA = m.ps("pA", [P, 512])
        weights_in = m.sem("weights_in")
        weights_ready = m.sem("weights_ready")
        diag_ready = m.sem("diag_ready")
        spread_out = m.sem("spread_out")
        normed = m.sem("normed")
        pos_ready = m.sem("pos_ready")
        z_ready = m.sem("z_ready")
        multiplied = m.sem("multiplied", starts=1)
        a_copied = m.sem("a_copied", starts=1)
        h_copied = m.sem("h_copied", starts=1)
        h_stored = m.sem("h_stored")
        h_free = m.sem("h_free", starts=1)
        m.clear_semaphores()
        with nc.Block() as block:

            @block.sync
            def _(sp):
                loads = [(w2[:, :, :], d["w2"].rearrange("(b p) c -> p b c", p=P)), (avec[:, 0:1, :], d["a_src2"].partition_broadcast(P)),
                         (avec[:, 1:2, :], d["a_dst2"].partition_broadcast(P)), (slope[:, :], d["prelu_w"].partition_broadcast(P))]
                for to, of in loads:
                    sp.dma_start(to, of).then_inc(weights_in, 16)
                sp.dma_start(bias[:, :], d["b1"].rearrange("(b p) -> p b", p=P), allow_slow_non_contiguous=True).then_inc(weights_in, 16)
                with sp.Fori(0, TRIPS) as i:
                    after(sp, h_copied, (i + 1) * U)
                    sp.dma_start(d["h2"].rearrange("(t p) c -> p t c", p=P)[:, bass.ds(i * U, U), :], h_out[:, :, :]).then_inc(h_stored, 16)
                    sp.wait_ge(h_stored, 16 * (i + 1))
                    sp.sem_inc(h_free, 1)
                sp.wait_ge(h_stored, 16 * TRIPS)

            @block.vector
            def _(dve):
                dve.wait_ge(weights_in, 16 * 5)
                for s in range(2):
                    nc.vector.tensor_tensor(aprod[:, :, :], w2[:, :, :], spread(avec[:, s, :], 1, NB), ALU.mult)
                    dve.drain()
                    nc.vector.tensor_reduce(wa[:, :, s], aprod[:, :, :], AX_X, ALU.add)
                    dve.drain()
                dve.sem_inc(weights_ready, 1)

                def diagonal(t, j):
                    nc.vector.tensor_tensor(diag[:, j % 2, :, :], spread(k["ident"][:, :], 1, HEADS1),
                                            spread(k["rdenom"][:, t, :], 2, P), ALU.mult).then_inc(diag_ready, 1)

                with dve.Fori(0, TRIPS) as i:
                    diagonal(i * U, 0)
                    for j in range(U):
                        t = i * U + j
                        b = j % 2
                        if j + 1 < U:
                            diagonal(t + 1, j + 1)
                        dve.wait_ge(spread_out, t + 1)
                        nc.vector.tensor_tensor(norm[:, b, :, :], acc[:, 0:NB, bass.ds(t * P, P)],
                                                pR[:, b, :].rearrange("p (b n) -> p b n", n=P), ALU.mult)
                        dve.drain()
                        nc.vector.tensor_tensor(norm[:, b, :, :], norm[:, b, :, :], spread(bias[:, :], 2, P), ALU.add)
                        dve.drain()
                        dve.sem_inc(normed, 1)
                        nc.vector.tensor_scalar(neg[:, b, :, :], norm[:, b, :, :], 0.0, slope[:, 0:1], ALU.min, ALU.mult)
                        dve.drain()
                        dve.wait_ge(pos_ready, t + 1)
                        after(dve, multiplied, i * U + max(j - 1, 0))
                        nc.vector.tensor_tensor(z[:, b, :, :], pos[:, b, :, :], neg[:, b, :, :], ALU.add).then_inc(z_ready, 1)
                        after(dve, multiplied, t + 1)
                        nc.vector.tensor_copy(k["attn2"][:, t, :], pA[:, 0:2]).then_inc(a_copied, 1)

            @block.scalar
            def _(act):
                with act.Fori(0, TRIPS) as i:
                    for j in range(U):
                        t = i * U + j
                        act.wait_ge(normed, t + 1)
                        nc.scalar.activation(pos[:, j % 2, :, :], norm[:, j % 2, :, :], ACT.Relu).then_inc(pos_ready, 1)
                        after(act, multiplied, t + 1)
                        act.wait_ge(h_free, i + 1)
                        nc.scalar.copy(h_out[:, j, :], pH[:, j % 2, 0:D]).then_inc(h_copied, 1)

            @block.tensor
            def _(pe):
                pe.wait_ge(weights_ready, 1)

                def spread_norm(t, j):
                    pe.wait_ge(diag_ready, t + 1)
                    nc.tensor.matmul(pR[:, j % 2, :], k["ones"][:, :], diag[:, j % 2, :, :].rearrange("p h n -> p (h n)"),
                                     start=True, stop=True).then_inc(spread_out, 1)

                with pe.Fori(0, TRIPS) as i:
                    spread_norm(i * U, 0)
                    for j in range(U):
                        t = i * U + j
                        if j + 1 < U:
                            spread_norm(t + 1, j + 1)
                        pe.wait_ge(z_ready, t + 1)
                        after(pe, h_copied, i * U + max(j - 1, 0))
                        after(pe, a_copied, t)
                        for b in range(NB):
                            nc.tensor.matmul(pH[:, j % 2, 0:D], z[:, j % 2, b, :], w2[:, b, :], start=(b == 0), stop=(b == NB - 1))
                        for b in range(NB):
                            last = nc.tensor.matmul(pA[:, 0:2], z[:, j % 2, b, :], wa[:, b, :], start=(b == 0), stop=(b == NB - 1))
                        last.then_inc(multiplied, 1)


def finish_layer2(nc, k, d, acc):
    with ExitStack() as ctx:
        m = Memory(nc, ctx, "finish2")
        x1 = m.sb("x1", [P, NT, D])
        y = m.sb("y", [P, NT, D])
        part = m.sb("part", [P, 2, DK, P])
        basein = m.sb("basein", [P, U, D])
        stats = m.sb("stats", [P, NT, 6])
        mean = m.sb("mean", [P, NT])
        half = m.sb("half", [P, NT])
        var = m.sb("var", [P, NT])
        rstd = m.sb("rstd", [P, NT])
        eps = m.sb("eps", [P, 1])
        yT = m.sb("yT", [P, 2, DK, P])
        ycur = m.sb("ycur", [P, 2, D])
        wg = m.sb("wg", [P, DK, NEXP])
        bg = m.sb("bg", [P, NEXP])
        logits = m.sb("logits", [P, NT, NEXP])
        code = m.sb("code", [P, NT, NEXP])
        first = m.sb("first", [P, NT, NEXP])
        second = m.sb("second", [P, NT, NEXP])
        work = m.sb("work", [P, NT, NEXP])
        rank8 = m.sb("rank8", [P, NEXP])
        top = m.sb("top", [P, 2, NT])
        best = m.sb("best", [P, NT])
        valid = m.sb("valid", [P, NT])
        tri = m.sb("tri", [P, P])
        before = m.sb("before", [P, NT, NEXP])
        total = m.sb("total", [P, NT, NEXP])
        ones_row = m.sb("ones_row", [P, NT])
        tiles_i = m.sb("tiles_i", [P, NEXP], I32)
        tiles_f = m.sb("tiles_f", [P, NEXP])
        tile_start = m.sb("tile_start", [P, NEXP])
        expert = m.sb("expert", [1, TT])
        zero = m.sb("zero", [P, SLOTS * D // P // 30])
        pT = m.ps("pT", [P, 2, 512])
        pG = m.ps("pG", [P, 2, 512])
        pB = m.ps("pB", [P, 512])
        pC = m.ps("pC", [P, 512])
        loads_in = m.sem("loads_in")
        zero_ready = m.sem("zero_ready")
        zeros_stored = m.sem("zeros_stored")
        tri_ready = m.sem("tri_ready")
        base_in = m.sem("base_in")
        part_ready = m.sem("part_ready")
        turned = m.sem("turned", starts=1)
        x1_ready = m.sem("x1_ready", starts=1)
        x1_stored = m.sem("x1_stored")
        stats_done = m.sem("stats_done")
        root_done = m.sem("root_done")
        y_ready = m.sem("y_ready")
        y_turned = m.sem("y_turned", starts=1)
        yT_ready = m.sem("yT_ready")
        gated = m.sem("gated")
        logits_ready = m.sem("logits_ready", starts=1)
        gap_ready = m.sem("gap_ready")
        gap_done = m.sem("gap_done")
        chosen = m.sem("chosen")
        counted = m.sem("counted")
        slots_ready = m.sem("slots_ready")
        scattered = m.swdge_sem("scattered")

        m.clear_semaphores()
        with nc.Block() as block:

            @block.sync
            def _(sp):
                sp.dma_start(wg[:, :, :], d["wg"].rearrange("(k p) e -> p k e", p=P)).then_inc(loads_in, 16)
                sp.dma_start(bg[:, :], d["bg"].partition_broadcast(P)).then_inc(loads_in, 16)
                sp.dma_start(valid[:, :], d["valid"]).then_inc(loads_in, 16)
                sp.wait_ge(zero_ready, 1)
                for a in range(30):
                    w = SLOTS * D // P // 30
                    sp.dma_start(d["xs"].rearrange("(p s) c -> p (s c)", p=P)[:, a * w:(a + 1) * w], zero[:, :]).then_inc(zeros_stored, 16)
                with sp.Fori(0, TRIPS) as i:
                    after(sp, x1_ready, i * U)
                    sp.dma_start(basein[:, :, :], d["base"].rearrange("(t p) c -> p t c", p=P)[:, bass.ds(i * U, U), :]).then_inc(base_in, 16)
                after(sp, x1_ready, NT)
                sp.dma_start(d["x1"].rearrange("(t p) c -> p t c", p=P), x1[:, :, :]).then_inc(x1_stored, 16)
                sp.wait_ge(x1_stored, 16)

            @block.gpsimd
            def _(pool):
                nc.gpsimd.memset(tri[:, :], 1.0)
                nc.gpsimd.memset(zero[:, :], 0.0)
                pool.drain()
                pool.sem_inc(zero_ready, 1)
                nc.gpsimd.affine_select(out=tri[:, :], in_=tri[:, :], compare_op=ALU.is_gt, fill=0.0,
                                        base=0, pattern=[[1, P]], channel_multiplier=-1)
                pool.drain()
                pool.sem_inc(tri_ready, 1)
                pool.wait_ge(slots_ready, 1)
                pool.wait_ge(zeros_stored, 480)
                for s in range(2):
                    for t in range(NT):
                        pool.indirect_dma_start(d["xs"], bass.IndirectOffsetOnAxis(ap=k["slot_out"][:, s, t:t + 1], axis=0),
                                                y[:, t, :], None, bounds_check=SLOTS - 1, oob_is_err=False).then_inc(scattered, 16)
                pool.wait_ge(scattered, 16 * 2 * NT)

            @block.scalar
            def _(act):
                with act.Fori(0, TRIPS) as i:
                    for j in range(U):
                        t = i * U + j
                        after(act, turned, i * U + max(j - 1, 0))
                        nc.scalar.copy(part[:, j % 2, :, :], acc[:, 0:DK, bass.ds(t * P, P)]).then_inc(part_ready, 1)
                act.wait_ge(stats_done, 1)
                nc.scalar.activation(half[:, :], var[:, :], ACT.Sqrt, bias=eps[:, 0:1]).then_inc(root_done, 1)
                with act.Fori(0, TRIPS) as i:
                    for j in range(U):
                        after(act, y_turned, i * U + j + 1)
                        nc.scalar.copy(yT[:, j % 2, :, :].rearrange("p k n -> p (k n)"), pT[:, j % 2, 0:D]).then_inc(yT_ready, 1)
                act.wait_ge(gap_ready, 1)
                nc.scalar.activation(best[:, :], best[:, :], ACT.Exp).then_inc(gap_done, 1)

            @block.tensor
            def _(pe):
                with pe.Fori(0, TRIPS) as i:
                    for j in range(U):
                        t = i * U + j
                        pe.wait_ge(part_ready, t + 1)
                        after(pe, x1_ready, i * U + max(j - 1, 0))
                        for kk in range(DK):
                            last = nc.tensor.transpose(pT[:, j % 2, kk * P:(kk + 1) * P], part[:, j % 2, kk, :], k["ident"][:, :])
                        last.then_inc(turned, 1)
                pe.wait_ge(loads_in, 48)
                with pe.Fori(0, TRIPS) as i:
                    for j in range(U):
                        t = i * U + j
                        pe.wait_ge(y_ready, t + 1)
                        for kk in range(DK):
                            last = nc.tensor.transpose(pT[:, j % 2, kk * P:(kk + 1) * P], ycur[:, j % 2, kk * P:(kk + 1) * P],
                                                       k["ident"][:, :])
                        last.then_inc(y_turned, 1)
                        pe.wait_ge(yT_ready, t + 1)
                        after(pe, logits_ready, i * U + max(j - 1, 0))
                        for kk in range(DK):
                            last = nc.tensor.matmul(pG[:, j % 2, 0:NEXP], yT[:, j % 2, kk, :], wg[:, kk, :],
                                                    start=(kk == 0), stop=(kk == 1))
                        last.then_inc(gated, 1)
                pe.wait_ge(tri_ready, 1)
                pe.wait_ge(chosen, 1)
                nc.tensor.matmul(pB[:, 0:NT * NEXP], tri[:, :], work[:, :, :].rearrange("p t e -> p (t e)"), start=True, stop=True)
                nc.tensor.matmul(pC[:, 0:NT * NEXP], k["ones"][:, :], work[:, :, :].rearrange("p t e -> p (t e)"),
                                 start=True, stop=True).then_inc(counted, 1)

            @block.vector
            def _(dve):
                nc.vector.memset(eps[:, :], EPS)
                nc.vector.memset(ones_row[:, :], 1.0)
                with dve.Fori(0, TRIPS) as i:
                    dve.wait_ge(base_in, 16 * (i + 1))
                    for j in range(U):
                        t = i * U + j
                        after(dve, turned, t + 1)
                        nc.vector.scalar_tensor_tensor(out=x1[:, t, :], in0=pT[:, j % 2, 0:D], scalar=k["rdenom"][:, t, 0:1],
                                                       in1=basein[:, j, :], op0=ALU.mult, op1=ALU.add).then_inc(x1_ready, 1)
                dve.drain()
                with dve.Fori(0, NT) as t:
                    nc.vector.bn_stats(stats[:, t, :], x1[:, t, :])
                dve.drain()
                nc.vector.tensor_tensor(mean[:, :], stats[:, :, 1], stats[:, :, 4], ALU.add)
                nc.vector.tensor_tensor(half[:, :], stats[:, :, 1], stats[:, :, 4], ALU.subtract)
                nc.vector.tensor_tensor(var[:, :], stats[:, :, 2], stats[:, :, 5], ALU.add)
                dve.drain()
                nc.vector.tensor_scalar(mean[:, :], mean[:, :], 0.5, None, ALU.mult)
                nc.vector.tensor_tensor(half[:, :], half[:, :], half[:, :], ALU.mult)
                nc.vector.tensor_scalar(var[:, :], var[:, :], 1.0 / D, None, ALU.mult)
                dve.drain()
                nc.vector.scalar_tensor_tensor(out=var[:, :], in0=half[:, :], scalar=0.25, in1=var[:, :],
                                               op0=ALU.mult, op1=ALU.add).then_inc(stats_done, 1)
                dve.wait_ge(root_done, 1)
                newton(nc, dve, rstd, half, var)
                with dve.Fori(0, TRIPS) as i:
                    for j in range(U):
                        t = i * U + j
                        after(dve, y_turned, i * U + max(j - 1, 0))
                        nc.vector.tensor_scalar(y[:, t, :], x1[:, t, :], mean[:, bass.ds(t, 1)], rstd[:, bass.ds(t, 1)],
                                                ALU.subtract, ALU.mult)
                        dve.drain()
                        nc.vector.tensor_copy(ycur[:, j % 2, :], y[:, t, :]).then_inc(y_ready, 1)
                        if j == 0:
                            dve.wait_ge(loads_in, 48)
                        else:
                            dve.wait_ge(gated, t)
                            nc.vector.tensor_tensor(logits[:, t - 1, :], pG[:, (j - 1) % 2, 0:NEXP], bg[:, :], ALU.add).then_inc(logits_ready, 1)
                    dve.wait_ge(gated, i * U + U)
                    nc.vector.tensor_tensor(logits[:, i * U + U - 1, :], pG[:, (U - 1) % 2, 0:NEXP], bg[:, :], ALU.add).then_inc(logits_ready, 1)
                nc.vector.tensor_scalar(rank8[:, :], k["count"][:, 0:NEXP], -1.0, float(NEXP), ALU.mult, ALU.add)
                dve.drain()
                for s, to in enumerate((first, second)):
                    nc.vector.tensor_reduce(top[:, s, :], logits[:, :, :], AX_X, ALU.max)
                    dve.drain()
                    nc.vector.tensor_tensor(code[:, :, :], logits[:, :, :], spread(top[:, s, :], 2, NEXP), ALU.is_equal)
                    dve.drain()
                    nc.vector.tensor_tensor(code[:, :, :], code[:, :, :], spread(rank8[:, :], 1, NT), ALU.mult)
                    dve.drain()
                    nc.vector.tensor_reduce(best[:, :], code[:, :, :], AX_X, ALU.max)
                    dve.drain()
                    nc.vector.tensor_tensor(to[:, :, :], code[:, :, :], spread(best[:, :], 2, NEXP), ALU.is_equal)
                    dve.drain()
                    if s == 0:
                        nc.vector.scalar_tensor_tensor(out=logits[:, :, :], in0=to[:, :, :], scalar=-BIG, in1=logits[:, :, :],
                                                       op0=ALU.mult, op1=ALU.add)
                        dve.drain()
                nc.vector.tensor_tensor(best[:, :], top[:, 1, :], top[:, 0, :], ALU.subtract).then_inc(gap_ready, 1)
                nc.vector.tensor_tensor(work[:, :, :], first[:, :, :], second[:, :, :], ALU.add)
                dve.drain()
                nc.vector.tensor_tensor(work[:, :, :], work[:, :, :], spread(valid[:, :], 2, NEXP), ALU.mult).then_inc(chosen, 1)
                dve.wait_ge(gap_done, 1)
                nc.vector.tensor_scalar(half[:, :], best[:, :], 1.0, None, ALU.add)
                dve.drain()
                nc.vector.reciprocal(k["mix_weight"][:, 0, :], half[:, :])
                dve.drain()
                nc.vector.tensor_tensor(k["mix_weight"][:, 1, :], k["mix_weight"][:, 0, :], best[:, :], ALU.mult)
                dve.wait_ge(counted, 1)
                nc.vector.tensor_copy(code[:, :, :].rearrange("p t e -> p (t e)"), pC[:, 0:NT * NEXP])
                nc.vector.tensor_copy(before[:, :, :].rearrange("p t e -> p (t e)"), pB[:, 0:NT * NEXP])
                dve.drain()
                for e in range(NEXP):
                    nc.vector.tensor_tensor_scan(total[:, :, e], ones_row[:, :], code[:, :, e], 0.0, ALU.mult, ALU.add)
                dve.drain()
                nc.vector.tensor_scalar(tiles_f[:, :], total[:, NT - 1, :], float(P - 1), None, ALU.add)
                nc.vector.tensor_tensor(before[:, :, :], before[:, :, :], total[:, :, :], ALU.add)
                dve.drain()
                nc.vector.tensor_tensor(before[:, :, :], before[:, :, :], code[:, :, :], ALU.subtract)
                nc.vector.tensor_copy(tiles_i[:, :], tiles_f[:, :])
                dve.drain()
                nc.vector.tensor_scalar(tiles_i[:, :], tiles_i[:, :], 7, None, ALU.arith_shift_right)
                dve.drain()
                nc.vector.tensor_copy(tiles_f[:, :], tiles_i[:, :])
                dve.drain()
                nc.vector.tensor_tensor_scan(tile_start[:, :], ones_row[:, 0:NEXP], tiles_f[:, :], 0.0, ALU.mult, ALU.add)
                dve.drain()
                nc.vector.tensor_tensor(tile_start[:, :], tile_start[:, :], tiles_f[:, :], ALU.subtract)
                dve.drain()
                nc.vector.scalar_tensor_tensor(out=before[:, :, :], in0=spread(tile_start[:, :], 1, NT), scalar=float(P),
                                               in1=before[:, :, :], op0=ALU.mult, op1=ALU.add)
                nc.vector.memset(expert[:, :], 0.0)
                nc.vector.tensor_scalar(half[:, :], valid[:, :], -float(OUT_OF_RANGE), float(OUT_OF_RANGE), ALU.mult, ALU.add)
                dve.drain()
                for s, of in enumerate((first, second)):
                    nc.vector.tensor_tensor(code[:, :, :], of[:, :, :], before[:, :, :], ALU.mult)
                    dve.drain()
                    nc.vector.tensor_reduce(mean[:, :], code[:, :, :], AX_X, ALU.add)
                    dve.drain()
                    nc.vector.tensor_tensor(mean[:, :], mean[:, :], half[:, :], ALU.add)
                    dve.drain()
                    nc.vector.tensor_copy(k["slot_out"][:, s, :], mean[:, :])
                    nc.vector.tensor_scalar(var[:, :], mean[:, :], float(SLOTS - 1), None, ALU.min)
                    dve.drain()
                    nc.vector.tensor_copy(k["slot_in"][:, s, :], var[:, :])
                dve.drain()
                dve.sem_inc(slots_ready, 1)
                for e in range(1, NEXP):
                    nc.vector.scalar_tensor_tensor(out=expert[:, :], in0=k["count"][0:1, 0:TT], scalar=tile_start[0:1, e:e + 1],
                                                   in1=expert[:, :], op0=ALU.is_ge, op1=ALU.add)
                    dve.drain()
                nc.vector.tensor_copy(k["expert"][:, :], expert[:, :])


def newton(nc, dve, rstd, root, var):
    nc.vector.reciprocal(rstd[:, :], root[:, :])
    nc.vector.tensor_scalar(var[:, :], var[:, :], EPS, None, ALU.add)
    dve.drain()
    nc.vector.tensor_tensor(root[:, :], rstd[:, :], rstd[:, :], ALU.mult)
    dve.drain()
    nc.vector.tensor_tensor(root[:, :], root[:, :], var[:, :], ALU.mult)
    dve.drain()
    nc.vector.tensor_scalar(root[:, :], root[:, :], -0.5, 1.5, ALU.mult, ALU.add)
    dve.drain()
    nc.vector.tensor_tensor(rstd[:, :], rstd[:, :], root[:, :], ALU.mult)
    dve.drain()


def expert_pass(nc, k, d):
    HC = HID // P
    ETRIPS = TT // U
    assert ETRIPS * U == TT
    with ExitStack() as ctx:
        m = Memory(nc, ctx, "expert")
        w1 = m.sb("w1", [P, NEXP, DK, HID])
        w2 = m.sb("w2", [P, NEXP, HC, D])
        b1 = m.sb("b1", [P, NEXP, HC])
        b2 = m.sb("b2", [P, NEXP, D])
        xin = m.sb("xin", [P, U, D])
        xT = m.sb("xT", [P, DK, P])
        pre = m.sb("pre", [P, HID])
        hT = m.sb("hT", [P, HC, P])
        out = m.sb("out", [P, U, D])
        pX = m.ps("pX", [P, 512])
        pH = m.ps("pH", [P, 2, 512])
        pG = m.ps("pG", [P, HC, P])
        pO = m.ps("pO", [P, 2, 512])
        weights_in = m.sem("weights_in")
        x_in = [m.sem(f"x_in{j}") for j in range(U)]
        x_turned = m.sem("x_turned", starts=1)
        xT_ready = m.sem("xT_ready")
        up_done = m.sem("up_done")
        pre_ready = m.sem("pre_ready", starts=1)
        pre_turned = m.sem("pre_turned")
        h_ready = m.sem("h_ready")
        down_done = m.sem("down_done")
        out_ready = m.sem("out_ready", starts=1)
        out_free = m.sem("out_free", starts=U)
        out_stored = [m.swdge_sem(f"out_stored{j}") for j in range(U)]

        m.clear_semaphores()
        with nc.Block() as block:

            @block.sync
            def _(sp):
                with sp.Fori(0, ETRIPS) as i:
                    for j in range(U):
                        after(sp, x_turned, i * U)
                        sp.dma_start(xin[:, j, :], d["xs"][bass.ds((i * U + j) * P, P), :]).then_inc(x_in[j], 16)

            @block.scalar
            def _(act):
                for e in range(NEXP):
                    act.dma_start(w1[:, e, :, :], d["fw1"][e].rearrange("(k p) h -> p k h", p=P)).then_inc(weights_in, 16)
                    act.dma_start(w2[:, e, :, :], d["fw2"][e].rearrange("(c p) o -> p c o", p=P)).then_inc(weights_in, 16)
                act.dma_start(b1[:, :, :], d["fb1_t"]).then_inc(weights_in, 16)
                act.dma_start(b2[:, :, :], d["fb2"].partition_broadcast(P)).then_inc(weights_in, 16)
                act.wait_ge(weights_in, 16 * 18)
                with act.Fori(0, ETRIPS) as i:
                    for j in range(U):
                        t = i * U + j
                        e = act.value_load(k["expert"][0:1, bass.ds(t, 1)], min_val=0, max_val=NEXP - 1)
                        after(act, x_turned, t + 1)
                        nc.scalar.copy(xT[:, :, :].rearrange("p k n -> p (k n)"), pX[:, 0:D]).then_inc(xT_ready, 1)
                        act.wait_ge(pre_turned, t + 1)
                        for c in range(HC):
                            nc.scalar.activation(hT[:, c, :], pG[:, c, :], ACT.Gelu, bias=b1[:, e, c:c + 1]).then_inc(h_ready, 1)

            @block.vector
            def _(dve):
                dve.wait_ge(weights_in, 16 * 18)

                def take_out(t, j, i):
                    e = dve.value_load(k["expert"][0:1, bass.ds(t, 1)], min_val=0, max_val=NEXP - 1)
                    dve.wait_ge(out_free, t + 1)
                    dve.wait_ge(down_done, t + 1)
                    nc.vector.tensor_tensor(out[:, j, :], pO[:, j % 2, 0:D], b2[:, e, :], ALU.add).then_inc(out_ready, 1)

                with dve.Fori(0, ETRIPS) as i:
                    for j in range(U):
                        t = i * U + j
                        dve.wait_ge(up_done, t + 1)
                        nc.vector.tensor_copy(pre[:, :], pH[:, :, :].rearrange("p a b -> p (a b)")).then_inc(pre_ready, 1)
                        if j:
                            take_out(t - 1, j - 1, i)
                    take_out(i * U + U - 1, U - 1, i)

            @block.tensor
            def _(pe):
                def up(t, j, i):
                    e = pe.value_load(k["expert"][0:1, bass.ds(t, 1)], min_val=0, max_val=NEXP - 1)
                    pe.wait_ge(x_in[j], 16 * (i + 1))
                    for kk in range(DK):
                        last = nc.tensor.transpose(pX[:, kk * P:(kk + 1) * P], xin[:, j, kk * P:(kk + 1) * P], k["ident"][:, :])
                    last.then_inc(x_turned, 1)
                    pe.wait_ge(xT_ready, t + 1)
                    after(pe, pre_ready, t)
                    for a in range(2):
                        for kk in range(DK):
                            last = nc.tensor.matmul(pH[:, a, :], xT[:, kk, :], w1[:, e, kk, a * 512:(a + 1) * 512],
                                                    start=(kk == 0), stop=(kk == 1))
                    last.then_inc(up_done, 1)
                    return e

                def turn(t):
                    after(pe, pre_ready, t + 1)
                    for c in range(HC):
                        last = nc.tensor.transpose(pG[:, c, :], pre[:, c * P:(c + 1) * P], k["ident"][:, :])
                    last.then_inc(pre_turned, 1)

                def down(t, j, i):
                    e = pe.value_load(k["expert"][0:1, bass.ds(t, 1)], min_val=0, max_val=NEXP - 1)
                    after(pe, out_ready, i * U + max(j - 1, 0))
                    for c in range(HC):
                        pe.wait_ge(h_ready, t * HC + c + 1)
                        last = nc.tensor.matmul(pO[:, j % 2, 0:D], hT[:, c, :], w2[:, e, c, :], start=(c == 0), stop=(c == HC - 1))
                    last.then_inc(down_done, 1)

                pe.wait_ge(weights_in, 16 * 18)
                with pe.Fori(0, ETRIPS) as i:
                    up(i * U, 0, i)
                    turn(i * U)
                    for j in range(U):
                        t = i * U + j
                        if j + 1 < U:
                            up(t + 1, j + 1, i)
                        down(t, j, i)
                        if j + 1 < U:
                            turn(t + 1)

            @block.gpsimd
            def _(pool):
                with pool.Fori(0, ETRIPS) as i:
                    for j in range(U):
                        after(pool, out_ready, i * U + j + 1)
                        pool.dma_start(d["ys"][bass.ds((i * U + j) * P, P), :], out[:, j, :]).then_inc(out_stored[j], 16)
                        pool.wait_ge(out_stored[j], 16 * (i + 1))
                        pool.sem_inc(out_free, 1)
                for j in range(U):
                    pool.wait_ge(out_stored[j], 16 * ETRIPS)


def combine_pass(nc, k, d):
    with ExitStack() as ctx:
        m = Memory(nc, ctx, "combine")
        x1 = m.sb("x1", [P, 2, U, D])
        rows = m.sb("rows", [P, 2, 2, U, D])
        x_in = [m.sem("x_in0"), m.sem("x_in1")]
        rows_in = [m.swdge_sem("rows_in0"), m.swdge_sem("rows_in1")]
        out_ready = m.sem("out_ready")
        out_stored = [m.sem("out_stored0"), m.sem("out_stored1")]
        m.clear_semaphores()
        with nc.Block() as block:

            @block.gpsimd
            def _(pool):
                for i in range(TRIPS):
                    if i >= 2:
                        pool.wait_ge(out_ready, i - 1)
                    for j in range(U):
                        for s in range(2):
                            pool.indirect_dma_start(rows[:, i % 2, s, j, :], None, d["ys"],
                                                    bass.IndirectOffsetOnAxis(ap=k["slot_in"][:, s, i * U + j:i * U + j + 1], axis=0)
                                                    ).then_inc(rows_in[i % 2], 16)

            @block.sync
            def _(sp):
                for i in range(TRIPS):
                    if i >= 2:
                        sp.wait_ge(out_stored[i % 2], 16 * (i // 2) if i < TRIPS else 0)
                    sp.dma_start(x1[:, i % 2, :, :], d["x1"].rearrange("(t p) c -> p t c", p=P)[:, i * U:(i + 1) * U, :]).then_inc(x_in[i % 2], 16)

            @block.scalar
            def _(act):
                for i in range(TRIPS):
                    act.wait_ge(out_ready, i + 1)
                    if i < TRIPS - 1:
                        act.dma_start(d["out"][i * U * P:(i + 1) * U * P, :].rearrange("(t p) c -> p t c", p=P),
                                      x1[:, i % 2, :, :]).then_inc(out_stored[i % 2], 16)
                    else:
                        act.dma_start(d["out"][i * U * P:(NT - 1) * P, :].rearrange("(t p) c -> p t c", p=P),
                                      x1[:, i % 2, 0:U - 1, :]).then_inc(out_stored[i % 2], 16)
                        act.dma_start(d["out"][(NT - 1) * P:N, :], x1[0:LAST, i % 2, U - 1, :]).then_inc(out_stored[i % 2], 16)
                act.wait_ge(out_stored[0], 16 * 5)
                act.wait_ge(out_stored[1], 16 * 3)

            @block.vector
            def _(dve):
                for i in range(TRIPS):
                    dve.wait_ge(x_in[i % 2], 16 * (i // 2 + 1))
                    dve.wait_ge(rows_in[i % 2], 16 * 2 * U * (i // 2 + 1))
                    for s in range(2):
                        for j in range(U):
                            t = i * U + j
                            last = nc.vector.scalar_tensor_tensor(out=x1[:, i % 2, j, :], in0=rows[:, i % 2, s, j, :],
                                                                  scalar=k["mix_weight"][:, s, t:t + 1], in1=x1[:, i % 2, j, :],
                                                                  op0=ALU.mult, op1=ALU.add)
                        dve.drain()
                    dve.sem_inc(out_ready, 1)


def build_program(nc, d, until=99):
    with ExitStack() as ctx:
        Memory.program = ctx
        m = Memory(nc, ctx, "all")
        k = dict(
            ident=m.sb("ident", [P, P]), ones=m.sb("ones", [P, P]), node_i=m.sb("node_i", [P, NT], I32),
            count_i=m.sb("count_i", [P, P], I32), node=m.sb("node", [P, NT]), count=m.sb("count", [P, P]),
            attn1=m.sb("attn1", [P, NT, 2 * HEADS1]), attn2=m.sb("attn2", [P, NT, 2]),
            no_edges=m.sb("no_edges", [P, NT]), last_i=m.sb("last_i", [P, NT], I32),
            start_i=m.sb("start_i", [P, NT], I32), etile_i=m.sb("etile_i", [P, SJ], I32),
            offset=m.sb("offset", [1, SP], I32), src_step=m.sb("src_step", [P, SP], I32),
            place=m.sb("place", [P, SP]), self_weight=m.sb("self_weight", [P, NT, HEADS1]),
            rdenom=m.sb("rdenom", [P, NT, HEADS1]), slot_out=m.sb("slot_out", [P, 2, NT], I32),
            slot_in=m.sb("slot_in", [P, 2, NT], I32), mix_weight=m.sb("mix_weight", [P, 2, NT]),
            expert=m.sb("expert", [1, TT], I32))

        def scratch(name, shape, dt=F32):
            return nc.dram_tensor(f"s_{name}", shape, dt, kind="Internal").ap()

        d["h1"] = scratch("h1", [NP, F1])
        d["base"] = scratch("base", [NP, D])
        constants(nc, k)
        d["offsets"] = scratch("offsets", [SP], I32)
        if until != 2:
            node_pass(nc, k, d)
        edge_pass(nc, k, d)
        d["terms"], d["spread"], d["scanned"], d["weights"], d["sums"], d["step_weights"] = {}, {}, {}, {}, {}, {}
        for H in (HEADS1, 1):
            d["terms"][H] = scratch(f"terms{H}", [NP, H])
            d["spread"][H] = scratch(f"spread{H}", [EP, 2 * H])
            d["scanned"][H] = scratch(f"scanned{H}", [EP, H])
            d["weights"][H] = scratch(f"weights{H}", [EP, H])
            d["sums"][H] = scratch(f"sums{H}", [EP, H])
            d["step_weights"][H] = scratch(f"step_weights{H}", [P, SP * H])
        d["h2"] = scratch("h2", [NP, D])
        attention_pass(nc, k, d, 1, HEADS1, k["attn1"])
        weight_table(nc, k, d, 1, HEADS1)
        with nc.sbuf_tensor("acc1", [P, F1 // P, NP], F32) as acc:
            self_messages(nc, k, d, 1, HEADS1, F1, acc, d["h1"])
            message_pass(nc, k, d, 1, HEADS1, F1, acc, d["h1"])
            finish_layer1(nc, k, d, acc)
        attention_pass(nc, k, d, 2, 1, k["attn2"])
        weight_table(nc, k, d, 2, 1)
        d["x1"] = scratch("x1", [NP, D])
        d["xs"] = scratch("xs", [SLOTS, D])
        d["ys"] = scratch("ys", [SLOTS, D])
        with nc.sbuf_tensor("acc2", [P, DK, NP], F32) as acc:
            self_messages(nc, k, d, 2, 1, D, acc, d["h2"])
            message_pass(nc, k, d, 2, 1, D, acc, d["h2"])
            finish_layer2(nc, k, d, acc)
        expert_pass(nc, k, d)
        combine_pass(nc, k, d)


def lay_out(inputs):
    import numpy as np

    g = {n: np.asarray(v) for n, v in inputs.items()}
    dst, src = g["dst"].astype(np.int32, copy=False), g["src"].astype(np.int32, copy=False)
    pad = EP - EDGES
    dst_ext = np.concatenate([np.full(1, -1, np.int32), dst, np.full(pad, N, np.int32)])
    src_pad = np.concatenate([src, np.zeros(pad, np.int32)])
    valid = np.ones((P, NT), np.float32)
    valid[LAST:, NT - 1] = 0.0
    c = np.ascontiguousarray
    return {
        "x": np.concatenate([g["x"], np.zeros((NP - N, D), np.float32)]),
        "src": c(src_pad), "dst": c(dst_ext[1:]), "dst_ext": c(dst_ext), "valid": valid,
        "w1": c(g["L0_gnn_W1"]), "a_src1": c(g["L0_gnn_a_src1"]), "a_dst1": c(g["L0_gnn_a_dst1"]),
        "b1": c(g["L0_gnn_b1"]), "prelu_w": c(g["L0_gnn_prelu_w"].reshape(1)), "w2": c(g["L0_gnn_W2"]),
        "a_src2": c(g["L0_gnn_a_src2"]), "a_dst2": c(g["L0_gnn_a_dst2"]), "b2": c(g["L0_gnn_b2"]),
        "wq": c(g["L0_mix_wq"]), "wk_t": c(g["L0_mix_wk"].T), "wv_t": c(g["L0_mix_wv"].T),
        "wo_t": c(g["L0_mix_wo"].T), "bo": c(g["L0_mix_bo"]),
        "ln_k_g": c(g["L0_mix_ln_k_g"]), "ln_k_b": c(g["L0_mix_ln_k_b"]),
        "ln_v_g": c(g["L0_mix_ln_v_g"]), "ln_v_b": c(g["L0_mix_ln_v_b"]),
        "wg": c(g["L0_ffn_Wg"]), "bg": c(g["L0_ffn_bg"]), "fw1": c(g["L0_ffn_W1"]), "fb1_t": c(g["L0_ffn_b1"].reshape(NEXP, HID // P, P).transpose(2, 0, 1)),
        "fw2": c(g["L0_ffn_W2"]), "fb2": c(g["L0_ffn_b2"]),
    }


def kernel(**inputs):
    import numpy as np
    import concourse.bacc as bacc
    from concourse.bass_utils import run_bass_kernel_spmd

    nc = bacc.Bacc("TRN2", target_bir_lowering=False, num_devices=1)
    arrays = {f"in_{n}_dram": a for n, a in lay_out(inputs).items()}
    d = {n[3:-5]: nc.dram_tensor(n, a.shape, mybir.dt.from_np(a.dtype), kind="ExternalInput").ap()
         for n, a in arrays.items()}
    d["out"] = nc.dram_tensor("out_dram", (N, D), F32, kind="ExternalOutput").ap()
    build_program(nc, d)
    return np.asarray(run_bass_kernel_spmd(nc, [arrays], core_ids=[0]).results[0]["out_dram"])
```

```python
from contextlib import ExitStack

import concourse.bass as bass
from concourse import mybir

ALU = mybir.AluOpType
ACT = mybir.ActivationFunctionType
F32 = mybir.dt.float32
I32 = mybir.dt.int32
BF16 = mybir.dt.bfloat16
AX_X = mybir.AxisListType.X

P = 128
N = 6250
D = 256
DK = D // P
NT = -(-N // P)
NP = NT * P
LAST = N - (NT - 1) * P
U = 7
TRIPS = NT // U
assert TRIPS * U == NT
EDGES = 200000
TPS = 2
BLOCK_BITS = (P * TPS).bit_length() - 1
BLOCKS = -(-EDGES // (P * TPS))
C = BLOCKS * TPS
EP = C * P
HEADS1 = 4
F1 = 512
MIX_HEADS = 8
HD = 64
EPS = 1e-5
SLOPE = 0.2
BIG = 1e30
W = P
NW = NP // W
STEPS = BLOCKS + NW - 1
SJ = -(-STEPS // P)
SP = SJ * P
G = 2
RING = 6
SETS = 3
AHEAD = 2
ROW_TILES = -(-C // P)
CHUNK = 4
FAR = 2.0 ** 100
OUT_OF_RANGE = 1 << 20
NEXP = 8
HID = 1024
TT = (2 * N + NEXP * (P - 1)) // P
SLOTS = TT * P


class Memory:

    program = None

    def __init__(self, nc, ctx, stage):
        self.nc, self.ctx, self.stage = nc, ctx, stage
        self.sems = []
        self.starts = []
        Memory.program = Memory.program or ctx

    def sb(self, name, shape, dt=F32):
        return self.ctx.enter_context(self.nc.sbuf_tensor(f"{self.stage}_{name}", shape, dt))

    def ps(self, name, shape, dt=F32):
        return self.ctx.enter_context(self.nc.psum_tensor(f"{self.stage}_{name}", shape, dt))

    def swdge_sem(self, name):
        self.sems.append(self.program.enter_context(self.nc.semaphore(f"{self.stage}_{name}")))
        return self.sems[-1]

    def sem(self, name, starts=0):
        self.sems.append(self.ctx.enter_context(self.nc.semaphore(f"{self.stage}_{name}")))
        self.starts.append((self.sems[-1], starts))
        return self.sems[-1]

    def clear_semaphores(self):
        with self.nc.Block() as block:

            @block.sync
            def _(sp):
                for sem in self.sems:
                    sp.sem_clear(sem)
                for sem, starts in self.starts:
                    if starts:
                        sp.sem_inc(sem, starts)


def after(engine, sem, n):
    engine.wait_ge(sem, n + 1)


def spread(ap, axis, n):
    shape = list(ap.shape)
    return ap.unsqueeze(axis).to_broadcast(shape[:axis] + [n] + shape[axis:])


def constants(nc, k):
    with nc.Block() as block:

        @block.gpsimd
        def _(pool):
            nc.gpsimd.memset(k["ident"][:, :], 0.0)
            nc.gpsimd.memset(k["ones"][:, :], 1.0)
            nc.gpsimd.iota(k["node_i"][:, :], [[P, NT]], base=0, channel_multiplier=1)
            nc.gpsimd.iota(k["count_i"][:, :], [[1, P]], base=0, channel_multiplier=0)
            pool.drain()
            nc.gpsimd.affine_select(out=k["ident"][:, :], in_=k["ident"][:, :], compare_op=ALU.not_equal, fill=1.0,
                                    base=0, pattern=[[-1, P]], channel_multiplier=1)
            nc.gpsimd.tensor_copy(k["node"][:, :], k["node_i"][:, :])
            nc.gpsimd.tensor_copy(k["count"][:, :], k["count_i"][:, :])


def node_pass(nc, k, d):
    with ExitStack() as ctx:
        m = Memory(nc, ctx, "node")
        x = m.sb("x", [P, NT, D])
        w1 = m.sb("w1", [P, DK, F1])
        avec = m.sb("avec", [P, 2 * HEADS1, P])
        aprod = m.sb("aprod", [P, HEADS1, P])
        wa = m.sb("wa", [P, DK, 2 * HEADS1])
        wkv = m.sb("wkv", [P, DK, MIX_HEADS, HD])
        wkv_mean = m.sb("wkv_mean", [P, DK * MIX_HEADS])
        wq = m.sb("wq", [P, DK, D])
        wo = m.sb("wo", [P, DK, D])
        gains = m.sb("gains", [P, 2, HD])
        shifts = m.sb("shifts", [P, 2, HD])
        rbias = m.sb("rbias", [P, 2, D])
        valid = m.sb("valid", [P, NT])
        stats = m.sb("stats", [P, NT, 6])
        mean = m.sb("mean", [P, NT])
        half = m.sb("half", [P, NT])
        var = m.sb("var", [P, NT])
        rstd = m.sb("rstd", [P, NT])
        eps = m.sb("eps", [P, 1])
        xn = m.sb("xn", [P, U, D])
        xT = m.sb("xT", [P, 2, DK, P])
        h_out = m.sb("h_out", [P, U, F1])
        square = m.sb("square", [P, 2, F1])
        ssum = m.sb("ssum", [P, 2, MIX_HEADS])
        sroot = m.sb("sroot", [P, 2, MIX_HEADS])
        srec = m.sb("srec", [P, 2, MIX_HEADS])
        kvn = m.sb("kvn", [P, 2, F1])
        kvg = m.sb("kvg", [P, 2, F1])
        kv = m.sb("kv", [P, U, F1])
        zero = m.sb("zero", [P, D])
        kvT = m.sb("kvT", [P, 2, P])
        kvo = m.sb("kvo", [P, 2, D])
        mix = m.sb("mix", [P, DK, D])
        xin = m.sb("xin", [P, U, D])
        base = m.sb("base", [P, U, D])
        pT = m.ps("pT", [P, 2, 512])
        pH = m.ps("pH", [P, 2, F1])
        pKV = m.ps("pKV", [P, 2, F1])
        pA = m.ps("pA", [P, 512])
        pS = m.ps("pS", [P, 4, P])
        loaded = m.sem("loaded")
        weights_in = m.sem("weights_in")
        weights_ready = m.sem("weights_ready")
        stats_done = m.sem("stats_done")
        root_done = m.sem("root_done")
        normed = m.sem("normed")
        turned = m.sem("turned")
        turned_out = m.sem("turned_out")
        multiplied = m.sem("multiplied")
        h_copied = m.sem("h_copied", starts=1)
        squared = m.sem("squared")
        summed = m.sem("summed", starts=1)
        rooted = m.sem("rooted")
        a_copied = m.sem("a_copied", starts=1)
        kv_normed = m.sem("kv_normed", starts=1)
        kv_scaled = m.sem("kv_scaled", starts=1)
        k_ready = m.sem("k_ready")
        v_ready = m.sem("v_ready")
        kv_used = m.sem("kv_used", starts=1)
        h_stored = m.sem("h_stored")
        h_free = m.sem("h_free", starts=1)
        mix_step = m.sem("mix_step")
        mix_copied = m.sem("mix_copied")
        x_in = m.sem("x_in")
        normed2 = m.sem("normed2")
        turned2 = m.sem("turned2")
        turned2_out = m.sem("turned2_out")
        mixed = m.sem("mixed")
        base_ready = m.sem("base_ready", starts=1)
        base_stored = m.sem("base_stored")
        base_free = m.sem("base_free", starts=1)
        WLOADS = 14

        m.clear_semaphores()
        with nc.Block() as block:

            @block.sync
            def _(sp):
                for c in range(0, NT, 10):
                    hi = min(c + 10, NT)
                    sp.dma_start(x[:, c:hi, :], d["x"].rearrange("(t p) c -> p t c", p=P)[:, c:hi, :]).then_inc(loaded, 16)
                with sp.Fori(0, TRIPS) as i:
                    after(sp, h_copied, (i + 1) * U)
                    sp.dma_start(d["h1"].rearrange("(t p) c -> p t c", p=P)[:, bass.ds(i * U, U), :],
                                 h_out[:, :, :]).then_inc(h_stored, 16)
                    sp.wait_ge(h_stored, 16 * (i + 1))
                    sp.sem_inc(h_free, 1)
                with sp.Fori(0, TRIPS) as i:
                    after(sp, base_ready, i * U)
                    sp.dma_start(xin[:, :, :], d["x"].rearrange("(t p) c -> p t c", p=P)[:, bass.ds(i * U, U), :]).then_inc(x_in, 16)
                    after(sp, base_ready, (i + 1) * U)
                    sp.dma_start(d["base"].rearrange("(t p) c -> p t c", p=P)[:, bass.ds(i * U, U), :],
                                 base[:, :, :]).then_inc(base_stored, 16)
                    sp.wait_ge(base_stored, 16 * (i + 1))
                    sp.sem_inc(base_free, 1)
                sp.wait_ge(h_stored, 16 * TRIPS)
                sp.wait_ge(base_stored, 16 * TRIPS)

            @block.scalar
            def _(act):
                loads = [
                    (w1[:, :, :], d["w1"].rearrange("(k p) f -> p k f", p=P)),
                    (avec[:, 0:HEADS1, :], d["a_src1"].partition_broadcast(P)),
                    (avec[:, HEADS1:, :], d["a_dst1"].partition_broadcast(P)),
                    (wkv[:, :, 0:4, :], d["wk_t"].rearrange("(k p) (h e) -> p k h e", p=P, e=HD)),
                    (wkv[:, :, 4:8, :], d["wv_t"].rearrange("(k p) (h e) -> p k h e", p=P, e=HD)),
                    (wq[:, :, :], d["wq"].rearrange("(k p) i -> p k i", p=P)),
                    (wo[:, :, :], d["wo_t"].rearrange("(k p) o -> p k o", p=P)),
                    (gains[:, 0, :], d["ln_k_g"].partition_broadcast(P)),
                    (gains[:, 1, :], d["ln_v_g"].partition_broadcast(P)),
                    (shifts[:, 0, :], d["ln_k_b"].partition_broadcast(P)),
                    (shifts[:, 1, :], d["ln_v_b"].partition_broadcast(P)),
                    (rbias[:, 0, :], d["bo"].partition_broadcast(P)),
                    (rbias[:, 1, :], d["b2"].partition_broadcast(P)),
                    (valid[:, :], d["valid"]),
                ]
                assert len(loads) == WLOADS
                for to, of in loads:
                    act.dma_start(to, of).then_inc(weights_in, 16)
                act.wait_ge(stats_done, 1)
                nc.scalar.activation(half[:, :], var[:, :], ACT.Sqrt, bias=eps[:, 0:1]).then_inc(root_done, 1)


                def copy_turned(t, j, done, copied):
                    act.wait_ge(done, t + 1)
                    nc.scalar.copy(xT[:, j % 2, :, :].rearrange("p k n -> p (k n)"), pT[:, j % 2, 0:D]).then_inc(copied, 1)

                with act.Fori(0, TRIPS) as i:
                    copy_turned(i * U, 0, turned, turned_out)
                    for j in range(U):
                        t = i * U + j
                        if j + 1 < U:
                            copy_turned(t + 1, j + 1, turned, turned_out)
                        act.wait_ge(multiplied, t + 1)
                        act.wait_ge(h_free, i + 1)
                        nc.scalar.copy(h_out[:, j, :], pH[:, j % 2, :]).then_inc(h_copied, 1)
                        after(act, summed, t)
                        nc.scalar.activation(square[:, j % 2, :], pKV[:, j % 2, :], ACT.Square).then_inc(squared, 1)
                        after(act, summed, t + 1)
                        nc.scalar.activation(sroot[:, j % 2, :], ssum[:, j % 2, :], ACT.Sqrt, bias=eps[:, 0:1],
                                             scale=1.0 / HD).then_inc(rooted, 1)
                with act.Fori(0, TRIPS) as i:
                    for j in range(U):
                        copy_turned(i * U + j, j, turned2, turned2_out)

            @block.vector
            def _(dve):
                dve.wait_ge(loaded, 16 * 5)
                with dve.Fori(0, NT) as t:
                    nc.vector.bn_stats(stats[:, t, :], x[:, t, :])
                nc.vector.memset(eps[:, :], EPS)
                nc.vector.memset(zero[:, :], 0.0)
                nc.vector.memset(kvT[:, :, :], 0.0)
                dve.drain()
                nc.vector.tensor_tensor(mean[:, :], stats[:, :, 1], stats[:, :, 4], ALU.add)
                nc.vector.tensor_tensor(half[:, :], stats[:, :, 1], stats[:, :, 4], ALU.subtract)
                nc.vector.tensor_tensor(var[:, :], stats[:, :, 2], stats[:, :, 5], ALU.add)
                dve.drain()
                nc.vector.tensor_scalar(mean[:, :], mean[:, :], 0.5, None, ALU.mult)
                nc.vector.tensor_tensor(half[:, :], half[:, :], half[:, :], ALU.mult)
                nc.vector.tensor_scalar(var[:, :], var[:, :], 1.0 / D, None, ALU.mult)
                dve.drain()
                nc.vector.scalar_tensor_tensor(out=var[:, :], in0=half[:, :], scalar=0.25, in1=var[:, :],
                                               op0=ALU.mult, op1=ALU.add).then_inc(stats_done, 1)
                dve.wait_ge(weights_in, 16 * WLOADS)
                for kk in range(DK):
                    for s in range(2):
                        nc.vector.tensor_tensor(aprod[:, :, :], w1[:, kk, :].rearrange("p (h f) -> p h f", f=P),
                                                avec[:, s * HEADS1:(s + 1) * HEADS1, :], ALU.mult)
                        dve.drain()
                        nc.vector.tensor_reduce(wa[:, kk, s * HEADS1:(s + 1) * HEADS1], aprod[:, :, :], AX_X, ALU.add)
                        dve.drain()
                wkv_v = wkv[:, :, :, :].rearrange("p k h e -> p (k h) e")
                nc.vector.tensor_reduce(wkv_mean[:, :], wkv_v, AX_X, ALU.add)
                dve.drain()
                nc.vector.tensor_scalar(wkv_mean[:, :], wkv_mean[:, :], 1.0 / HD, None, ALU.mult)
                dve.drain()
                nc.vector.tensor_tensor(wkv_v, wkv_v, spread(wkv_mean[:, :], 2, HD), ALU.subtract)
                nc.vector.tensor_tensor(rbias[:, 0, :], rbias[:, 0, :], rbias[:, 1, :], ALU.add)
                dve.drain()
                dve.sem_inc(weights_ready, 1)
                dve.wait_ge(root_done, 1)
                nc.vector.reciprocal(rstd[:, :], half[:, :])
                nc.vector.tensor_scalar(var[:, :], var[:, :], EPS, None, ALU.add)
                dve.drain()
                nc.vector.tensor_tensor(half[:, :], rstd[:, :], rstd[:, :], ALU.mult)
                dve.drain()
                nc.vector.tensor_tensor(half[:, :], half[:, :], var[:, :], ALU.mult)
                dve.drain()
                nc.vector.tensor_scalar(half[:, :], half[:, :], -0.5, 1.5, ALU.mult, ALU.add)
                dve.drain()
                nc.vector.tensor_tensor(rstd[:, :], rstd[:, :], half[:, :], ALU.mult)
                dve.drain()

                def norm(t, j, of, done):
                    nc.vector.tensor_scalar(xn[:, j, :], of, mean[:, bass.ds(t, 1)], rstd[:, bass.ds(t, 1)],
                                            ALU.subtract, ALU.mult).then_inc(done, 1)

                with dve.Fori(0, TRIPS) as i:
                    for j in range(U):
                        norm(i * U + j, j, x[:, i * U + j, :], normed)
                    for j in range(U):
                        t = i * U + j
                        b = j % 2
                        dve.wait_ge(squared, t + 1)
                        nc.vector.tensor_reduce(ssum[:, b, :], square[:, b, :].rearrange("p (h e) -> p h e", e=HD),
                                                AX_X, ALU.add).then_inc(summed, 1)
                        nc.vector.tensor_copy(k["attn1"][:, t, :], pA[:, 0:2 * HEADS1]).then_inc(a_copied, 1)
                        dve.wait_ge(rooted, t + 1)
                        nc.vector.reciprocal(srec[:, b, :], sroot[:, b, :])
                        dve.drain()
                        after(dve, kv_scaled, t)
                        nc.vector.tensor_tensor(kvn[:, b, :].rearrange("p (h e) -> p h e", e=HD),
                                                pKV[:, b, :].rearrange("p (h e) -> p h e", e=HD),
                                                spread(srec[:, b, :], 2, HD), ALU.mult).then_inc(kv_normed, 1)
                        after(dve, kv_scaled, t + 1)
                        nc.vector.scalar_tensor_tensor(
                            out=kv[:, j, D:].rearrange("p (h e) -> p h e", e=HD),
                            in0=spread(shifts[:, 1, :], 1, 4), scalar=valid[:, bass.ds(t, 1)],
                            in1=kvg[:, b, D:].rearrange("p (h e) -> p h e", e=HD),
                            op0=ALU.mult, op1=ALU.add).then_inc(v_ready, 1)
                dve.wait_ge(mix_step, 1)
                for q in range(2):
                    for s in range(2):
                        r = slice(s * HD, (s + 1) * HD)
                        nc.vector.tensor_scalar(kvT[r, q, r], pS[r, q, r], 1.0 / N, None, ALU.mult)
                dve.drain()
                dve.sem_inc(mix_copied, 1)
                for q in range(2):
                    dve.wait_ge(mix_step, 2 + q)
                    nc.vector.tensor_copy(kvo[:, q, :], pH[:, q, 0:D]).then_inc(mix_copied, 1)
                for q in range(2):
                    dve.wait_ge(mix_step, 4 + q)
                    nc.vector.tensor_copy(mix[:, q, :], pKV[:, q, 0:D]).then_inc(mix_copied, 1)
                with dve.Fori(0, TRIPS) as i:
                    dve.wait_ge(x_in, 16 * (i + 1))
                    for j in range(U):
                        norm(i * U + j, j, xin[:, j, :], normed2)
                    dve.drain()
                    nc.vector.tensor_tensor(xin[:, :, :], xin[:, :, :], spread(rbias[:, 0, :], 1, U), ALU.add)
                    dve.drain()
                    for j in range(U):
                        dve.wait_ge(mixed, i * U + j + 1)
                        dve.wait_ge(base_free, i + 1)
                        nc.vector.tensor_tensor(base[:, j, :], pH[:, j % 2, 0:D], xin[:, j, :], ALU.add).then_inc(base_ready, 1)

            @block.gpsimd
            def _(pool):
                pool.wait_ge(weights_ready, 1)
                with pool.Fori(0, TRIPS) as i:
                    for j in range(U):
                        t = i * U + j
                        after(pool, kv_normed, t + 1)
                        for s in range(2):
                            last = nc.gpsimd.tensor_tensor(
                                kvg[:, j % 2, s * D:(s + 1) * D].rearrange("p (h e) -> p h e", e=HD),
                                kvn[:, j % 2, s * D:(s + 1) * D].rearrange("p (h e) -> p h e", e=HD),
                                spread(gains[:, s, :], 1, 4), ALU.mult)
                        last.then_inc(kv_scaled, 1)
                        after(pool, kv_scaled, t + 1)
                        after(pool, kv_used, i)
                        nc.gpsimd.tensor_tensor(kv[:, j, 0:D].rearrange("p (h e) -> p h e", e=HD),
                                                kvg[:, j % 2, 0:D].rearrange("p (h e) -> p h e", e=HD),
                                                spread(shifts[:, 0, :], 1, 4), ALU.add).then_inc(k_ready, 1)

            @block.tensor
            def _(pe):
                pe.wait_ge(weights_ready, 1)
                nc.tensor.matmul(pS[:, 0:2, :].rearrange("p q n -> p (q n)"), zero[:, 0:P], zero[:, :], start=True, stop=False,
                                 skip_group_check=True)

                def turn(t, j, ready, done):
                    pe.wait_ge(ready, t + 1)
                    for kk in range(DK):
                        last = nc.tensor.transpose(pT[:, j % 2, kk * P:(kk + 1) * P], xn[:, j, kk * P:(kk + 1) * P],
                                                   k["ident"][:, :])
                    last.then_inc(done, 1)

                with pe.Fori(0, TRIPS) as i:
                    turn(i * U, 0, normed, turned)
                    for j in range(U):
                        t = i * U + j
                        b = j % 2
                        if j + 1 < U:
                            turn(t + 1, j + 1, normed, turned)
                        pe.wait_ge(turned_out, t + 1)
                        if j >= 2:
                            after(pe, h_copied, t - 1)
                            after(pe, kv_normed, t - 1)
                        else:
                            after(pe, h_copied, i * U)
                            after(pe, kv_normed, i * U)
                        for kk in range(DK):
                            nc.tensor.matmul(pH[:, b, :], xT[:, b, kk, :], w1[:, kk, :], start=(kk == 0), stop=(kk == 1))
                        for kk in range(DK):
                            nc.tensor.matmul(pKV[:, b, :], xT[:, b, kk, :], wkv[:, kk, :, :].rearrange("p h e -> p (h e)"),
                                             start=(kk == 0), stop=(kk == 1))
                        after(pe, a_copied, t)
                        for kk in range(DK):
                            last = nc.tensor.matmul(pA[:, 0:2 * HEADS1], xT[:, b, kk, :], wa[:, kk, :],
                                                    start=(kk == 0), stop=(kk == 1))
                        last.then_inc(multiplied, 1)
                    for j in range(U):
                        pe.wait_ge(k_ready, i * U + j + 1)
                        pe.wait_ge(v_ready, i * U + j + 1)
                        for q in range(2):
                            last = nc.tensor.matmul(pS[:, q, :], kv[:, j, D + q * P:D + (q + 1) * P],
                                                    kv[:, j, q * P:(q + 1) * P], start=False, stop=False,
                                                    skip_group_check=True)
                    last.then_inc(kv_used, 1)
                nc.tensor.matmul(pS[:, 0:2, :].rearrange("p q n -> p (q n)"), zero[:, 0:P], zero[:, :], start=False, stop=True,
                                 skip_group_check=True).then_inc(mix_step, 1)
                pe.wait_ge(mix_copied, 1)
                for q in range(2):
                    nc.tensor.matmul(pH[:, q, 0:D], kvT[:, q, :], wo[:, q, :], start=True, stop=True).then_inc(mix_step, 1)
                pe.wait_ge(mix_copied, 3)
                for c in range(DK):
                    for q in range(2):
                        last = nc.tensor.matmul(pKV[:, c, 0:D], wq[:, q, c * P:(c + 1) * P], kvo[:, q, :],
                                                start=(q == 0), stop=(q == 1))
                    last.then_inc(mix_step, 1)
                pe.wait_ge(mix_copied, 5)
                with pe.Fori(0, TRIPS) as i:
                    for j in range(U):
                        t = i * U + j
                        if j >= 2:
                            pe.wait_ge(turned2_out, t - 1)
                        turn(t, j, normed2, turned2)
                        pe.wait_ge(turned2_out, t + 1)
                        if j >= 2:
                            after(pe, base_ready, t - 1)
                        else:
                            after(pe, base_ready, i * U)
                        for kk in range(DK):
                            last = nc.tensor.matmul(pH[:, j % 2, 0:D], xT[:, j % 2, kk, :], mix[:, kk, :],
                                                    start=(kk == 0), stop=(kk == 1))
                        last.then_inc(mixed, 1)


def edge_pass(nc, k, d):
    with ExitStack() as ctx:
        m = Memory(nc, ctx, "edge")
        first_i = m.sb("first_i", [1, C], I32)
        first_f = m.sb("first_f", [1, C])
        firsts = m.sb("firsts", [P, C])
        leq = m.sb("leq", [P, C])
        tiles_leq = m.sb("tiles_leq", [P, NT])
        tile_i = m.sb("tile_i", [P, NT], I32)
        run_i = m.sb("run_i", [P, NT, P], I32)
        run_f = m.sb("run_f", [P, NT, P])
        rowend = m.sb("rowend", [P, NT])
        rowstart = m.sb("rowstart", [P, NT])
        tmp = m.sb("tmp", [P, NT])
        follow = m.sb("follow", [P, P])
        carry = m.sb("carry", [P, P])
        pick = m.sb("pick", [P, P])
        bound_i = m.sb("bound_i", [P, NW], I32)
        bound = m.sb("bound", [P, NW])
        window_i = m.sb("window_i", [P, NW], I32)
        window = m.sb("window", [P, NW])
        leq_w = m.sb("leq_w", [P, NW])
        at_window = m.sb("at_window", [P, SJ])
        etile = m.sb("etile", [P, SJ])
        over = m.sb("over", [P, SJ])
        lift = m.sb("lift", [P, SJ])
        offset_i = m.sb("offset_i", [P, SJ], I32)
        offset_f = m.sb("offset_f", [P, SJ])
        off_t = m.sb("off_t", [SJ, P], I32)
        src_i = m.sb("src_i", [P, SJ, TPS * P], I32)
        dst_i = m.sb("dst_i", [P, SJ, TPS * P], I32)
        src_f = m.sb("src_f", [P, SJ, TPS * P])
        dst_f = m.sb("dst_f", [P, SJ, TPS * P])
        pB = m.ps("pB", [P, 4, 512])
        pT = m.ps("pT", [P, 2, 4, P])
        pR = m.ps("pR", [P, 512])
        pO = m.ps("pO", [P, 512])
        first_in = m.sem("first_in")
        first_ready = m.sem("first_ready")
        firsts_out = m.sem("firsts_out")
        tiles_ready = m.sem("tiles_ready")
        runs_in = m.swdge_sem("runs_in")
        masks_ready = m.sem("masks_ready")
        ends_ready = m.sem("ends_ready")
        starts_out = m.sem("starts_out")
        walk_ready = m.sem("walk_ready")
        rows_in = m.swdge_sem("rows_in")
        rows_ready = m.sem("rows_ready")
        turned = m.sem("turned")
        copied = m.sem("copied")
        offsets_turned = m.sem("offsets_turned")
        offsets_ready = m.sem("offsets_ready")
        offsets_out = m.sem("offsets_out")
        offsets_in = m.sem("offsets_in")
        QUADS = SJ * TPS // 2

        m.clear_semaphores()
        with nc.Block() as block:

            @block.sync
            def _(sp):
                sp.dma_start(first_i[:, :], d["dst"].rearrange("(c e) -> e c", e=P)[0:1, :],
                             allow_slow_non_contiguous=True).then_inc(first_in, 16)
                sp.wait_ge(offsets_ready, 1)
                sp.dma_start(d["offsets"].rearrange("(j p) -> j p", p=P), off_t[:, :]).then_inc(offsets_out, 16)
                sp.wait_ge(offsets_out, 16)
                sp.dma_start(k["offset"][:, :], d["offsets"].unsqueeze(0)).then_inc(offsets_in, 16)
                sp.wait_ge(offsets_in, 16)

            @block.gpsimd
            def _(pool):
                nc.gpsimd.memset(follow[:, :], 0.0)
                nc.gpsimd.memset(carry[:, :], 0.0)
                nc.gpsimd.memset(pick[:, :], 0.0)
                nc.gpsimd.iota(window_i[:, :], [[1, NW]], base=1, channel_multiplier=0)
                pool.drain()
                nc.gpsimd.affine_select(out=follow[:, :], in_=follow[:, :], compare_op=ALU.not_equal, fill=1.0,
                                        base=1, pattern=[[-1, P]], channel_multiplier=1)
                nc.gpsimd.affine_select(out=carry[:, :], in_=carry[:, :], compare_op=ALU.not_equal, fill=1.0,
                                        base=1 - P, pattern=[[-P, P]], channel_multiplier=1)
                nc.gpsimd.affine_select(out=pick[:, :], in_=pick[:, :], compare_op=ALU.not_equal, fill=1.0,
                                        base=1 - P, pattern=[[0, P]], channel_multiplier=1)
                nc.gpsimd.tensor_copy(window[:, :], window_i[:, :])
                pool.drain()
                pool.sem_inc(masks_ready, 1)
                pool.wait_ge(tiles_ready, 1)
                for t in range(NT):
                    pool.indirect_dma_start(run_i[:, t, :], None, d["dst"].rearrange("(c e) -> c e", e=P),
                                            bass.IndirectOffsetOnAxis(ap=tile_i[:, t:t + 1], axis=0)).then_inc(runs_in, 16)
                pool.wait_ge(walk_ready, 1)
                for j in range(SJ):
                    for to, of in ((src_i, d["src"]), (dst_i, d["dst"])):
                        pool.indirect_dma_start(to[:, j, :], None, of.rearrange("(c e) -> c e", e=TPS * P),
                                                bass.IndirectOffsetOnAxis(ap=k["etile_i"][:, j:j + 1], axis=0)).then_inc(rows_in, 16)

            @block.vector
            def _(dve):
                dve.wait_ge(first_in, 16)
                nc.vector.tensor_copy(first_f[:, :], first_i[:, :]).then_inc(first_ready, 1)
                dve.wait_ge(firsts_out, 1)
                nc.vector.tensor_copy(firsts[:, :], pB[:, :, :].rearrange("p a b -> p (a b)")[:, 0:C])
                dve.drain()
                with dve.Fori(0, NT) as t:
                    nc.vector.tensor_scalar(leq[:, :], firsts[:, :], k["node"][:, bass.ds(t, 1)], 0.0, ALU.is_le, ALU.add,
                                            accum_out=tiles_leq[:, bass.ds(t, 1)])
                    dve.drain()
                nc.vector.tensor_scalar(tiles_leq[:, :], tiles_leq[:, :], -1.0, 0.0, ALU.add, ALU.max)
                dve.drain()
                nc.vector.tensor_copy(tile_i[:, :], tiles_leq[:, :]).then_inc(tiles_ready, 1)
                dve.wait_ge(runs_in, 16 * NT)
                nc.vector.tensor_tensor(run_f[:, :, :], run_i[:, :, :], spread(k["node"][:, :], 2, P), ALU.is_le)
                dve.drain()
                nc.vector.tensor_reduce(rowend[:, :], run_f[:, :, :], AX_X, ALU.add)
                dve.drain()
                nc.vector.scalar_tensor_tensor(out=rowend[:, :], in0=tiles_leq[:, :], scalar=float(P), in1=rowend[:, :],
                                               op0=ALU.mult, op1=ALU.add).then_inc(ends_ready, 1)
                dve.wait_ge(starts_out, 1)
                nc.vector.tensor_copy(rowstart[:, :], pR[:, 0:NT])
                nc.vector.tensor_copy(bound_i[:, :], pO[:, 0:NW])
                dve.drain()
                nc.vector.tensor_tensor(k["no_edges"][:, :], rowstart[:, :], rowend[:, :], ALU.is_equal)
                nc.vector.tensor_scalar(tmp[:, :], rowend[:, :], -1.0, 0.0, ALU.add, ALU.max)
                nc.vector.tensor_scalar(bound_i[:, :], bound_i[:, :], BLOCK_BITS, None, ALU.arith_shift_right)
                dve.drain()
                nc.vector.tensor_copy(k["last_i"][:, :], tmp[:, :])
                nc.vector.scalar_tensor_tensor(out=rowstart[:, :], in0=k["no_edges"][:, :], scalar=float(OUT_OF_RANGE),
                                               in1=rowstart[:, :], op0=ALU.mult, op1=ALU.add)
                nc.vector.tensor_tensor(bound[:, :], bound_i[:, :], window[:, :], ALU.add)
                dve.drain()
                nc.vector.tensor_copy(k["start_i"][:, :], rowstart[:, :])
                for j in range(SJ):
                    nc.vector.tensor_scalar(leq_w[:, 0:NW - 1], bound[:, 0:NW - 1], k["node"][:, j:j + 1], 0.0, ALU.is_le,
                                            ALU.add, accum_out=at_window[:, j:j + 1])
                    dve.drain()
                nc.vector.tensor_tensor(etile[:, :], k["node"][:, 0:SJ], at_window[:, :], ALU.subtract)
                nc.vector.tensor_scalar(offset_f[:, :], at_window[:, :], float(W), None, ALU.mult)
                dve.drain()
                nc.vector.tensor_scalar(over[:, :], etile[:, :], float(BLOCKS - 1), float(OUT_OF_RANGE), ALU.is_gt, ALU.mult)
                nc.vector.tensor_scalar(etile[:, :], etile[:, :], float(BLOCKS - 1), None, ALU.min)
                dve.drain()
                nc.vector.tensor_tensor(lift[:, :], offset_f[:, :], over[:, :], ALU.subtract)
                nc.vector.tensor_copy(k["etile_i"][:, :], etile[:, :])
                dve.drain()
                dve.sem_inc(walk_ready, 1)
                dve.wait_ge(offsets_turned, 1)
                nc.vector.tensor_copy(off_t[:, :], pR[0:SJ, 0:P]).then_inc(offsets_ready, 1)
                dve.wait_ge(rows_in, 2 * 16 * SJ)
                nc.vector.tensor_copy(src_f[:, :, :], src_i[:, :, :])
                nc.vector.tensor_tensor(dst_f[:, :, :], dst_i[:, :, :], spread(lift[:, :], 2, TPS * P), ALU.subtract)
                dve.drain()
                dve.sem_inc(rows_ready, 1)
                for a in range(QUADS):
                    dve.wait_ge(turned, a + 1)
                    for n, to in enumerate((k["src_step"], k["place"])):
                        last = nc.vector.tensor_copy(to[:, a * P:(a + 1) * P, :],
                                                     pT[:, a % 2, n * TPS:(n + 1) * TPS, :].rearrange("p u s -> p s u"))
                    last.then_inc(copied, 1)

            @block.tensor
            def _(pe):
                pe.wait_ge(first_ready, 1)
                for a in range(4):
                    w = min(512, C - 512 * a)
                    last = nc.tensor.matmul(pB[:, a, 0:w], k["ones"][0:1, :], first_f[:, 512 * a:512 * a + w], start=True, stop=True)
                last.then_inc(firsts_out, 1)
                pe.wait_ge(masks_ready, 1)
                pe.wait_ge(ends_ready, 1)
                nc.tensor.matmul(pR[:, 0:NT], follow[:, :], rowend[:, :], start=True, stop=False, skip_group_check=True)
                nc.tensor.matmul(pR[:, 1:NT], carry[:, :], rowend[:, 0:NT - 1], start=False, stop=True, skip_group_check=True)
                nc.tensor.matmul(pO[:, 0:NW], pick[:, :], rowend[:, :], start=True, stop=True).then_inc(starts_out, 1)
                pe.wait_ge(walk_ready, 1)
                nc.tensor.transpose(pR[0:SJ, 0:P], offset_f[:, :], k["ident"][:, :]).then_inc(offsets_turned, 1)
                pe.wait_ge(rows_ready, 1)
                for a in range(QUADS):
                    if a >= 2:
                        pe.wait_ge(copied, a - 1)
                    for n, of in enumerate((src_f, dst_f)):
                        for u in range(TPS):
                            last = nc.tensor.transpose(pT[:, a % 2, n * TPS + u, :], of[:, a, u * P:(u + 1) * P], k["ident"][:, :])
                    last.then_inc(turned, 1)


def attention_pass(nc, k, d, layer, H, attn):
    with ExitStack() as ctx:
        m = Memory(nc, ctx, f"attn{layer}")
        CHUNKS = [range(t, min(t + CHUNK, ROW_TILES)) for t in range(0, ROW_TILES, CHUNK)]
        NQ = len(CHUNKS)
        src_row = m.sb("src_row", [P, C], I32)
        part_i = m.sb("part_i", [P, C], I32)
        place_in_tile = m.sb("place_in_tile", [P, ROW_TILES * P], BF16)
        node_tile = m.sb("node_tile", [P, ROW_TILES * P], BF16)
        eye = m.sb("eye", [P, P], BF16)
        far = m.sb("far", [NT, H, NT], BF16)
        minus = m.sb("minus", [P, 1])
        left = m.sb("left", [P, H, NT])
        table = m.sb("table", [P, 3, H, NT], BF16)
        one_hot = m.sb("one_hot", [P, 2, CHUNK * P], BF16)
        distance = m.sb("distance", [NT, 2, CHUNK * P], BF16)
        dst_row = m.sb("dst_row", [P, C], I32)
        dst_before = m.sb("dst_before", [P, C], I32)
        same = m.sb("same", [P, C])
        reset = m.sb("reset", [P, C])
        zero = m.sb("zero", [P, C])
        first_scan = m.sb("first_scan", [P, C])
        term = m.sb("term", [P, C, H])
        scan = m.sb("scan", [P, C, H])
        target = m.sb("target", [P, C, 2 * H])
        node_in = m.sb("node_in", [P, NT, H])
        node_out = m.sb("node_out", [P, NT, 2 * H])
        logit = m.sb("logit", [P, NT, H])
        peak = m.sb("peak", [P, NT, H])
        through = m.sb("through", [P, 1])
        flags = m.sb("flags", [P, 2, 2 * H])
        ends = m.sb("ends", [P, 2 * H])
        row_flags = m.sb("row_flags", [2 * H, P])
        row_ends = m.sb("row_ends", [2 * H, P])
        row_scan = m.sb("row_scan", [2 * H, P + 1])
        carried = m.sb("carried", [P, 2 * H])
        pPlace = m.ps("pPlace", [P, 2, 512])
        pTile = m.ps("pTile", [P, 2, 512])
        pTerm = m.ps("pTerm", [P, 2, CHUNK // 2, 512])
        pF, pE, pK = pPlace[:, 0, :], pPlace[:, 1, :], pTile[:, 0, :]
        by_place = target[:, :, :].rearrange("p c h -> p (c h)")[:, 0:P * ROW_TILES * H].rearrange("p (r j h) -> p r j h", r=P, h=H)
        lookup_ready = m.sem("lookup_ready")
        spread_out = m.sem("spread_out")
        one_hot_ready = m.sem("one_hot_ready", starts=2)
        distance_ready = m.sem("distance_ready", starts=2)
        picked = m.sem("picked", starts=2)
        reduced = m.sem("reduced", starts=2)
        all_reduced = m.sem("all_reduced")
        turned = m.sem("turned")
        copied = m.sem("copied")
        rows_in = m.sem("rows_in")
        zero_ready = m.sem("zero_ready")
        zeros_stored = m.sem("zeros_stored")
        carry_in = m.sem("carry_in")
        carry_turned = m.sem("carry_turned")
        carry_scanned = m.sem("carry_scanned")
        carry_back = m.sem("carry_back")
        peaks_ready = m.sem("peaks_ready")
        peaks_stored = m.sem("peaks_stored")
        node_peaks_in = m.swdge_sem("node_peaks_in")
        self_ready = m.sem("self_ready")
        self_done = m.sem("self_done")
        node_ready = m.sem("node_ready")
        node_scattered = m.swdge_sem("node_scattered")
        target_in = m.sem("target_in")
        logits_ready = m.sem("logits_ready")
        weights_ready = m.sem("weights_ready")
        weights_stored = m.sem("weights_stored")
        sums_ready = m.sem("sums_ready")
        sums_stored = m.sem("sums_stored")
        node_sums_in = m.swdge_sem("node_sums_in")
        SCANS = [(H, True), (2 * H, False), (H, False)]

        def tile_edges(t):
            return min(P, C - t * P)

        def chunk_edges(q):
            return P * len(CHUNKS[q])

        def g_half(q):
            assert NQ % 2 == 0
            return q % 2

        def flat(ap):
            return ap.rearrange("p c h -> p (c h)")

        def dram_rows(ap):
            return ap.rearrange("(p c) h -> p (c h)", p=P)

        m.clear_semaphores()
        with nc.Block() as block:

            @block.sync
            def _(sp):
                sp.dma_start(src_row[:, :], d["src"].rearrange("(p c) -> p c", p=P)).then_inc(rows_in, 16)
                sp.dma_start(dst_row[:, :], d["dst"].rearrange("(p c) -> p c", p=P)).then_inc(rows_in, 16)
                sp.dma_start(dst_before[:, :], d["dst_ext"][0:EP].rearrange("(p c) -> p c", p=P)).then_inc(rows_in, 16)
                sp.wait_ge(zero_ready, 1)
                for a in range(2 * H):
                    sp.dma_start(dram_rows(d["spread"][H])[:, a * C:(a + 1) * C], zero[:, :]).then_inc(zeros_stored, 16)
                sp.wait_ge(peaks_ready, 1)
                sp.dma_start(dram_rows(d["scanned"][H]), flat(scan[:, :, :])).then_inc(peaks_stored, 16)
                sp.wait_ge(node_scattered, 16 * NT)
                sp.dma_start(flat(target[:, :, :]), dram_rows(d["spread"][H])).then_inc(target_in, 16)
                sp.wait_ge(weights_ready, 1)
                sp.dma_start(dram_rows(d["weights"][H]), flat(term[:, :, :])).then_inc(weights_stored, 16)
                sp.wait_ge(sums_ready, 1)
                sp.dma_start(dram_rows(d["sums"][H]), flat(scan[:, :, :])).then_inc(sums_stored, 16)
                sp.wait_ge(weights_stored, 16)
                sp.wait_ge(sums_stored, 16)

            @block.scalar
            def _(act):
                def distances(g, q):
                    n = chunk_edges(q)
                    act.wait_ge(spread_out, g + 1)
                    act.wait_ge(picked, g + 1)
                    nc.scalar.activation(distance[:, g_half(q), 0:n], pTile[0:NT, g_half(q), 0:n], ACT.Square,
                                         bias=minus[0:NT, 0:1]).then_inc(distance_ready, 1)

                act.wait_ge(lookup_ready, 1)
                with act.Fori(0, P) as row:
                    for q in range(NQ):
                        distances(row * NQ + q, q)
                act.wait_ge(self_ready, 1)
                nc.scalar.activation(k["self_weight"][:, :, 0:H], logit[:, :, :], ACT.Exp).then_inc(self_done, 1)
                act.wait_ge(logits_ready, 1)
                nc.scalar.activation(flat(term[:, :, :]), flat(term[:, :, :]), ACT.Exp).then_inc(weights_ready, 1)

            @block.gpsimd
            def _(pool):
                def gather_last(table, done):
                    for t in range(NT):
                        pool.indirect_dma_start(node_in[:, t, :], None, table,
                                                bass.IndirectOffsetOnAxis(ap=k["last_i"][:, t:t + 1], axis=0)).then_inc(done, 16)

                pool.wait_ge(peaks_stored, 16)
                gather_last(d["scanned"][H], node_peaks_in)
                pool.wait_ge(node_ready, 1)
                pool.wait_ge(zeros_stored, 16 * 2 * H)
                for t in range(NT):
                    pool.indirect_dma_start(d["spread"][H], bass.IndirectOffsetOnAxis(ap=k["start_i"][:, t:t + 1], axis=0),
                                            node_out[:, t, :], None, bounds_check=EP - 1, oob_is_err=False
                                            ).then_inc(node_scattered, 16)
                pool.wait_ge(sums_stored, 16)
                gather_last(d["sums"][H], node_sums_in)

            @block.tensor
            def _(pe):
                def spread_row(row, g, q):
                    n, first = chunk_edges(q), CHUNKS[q][0] * P
                    pe.wait_ge(one_hot_ready, g + 1)
                    pe.wait_ge(distance_ready, g + 1)
                    nc.tensor.matmul(pPlace[:, g_half(q), 0:n], eye[:, bass.ds(row, 1)].to_broadcast([P, P]),
                                     place_in_tile[:, first:first + n], start=True, stop=True)
                    nc.tensor.matmul(pTile[0:NT, g_half(q), 0:n], eye[:, bass.ds(row, 1)].to_broadcast([P, NT]),
                                     node_tile[:, first:first + n], start=True, stop=True).then_inc(spread_out, 1)

                def pick(g, q):
                    pe.wait_ge(one_hot_ready, g + 3)
                    pe.wait_ge(distance_ready, g + 3)
                    pe.wait_ge(reduced, g + 1)
                    for t in CHUNKS[q]:
                        u = t % CHUNK
                        edges = slice(u * P, (u + 1) * P)
                        to = pTerm[:, g_half(q), u // 2, u % 2 * H * NT:(u % 2 + 1) * H * NT]
                        nc.tensor.matmul(to, distance[:, g_half(q), edges], far[:, :, :].rearrange("p h t -> p (h t)"),
                                         start=True, stop=False)
                        for part in range(3):
                            last = nc.tensor.matmul(to, one_hot[:, g_half(q), edges],
                                                    table[:, part, :, :].rearrange("p h t -> p (h t)"),
                                                    start=False, stop=(part == 2))
                    last.then_inc(picked, 1)

                pe.wait_ge(lookup_ready, 1)
                spread_row(0, 0, 0)
                with pe.Fori(0, P - 1) as row:
                    for q in range(NQ):
                        spread_row(row + (q + 1) // NQ, row * NQ + q + 1, (q + 1) % NQ)
                        pick(row * NQ + q, q)
                for q in range(NQ):
                    if q + 1 < NQ:
                        spread_row(P - 1, (P - 1) * NQ + q + 1, q + 1)
                    pick((P - 1) * NQ + q, q)
                pe.wait_ge(all_reduced, 1)
                for j in range(ROW_TILES):
                    e = tile_edges(j)
                    if j >= 2:
                        pe.wait_ge(copied, j - 1)
                    for h in range(H):
                        last = nc.tensor.transpose(pTerm[:, j % 2, 0, h * P:h * P + e], by_place[0:e, :, j, h], k["ident"][0:e, 0:e])
                    last.then_inc(turned, 1)

                for r, (n, _) in enumerate(SCANS):
                    pe.wait_ge(carry_in, r + 1)
                    nc.tensor.transpose(pF[0:n, 0:P], flags[:, 1 if r == 0 else 0, 0:n], k["ident"][:, :])
                    nc.tensor.transpose(pE[0:n, 0:P], ends[:, 0:n], k["ident"][:, :]).then_inc(carry_turned, 1)
                    pe.wait_ge(carry_scanned, r + 1)
                    nc.tensor.transpose(pK[:, 0:n], row_scan[0:n, 0:P], k["ident"][0:n, 0:n]).then_inc(carry_back, 1)

            @block.vector
            def _(dve):
                nc.vector.memset(zero[:, :], 0.0)
                dve.drain()
                dve.sem_inc(zero_ready, 1)
                dve.wait_ge(rows_in, 48)
                nc.vector.tensor_scalar(part_i[:, :], src_row[:, :], P - 1, None, ALU.bitwise_and)
                nc.vector.tensor_scalar(src_row[:, :], src_row[:, :], P.bit_length() - 1, None, ALU.arith_shift_right)
                nc.vector.tensor_copy(eye[:, :], k["ident"][:, :])
                nc.vector.tensor_scalar(far[:, :, :], spread(k["ident"][0:NT, 0:NT], 1, H), -FAR, None, ALU.mult)
                nc.vector.tensor_scalar(minus[:, :], k["node"][:, 0:1], -1.0, None, ALU.mult)
                nc.vector.tensor_copy(left[:, :, :], attn[:, :, 0:H].rearrange("p t h -> p h t"))
                dve.drain()
                nc.vector.tensor_copy(place_in_tile[:, 0:C], part_i[:, :])
                nc.vector.tensor_copy(node_tile[:, 0:C], src_row[:, :])
                nc.vector.memset(place_in_tile[:, C:], 0.0)
                nc.vector.memset(node_tile[:, C:], 0.0)
                for part in range(3):
                    nc.vector.tensor_copy(table[:, part, :, :], left[:, :, :])
                    dve.drain()
                    nc.vector.tensor_tensor(left[:, :, :], left[:, :, :], table[:, part, :, :], ALU.subtract)
                    dve.drain()
                dve.sem_inc(lookup_ready, 1)
                nc.vector.tensor_tensor(same[:, :], dst_row[:, :], dst_before[:, :], ALU.is_equal)
                dve.drain()
                nc.vector.tensor_scalar(reset[:, :], same[:, :], -1.0, BIG, ALU.add, ALU.mult)
                nc.vector.tensor_reduce(through[:, :], same[:, :], AX_X, ALU.min)
                dve.drain()
                nc.vector.tensor_copy(flags[:, 0, :], through[:, 0:1].to_broadcast([P, 2 * H]))
                nc.vector.tensor_scalar(flags[:, 1, :], through[:, 0:1].to_broadcast([P, 2 * H]), -1.0, BIG, ALU.add, ALU.mult)

                def one_hots(g, q):
                    n = chunk_edges(q)
                    dve.wait_ge(spread_out, g + 1)
                    dve.wait_ge(picked, g + 1)
                    nc.vector.tensor_scalar(one_hot[:, g_half(q), 0:n], pPlace[:, g_half(q), 0:n], k["node"][:, 0:1], None,
                                            ALU.is_equal).then_inc(one_hot_ready, 1)

                def reduce_terms(row, g, q):
                    tiles = CHUNKS[q]
                    dve.wait_ge(picked, g + 3)
                    banks, pair = -(-len(tiles) // 2), min(len(tiles), 2)
                    nc.vector.tensor_reduce(
                        by_place[:, bass.ds(row, 1), tiles[0]:tiles[-1] + 1, :].rearrange("p r (b u) h -> p (r b) (u h)", b=banks),
                        pTerm[:, g_half(q), 0:banks, 0:pair * H * NT].rearrange("p b (u t) -> p b u t", t=NT),
                        AX_X, ALU.max).then_inc(reduced, 1)

                one_hots(0, 0)
                with dve.Fori(0, P - 1) as row:
                    for q in range(NQ):
                        one_hots(row * NQ + q + 1, (q + 1) % NQ)
                        reduce_terms(row, row * NQ + q, q)
                for q in range(NQ):
                    if q + 1 < NQ:
                        one_hots((P - 1) * NQ + q + 1, q + 1)
                    reduce_terms(P - 1, (P - 1) * NQ + q, q)
                dve.drain()
                dve.sem_inc(all_reduced, 1)
                for j in range(ROW_TILES):
                    e = tile_edges(j)
                    dve.wait_ge(turned, j + 1)
                    nc.vector.tensor_copy(term[:, j * P:j * P + e, :].rearrange("p c h -> p h c"),
                                          pTerm[:, j % 2, 0, 0:H * P].rearrange("p (h e) -> p h e", h=H)[:, :, 0:e]).then_inc(copied, 1)
                dve.drain()

                def run_scan(r, of, to):
                    n, peak_scan = SCANS[r]
                    mark, op0, op1, empty = (reset, ALU.add, ALU.max, -BIG) if peak_scan else (same, ALU.mult, ALU.add, 0.0)
                    for h in range(n):
                        nc.vector.tensor_tensor_scan(first_scan[:, :], mark[:, :], of(h), empty, op0, op1)
                        dve.drain()
                        nc.vector.tensor_copy(ends[:, h:h + 1], first_scan[:, C - 1:C])
                        dve.drain()
                    dve.sem_inc(carry_in, 1)
                    dve.wait_ge(carry_turned, r + 1)
                    nc.vector.tensor_copy(row_flags[0:n, :], pF[0:n, 0:P])
                    nc.vector.tensor_copy(row_ends[0:n, :], pE[0:n, 0:P])
                    nc.vector.memset(row_scan[0:n, 0:1], empty)
                    dve.drain()
                    nc.vector.tensor_tensor_scan(row_scan[0:n, 1:P + 1], row_flags[0:n, :], row_ends[0:n, :], empty, op0, op1)
                    dve.drain()
                    dve.sem_inc(carry_scanned, 1)
                    dve.wait_ge(carry_back, r + 1)
                    nc.vector.tensor_copy(carried[:, 0:n], pK[:, 0:n])
                    dve.drain()
                    for h in range(n):
                        nc.vector.tensor_tensor_scan(to(h), mark[:, :], of(h), carried[:, h:h + 1], op0, op1)
                    dve.drain()

                def leaky(ap):
                    nc.vector.scalar_tensor_tensor(out=ap, in0=ap, scalar=SLOPE, in1=ap, op0=ALU.mult, op1=ALU.max)
                    dve.drain()

                run_scan(0, lambda h: term[:, :, h], lambda h: scan[:, :, h])
                dve.sem_inc(peaks_ready, 1)
                dve.wait_ge(node_peaks_in, 16 * NT)
                nc.vector.scalar_tensor_tensor(out=peak[:, :, :], in0=spread(k["no_edges"][:, :], 2, H), scalar=-BIG,
                                               in1=node_in[:, :, :], op0=ALU.mult, op1=ALU.add)
                nc.vector.tensor_tensor(logit[:, :, :], attn[:, :, 0:H], attn[:, :, H:2 * H], ALU.add)
                dve.drain()
                nc.vector.tensor_tensor(peak[:, :, :], peak[:, :, :], attn[:, :, 0:H], ALU.max)
                dve.drain()
                nc.vector.tensor_tensor(peak[:, :, :], peak[:, :, :], attn[:, :, H:2 * H], ALU.add)
                dve.drain()
                leaky(logit[:, :, :])
                leaky(peak[:, :, :])
                nc.vector.tensor_tensor(logit[:, :, :], logit[:, :, :], peak[:, :, :], ALU.subtract).then_inc(self_ready, 1)
                nc.vector.tensor_copy(node_out[:, :, 0:H], attn[:, :, H:2 * H])
                nc.vector.tensor_copy(node_out[:, :, H:2 * H], peak[:, :, :])
                dve.drain()
                dve.sem_inc(node_ready, 1)
                dve.wait_ge(target_in, 16)
                run_scan(1, lambda h: target[:, :, h], lambda h: target[:, :, h])
                nc.vector.tensor_tensor(term[:, :, :], term[:, :, :], target[:, :, 0:H], ALU.add)
                dve.drain()
                leaky(term[:, :, :])
                nc.vector.tensor_tensor(term[:, :, :], term[:, :, :], target[:, :, H:2 * H], ALU.subtract).then_inc(logits_ready, 1)
                dve.wait_ge(weights_ready, 1)
                run_scan(2, lambda h: term[:, :, h], lambda h: scan[:, :, h])
                dve.sem_inc(sums_ready, 1)
                dve.wait_ge(node_sums_in, 16 * NT)
                nc.vector.tensor_scalar(logit[:, :, 0], k["no_edges"][:, :], -1.0, 1.0, ALU.mult, ALU.add)
                dve.drain()
                nc.vector.tensor_tensor(node_in[:, :, :], node_in[:, :, :], spread(logit[:, :, 0], 2, H), ALU.mult)
                dve.drain()
                nc.vector.tensor_tensor(node_in[:, :, :], node_in[:, :, :], k["self_weight"][:, :, 0:H], ALU.add)
                dve.drain()
                nc.vector.reciprocal(k["rdenom"][:, :, 0:H], node_in[:, :, :])



def weight_table(nc, k, d, layer, H):
    with ExitStack() as ctx:
        m = Memory(nc, ctx, f"table{layer}")
        rows = m.sb("rows", [P, SJ, TPS * P * H])
        turned = m.sb("turned", [P, 2, P, TPS, H])
        pT = m.ps("pT", [P, 2, TPS, 4, P])
        rows_in = m.swdge_sem("rows_in")
        done = m.sem("done")
        copied = m.sem("copied")
        stored = [m.sem("stored0"), m.sem("stored1")]

        m.clear_semaphores()
        with nc.Block() as block:

            @block.gpsimd
            def _(pool):
                for j in range(SJ):
                    pool.indirect_dma_start(rows[:, j, :], None, d["weights"][H].rearrange("(c e) h -> c (e h)", e=TPS * P),
                                            bass.IndirectOffsetOnAxis(ap=k["etile_i"][:, j:j + 1], axis=0)).then_inc(rows_in, 16)

            @block.tensor
            def _(pe):
                pe.wait_ge(rows_in, 16 * SJ)
                for j in range(SJ):
                    if j >= 2:
                        pe.wait_ge(copied, j - 1)
                    for u in range(TPS):
                        for h in range(H):
                            last = nc.tensor.transpose(pT[:, j % 2, u, h, :],
                                                       rows[:, j, u * P * H:(u + 1) * P * H].rearrange("p (e h) -> p h e", h=H)[:, h, :],
                                                       k["ident"][:, :])
                    last.then_inc(done, 1)

            @block.vector
            def _(dve):
                for j in range(SJ):
                    dve.wait_ge(done, j + 1)
                    if j >= 2:
                        dve.wait_ge(stored[j % 2], 16 * (j // 2))
                    for u in range(TPS):
                        last = nc.vector.tensor_copy(turned[:, j % 2, :, u, :], pT[:, j % 2, u, 0:H, :].rearrange("p h s -> p s h"))
                    last.then_inc(copied, 1)

            @block.sync
            def _(sp):
                for j in range(SJ):
                    sp.wait_ge(copied, j + 1)
                    sp.dma_start(d["step_weights"][H][:, j * P * TPS * H:(j + 1) * P * TPS * H],
                                 turned[:, j % 2, :, :, :].rearrange("p s u h -> p (s u h)")).then_inc(stored[j % 2], 16)
                sp.wait_ge(stored[0], 16 * (-(-SJ // 2)))
                sp.wait_ge(stored[1], 16 * (SJ // 2))


def self_messages(nc, k, d, layer, H, F, acc, table):
    NB = F // P
    with ExitStack() as ctx:
        m = Memory(nc, ctx, f"self{layer}")
        rows = m.sb("rows", [P, U, F])
        diag = m.sb("diag", [P, 2, H, P])
        pM = m.ps("pM", [P, 2, 512])
        rows_in = m.sem("rows_in")
        diag_ready = m.sem("diag_ready")
        multiplied = m.sem("multiplied", starts=1)
        copied = m.sem("copied", starts=1)
        m.clear_semaphores()
        with nc.Block() as block:

            @block.sync
            def _(sp):
                with sp.Fori(0, TRIPS) as i:
                    after(sp, multiplied, i * U)
                    sp.dma_start(rows[:, :, :], table.rearrange("(t p) c -> p t c", p=P)[:, bass.ds(i * U, U), :]).then_inc(rows_in, 16)

            @block.vector
            def _(dve):
                with dve.Fori(0, TRIPS) as i:
                    for j in range(U):
                        t = i * U + j
                        after(dve, multiplied, i * U + max(j - 1, 0))
                        nc.vector.tensor_tensor(diag[:, j % 2, :, :], spread(k["ident"][:, :], 1, H),
                                                spread(k["self_weight"][:, t, 0:H], 2, P), ALU.mult).then_inc(diag_ready, 1)

            @block.tensor
            def _(pe):
                with pe.Fori(0, TRIPS) as i:
                    pe.wait_ge(rows_in, 16 * (i + 1))
                    for j in range(U):
                        t = i * U + j
                        pe.wait_ge(diag_ready, t + 1)
                        after(pe, copied, i * U + max(j - 1, 0))
                        for b in range(NB):
                            last = nc.tensor.matmul(pM[:, j % 2, b * P:(b + 1) * P], rows[:, j, b * P:(b + 1) * P],
                                                    diag[:, j % 2, b % H, :], start=True, stop=True)
                        last.then_inc(multiplied, 1)

            @block.scalar
            def _(act):
                with act.Fori(0, TRIPS) as i:
                    for j in range(U):
                        t = i * U + j
                        after(act, multiplied, t + 1)
                        nc.scalar.copy(acc[:, 0:NB, bass.ds(t * P, P)],
                                       pM[:, j % 2, 0:F].rearrange("p (b n) -> p b n", n=P)).then_inc(copied, 1)


def message_pass(nc, k, d, layer, H, F, acc, table):
    NB = F // P
    GROUPS = -(-STEPS // G)
    WTRIPS = -(-(GROUPS - AHEAD) // RING)
    GT = G * TPS
    assert (WTRIPS * RING + AHEAD) * G <= SP and AHEAD <= SETS and 2 * SETS == RING
    with ExitStack() as ctx:
        m = Memory(nc, ctx, f"walk{layer}")
        index = m.sb("index", [P, RING, G, TPS], I32)
        rows = m.sb("rows", [P, RING, GT, F])
        stepw = m.sb("stepw", [P, 2, SETS * GT * H])
        hit = m.sb("hit", [P, 2, GT, W])
        placed = m.sb("placed", [P, SETS, GT, H, W])
        pM = m.ps("pM", [P, SETS * G, 512])
        index_ready = m.sem("index_ready")
        index_seen = m.sem("index_seen")
        rows_in = [m.swdge_sem(f"rows_in{r}") for r in range(RING)]
        stepw_in = [m.sem("stepw_in0"), m.sem("stepw_in1")]
        hit_ready = m.sem("hit_ready")
        placed_ready = m.sem("placed_ready")
        multiplied = m.sem("multiplied", starts=RING * G)
        added = m.sem("added", starts=SETS * G)

        def loop(eng, body):
            with eng.Fori(0, WTRIPS) as i:
                for r in range(RING):
                    body(i * RING + r, r, i)
            for r in range(AHEAD):
                body(WTRIPS * RING + r, r, WTRIPS)

        m.clear_semaphores()
        with nc.Block() as block:

            @block.sync
            def _(sp):
                def load(q, half, n):
                    sp.dma_start(stepw[:, half, 0:n * GT * H],
                                 d["step_weights"][H][:, bass.ds(q * (GT * H), n * GT * H)]).then_inc(stepw_in[half], 16)

                for half in range(2):
                    load(half * SETS, half, SETS)
                with sp.Fori(1, WTRIPS) as i:
                    for half in range(2):
                        q = i * RING + half * SETS
                        sp.wait_ge(placed_ready, q - SETS)
                        load(q, half, SETS)
                sp.wait_ge(placed_ready, WTRIPS * RING - SETS)
                load(WTRIPS * RING, 0, AHEAD)

            @block.scalar
            def _(act):
                def bring_index(q, r, trip):
                    act.wait_ge(multiplied, q * G + G)
                    nc.scalar.copy(index[:, r, :, :], k["src_step"][:, bass.ds(q * G, G), :]).then_inc(index_ready, 1)

                loop(act, bring_index)

            @block.gpsimd
            def _(pool):
                def gather(q, r, trip):
                    pool.wait_ge(index_ready, q + 1)
                    pool.sem_inc(index_seen, 1)
                    for a in range(G):
                        for u in range(TPS):
                            pool.indirect_dma_start(rows[:, r, a * TPS + u, :], None, table,
                                                    bass.IndirectOffsetOnAxis(ap=index[:, r, a, u:u + 1], axis=0)
                                                    ).then_inc(rows_in[r], 16)

                loop(pool, gather)

            @block.tensor
            def _(pe):
                def multiply(q, r, trip):
                    s = r % SETS
                    pe.wait_ge(placed_ready, q + 1)
                    pe.wait_ge(rows_in[r], (trip + 1) * (16 * GT))
                    for a in range(G):
                        pe.wait_ge(added, q * G + a + 1)
                        for b in range(NB):
                            for u in range(TPS):
                                last = nc.tensor.matmul(pM[:, s * G + a, b * W:(b + 1) * W],
                                                        rows[:, r, a * TPS + u, b * P:(b + 1) * P],
                                                        placed[:, s, a * TPS + u, b % H, :], start=(u == 0), stop=(u == TPS - 1))
                        last.then_inc(multiplied, 1)

                loop(pe, multiply)

            @block.vector
            def _(dve):

                def prepare(q, r, trip):
                    s, half = r % SETS, r // SETS
                    dve.wait_ge(multiplied, (q - SETS) * G + G + RING * G)
                    nc.vector.tensor_tensor(hit[:, r % 2, :, :], spread(k["count"][:, 0:W], 1, GT),
                                            spread(k["place"][:, bass.ds(q * G, G), :].rearrange("p g u -> p (g u)"), 2, W),
                                            ALU.is_equal).then_inc(hit_ready, 1)
                    dve.wait_ge(stepw_in[half], 16 * (trip + 1))
                    dve.wait_ge(hit_ready, q + 1)
                    nc.vector.tensor_tensor(placed[:, s, :, :, :], spread(hit[:, r % 2, :, :], 2, H),
                                            spread(stepw[:, half, s * GT * H:(s + 1) * GT * H].rearrange("p (g h) -> p g h", h=H), 3, W),
                                            ALU.mult).then_inc(placed_ready, 1)

                def add(q, r):
                    for a in range(G):
                        node = dve.value_load(k["offset"][0:1, bass.ds(q * G + a, 1)], min_val=0, max_val=NP - W)
                        dve.wait_ge(multiplied, q * G + a + 1 + RING * G)
                        dve.wait_ge(added, q * G + a + SETS * G)
                        to = acc[:, 0:NB, bass.ds(node, W)]
                        nc.vector.tensor_tensor(to, pM[:, r % SETS * G + a, 0:NB * W].rearrange("p (b w) -> p b w", w=W), to,
                                                ALU.add).then_inc(added, 1)

                for q in range(AHEAD):
                    prepare(q, q, 0)
                with dve.Fori(0, WTRIPS) as i:
                    for r in range(RING):
                        prepare(i * RING + r + AHEAD, (r + AHEAD) % RING, i + (r + AHEAD) // RING)
                        add(i * RING + r, r)
                for r in range(AHEAD):
                    add(WTRIPS * RING + r, r)


def finish_layer1(nc, k, d, acc):
    NB = F1 // P
    with ExitStack() as ctx:
        m = Memory(nc, ctx, "finish1")
        w2 = m.sb("w2", [P, NB, D])
        avec = m.sb("avec", [P, 2, D])
        aprod = m.sb("aprod", [P, NB, D])
        wa = m.sb("wa", [P, NB, 2])
        bias = m.sb("bias", [P, NB])
        slope = m.sb("slope", [P, 1])
        diag = m.sb("diag", [P, 2, HEADS1, P])
        norm = m.sb("norm", [P, 2, NB, P])
        pos = m.sb("pos", [P, 2, NB, P])
        neg = m.sb("neg", [P, 2, NB, P])
        z = m.sb("z", [P, 2, NB, P])
        h_out = m.sb("h_out", [P, U, D])
        pR = m.ps("pR", [P, 2, 512])
        pH = m.ps("pH", [P, 2, 512])
        pA = m.ps("pA", [P, 512])
        weights_in = m.sem("weights_in")
        weights_ready = m.sem("weights_ready")
        diag_ready = m.sem("diag_ready")
        spread_out = m.sem("spread_out")
        normed = m.sem("normed")
        pos_ready = m.sem("pos_ready")
        z_ready = m.sem("z_ready")
        multiplied = m.sem("multiplied", starts=1)
        a_copied = m.sem("a_copied", starts=1)
        h_copied = m.sem("h_copied", starts=1)
        h_stored = m.sem("h_stored")
        h_free = m.sem("h_free", starts=1)
        m.clear_semaphores()
        with nc.Block() as block:

            @block.sync
            def _(sp):
                loads = [(w2[:, :, :], d["w2"].rearrange("(b p) c -> p b c", p=P)), (avec[:, 0:1, :], d["a_src2"].partition_broadcast(P)),
                         (avec[:, 1:2, :], d["a_dst2"].partition_broadcast(P)), (slope[:, :], d["prelu_w"].partition_broadcast(P))]
                for to, of in loads:
                    sp.dma_start(to, of).then_inc(weights_in, 16)
                sp.dma_start(bias[:, :], d["b1"].rearrange("(b p) -> p b", p=P), allow_slow_non_contiguous=True).then_inc(weights_in, 16)
                with sp.Fori(0, TRIPS) as i:
                    after(sp, h_copied, (i + 1) * U)
                    sp.dma_start(d["h2"].rearrange("(t p) c -> p t c", p=P)[:, bass.ds(i * U, U), :], h_out[:, :, :]).then_inc(h_stored, 16)
                    sp.wait_ge(h_stored, 16 * (i + 1))
                    sp.sem_inc(h_free, 1)
                sp.wait_ge(h_stored, 16 * TRIPS)

            @block.vector
            def _(dve):
                dve.wait_ge(weights_in, 16 * 5)
                for s in range(2):
                    nc.vector.tensor_tensor(aprod[:, :, :], w2[:, :, :], spread(avec[:, s, :], 1, NB), ALU.mult)
                    dve.drain()
                    nc.vector.tensor_reduce(wa[:, :, s], aprod[:, :, :], AX_X, ALU.add)
                    dve.drain()
                dve.sem_inc(weights_ready, 1)

                def diagonal(t, j):
                    nc.vector.tensor_tensor(diag[:, j % 2, :, :], spread(k["ident"][:, :], 1, HEADS1),
                                            spread(k["rdenom"][:, t, :], 2, P), ALU.mult).then_inc(diag_ready, 1)

                with dve.Fori(0, TRIPS) as i:
                    diagonal(i * U, 0)
                    for j in range(U):
                        t = i * U + j
                        b = j % 2
                        if j + 1 < U:
                            diagonal(t + 1, j + 1)
                        dve.wait_ge(spread_out, t + 1)
                        nc.vector.tensor_tensor(norm[:, b, :, :], acc[:, 0:NB, bass.ds(t * P, P)],
                                                pR[:, b, :].rearrange("p (b n) -> p b n", n=P), ALU.mult)
                        dve.drain()
                        nc.vector.tensor_tensor(norm[:, b, :, :], norm[:, b, :, :], spread(bias[:, :], 2, P), ALU.add)
                        dve.drain()
                        dve.sem_inc(normed, 1)
                        nc.vector.tensor_scalar(neg[:, b, :, :], norm[:, b, :, :], 0.0, slope[:, 0:1], ALU.min, ALU.mult)
                        dve.drain()
                        dve.wait_ge(pos_ready, t + 1)
                        after(dve, multiplied, i * U + max(j - 1, 0))
                        nc.vector.tensor_tensor(z[:, b, :, :], pos[:, b, :, :], neg[:, b, :, :], ALU.add).then_inc(z_ready, 1)
                        after(dve, multiplied, t + 1)
                        nc.vector.tensor_copy(k["attn2"][:, t, :], pA[:, 0:2]).then_inc(a_copied, 1)

            @block.scalar
            def _(act):
                with act.Fori(0, TRIPS) as i:
                    for j in range(U):
                        t = i * U + j
                        act.wait_ge(normed, t + 1)
                        nc.scalar.activation(pos[:, j % 2, :, :], norm[:, j % 2, :, :], ACT.Relu).then_inc(pos_ready, 1)
                        after(act, multiplied, t + 1)
                        act.wait_ge(h_free, i + 1)
                        nc.scalar.copy(h_out[:, j, :], pH[:, j % 2, 0:D]).then_inc(h_copied, 1)

            @block.tensor
            def _(pe):
                pe.wait_ge(weights_ready, 1)

                def spread_norm(t, j):
                    pe.wait_ge(diag_ready, t + 1)
                    nc.tensor.matmul(pR[:, j % 2, :], k["ones"][:, :], diag[:, j % 2, :, :].rearrange("p h n -> p (h n)"),
                                     start=True, stop=True).then_inc(spread_out, 1)

                with pe.Fori(0, TRIPS) as i:
                    spread_norm(i * U, 0)
                    for j in range(U):
                        t = i * U + j
                        if j + 1 < U:
                            spread_norm(t + 1, j + 1)
                        pe.wait_ge(z_ready, t + 1)
                        after(pe, h_copied, i * U + max(j - 1, 0))
                        after(pe, a_copied, t)
                        for b in range(NB):
                            nc.tensor.matmul(pH[:, j % 2, 0:D], z[:, j % 2, b, :], w2[:, b, :], start=(b == 0), stop=(b == NB - 1))
                        for b in range(NB):
                            last = nc.tensor.matmul(pA[:, 0:2], z[:, j % 2, b, :], wa[:, b, :], start=(b == 0), stop=(b == NB - 1))
                        last.then_inc(multiplied, 1)


def finish_layer2(nc, k, d, acc):
    with ExitStack() as ctx:
        m = Memory(nc, ctx, "finish2")
        x1 = m.sb("x1", [P, NT, D])
        y = m.sb("y", [P, NT, D])
        part = m.sb("part", [P, 2, DK, P])
        basein = m.sb("basein", [P, U, D])
        stats = m.sb("stats", [P, NT, 6])
        mean = m.sb("mean", [P, NT])
        half = m.sb("half", [P, NT])
        var = m.sb("var", [P, NT])
        rstd = m.sb("rstd", [P, NT])
        eps = m.sb("eps", [P, 1])
        yT = m.sb("yT", [P, 2, DK, P])
        ycur = m.sb("ycur", [P, 2, D])
        wg = m.sb("wg", [P, DK, NEXP])
        bg = m.sb("bg", [P, NEXP])
        logits = m.sb("logits", [P, NT, NEXP])
        code = m.sb("code", [P, NT, NEXP])
        first = m.sb("first", [P, NT, NEXP])
        second = m.sb("second", [P, NT, NEXP])
        work = m.sb("work", [P, NT, NEXP])
        rank8 = m.sb("rank8", [P, NEXP])
        top = m.sb("top", [P, 2, NT])
        best = m.sb("best", [P, NT])
        valid = m.sb("valid", [P, NT])
        tri = m.sb("tri", [P, P])
        before = m.sb("before", [P, NT, NEXP])
        total = m.sb("total", [P, NT, NEXP])
        ones_row = m.sb("ones_row", [P, NT])
        tiles_i = m.sb("tiles_i", [P, NEXP], I32)
        tiles_f = m.sb("tiles_f", [P, NEXP])
        tile_start = m.sb("tile_start", [P, NEXP])
        expert = m.sb("expert", [1, TT])
        zero = m.sb("zero", [P, SLOTS * D // P // 30])
        pT = m.ps("pT", [P, 2, 512])
        pG = m.ps("pG", [P, 2, 512])
        pB = m.ps("pB", [P, 512])
        pC = m.ps("pC", [P, 512])
        loads_in = m.sem("loads_in")
        zero_ready = m.sem("zero_ready")
        zeros_stored = m.sem("zeros_stored")
        tri_ready = m.sem("tri_ready")
        base_in = m.sem("base_in")
        part_ready = m.sem("part_ready")
        turned = m.sem("turned", starts=1)
        x1_ready = m.sem("x1_ready", starts=1)
        x1_stored = m.sem("x1_stored")
        stats_done = m.sem("stats_done")
        root_done = m.sem("root_done")
        y_ready = m.sem("y_ready")
        y_turned = m.sem("y_turned", starts=1)
        yT_ready = m.sem("yT_ready")
        gated = m.sem("gated")
        logits_ready = m.sem("logits_ready", starts=1)
        gap_ready = m.sem("gap_ready")
        gap_done = m.sem("gap_done")
        chosen = m.sem("chosen")
        counted = m.sem("counted")
        slots_ready = m.sem("slots_ready")
        scattered = m.swdge_sem("scattered")

        m.clear_semaphores()
        with nc.Block() as block:

            @block.sync
            def _(sp):
                sp.dma_start(wg[:, :, :], d["wg"].rearrange("(k p) e -> p k e", p=P)).then_inc(loads_in, 16)
                sp.dma_start(bg[:, :], d["bg"].partition_broadcast(P)).then_inc(loads_in, 16)
                sp.dma_start(valid[:, :], d["valid"]).then_inc(loads_in, 16)
                sp.wait_ge(zero_ready, 1)
                for a in range(30):
                    w = SLOTS * D // P // 30
                    sp.dma_start(d["xs"].rearrange("(p s) c -> p (s c)", p=P)[:, a * w:(a + 1) * w], zero[:, :]).then_inc(zeros_stored, 16)
                with sp.Fori(0, TRIPS) as i:
                    after(sp, x1_ready, i * U)
                    sp.dma_start(basein[:, :, :], d["base"].rearrange("(t p) c -> p t c", p=P)[:, bass.ds(i * U, U), :]).then_inc(base_in, 16)
                after(sp, x1_ready, NT)
                sp.dma_start(d["x1"].rearrange("(t p) c -> p t c", p=P), x1[:, :, :]).then_inc(x1_stored, 16)
                sp.wait_ge(x1_stored, 16)

            @block.gpsimd
            def _(pool):
                nc.gpsimd.memset(tri[:, :], 1.0)
                nc.gpsimd.memset(zero[:, :], 0.0)
                pool.drain()
                pool.sem_inc(zero_ready, 1)
                nc.gpsimd.affine_select(out=tri[:, :], in_=tri[:, :], compare_op=ALU.is_gt, fill=0.0,
                                        base=0, pattern=[[1, P]], channel_multiplier=-1)
                pool.drain()
                pool.sem_inc(tri_ready, 1)
                pool.wait_ge(slots_ready, 1)
                pool.wait_ge(zeros_stored, 480)
                for s in range(2):
                    for t in range(NT):
                        pool.indirect_dma_start(d["xs"], bass.IndirectOffsetOnAxis(ap=k["slot_out"][:, s, t:t + 1], axis=0),
                                                y[:, t, :], None, bounds_check=SLOTS - 1, oob_is_err=False).then_inc(scattered, 16)
                pool.wait_ge(scattered, 16 * 2 * NT)

            @block.scalar
            def _(act):
                with act.Fori(0, TRIPS) as i:
                    for j in range(U):
                        t = i * U + j
                        after(act, turned, i * U + max(j - 1, 0))
                        nc.scalar.copy(part[:, j % 2, :, :], acc[:, 0:DK, bass.ds(t * P, P)]).then_inc(part_ready, 1)
                act.wait_ge(stats_done, 1)
                nc.scalar.activation(half[:, :], var[:, :], ACT.Sqrt, bias=eps[:, 0:1]).then_inc(root_done, 1)
                with act.Fori(0, TRIPS) as i:
                    for j in range(U):
                        after(act, y_turned, i * U + j + 1)
                        nc.scalar.copy(yT[:, j % 2, :, :].rearrange("p k n -> p (k n)"), pT[:, j % 2, 0:D]).then_inc(yT_ready, 1)
                act.wait_ge(gap_ready, 1)
                nc.scalar.activation(best[:, :], best[:, :], ACT.Exp).then_inc(gap_done, 1)

            @block.tensor
            def _(pe):
                with pe.Fori(0, TRIPS) as i:
                    for j in range(U):
                        t = i * U + j
                        pe.wait_ge(part_ready, t + 1)
                        after(pe, x1_ready, i * U + max(j - 1, 0))
                        for kk in range(DK):
                            last = nc.tensor.transpose(pT[:, j % 2, kk * P:(kk + 1) * P], part[:, j % 2, kk, :], k["ident"][:, :])
                        last.then_inc(turned, 1)
                pe.wait_ge(loads_in, 48)
                with pe.Fori(0, TRIPS) as i:
                    for j in range(U):
                        t = i * U + j
                        pe.wait_ge(y_ready, t + 1)
                        for kk in range(DK):
                            last = nc.tensor.transpose(pT[:, j % 2, kk * P:(kk + 1) * P], ycur[:, j % 2, kk * P:(kk + 1) * P],
                                                       k["ident"][:, :])
                        last.then_inc(y_turned, 1)
                        pe.wait_ge(yT_ready, t + 1)
                        after(pe, logits_ready, i * U + max(j - 1, 0))
                        for kk in range(DK):
                            last = nc.tensor.matmul(pG[:, j % 2, 0:NEXP], yT[:, j % 2, kk, :], wg[:, kk, :],
                                                    start=(kk == 0), stop=(kk == 1))
                        last.then_inc(gated, 1)
                pe.wait_ge(tri_ready, 1)
                pe.wait_ge(chosen, 1)
                nc.tensor.matmul(pB[:, 0:NT * NEXP], tri[:, :], work[:, :, :].rearrange("p t e -> p (t e)"), start=True, stop=True)
                nc.tensor.matmul(pC[:, 0:NT * NEXP], k["ones"][:, :], work[:, :, :].rearrange("p t e -> p (t e)"),
                                 start=True, stop=True).then_inc(counted, 1)

            @block.vector
            def _(dve):
                nc.vector.memset(eps[:, :], EPS)
                nc.vector.memset(ones_row[:, :], 1.0)
                with dve.Fori(0, TRIPS) as i:
                    dve.wait_ge(base_in, 16 * (i + 1))
                    for j in range(U):
                        t = i * U + j
                        after(dve, turned, t + 1)
                        nc.vector.scalar_tensor_tensor(out=x1[:, t, :], in0=pT[:, j % 2, 0:D], scalar=k["rdenom"][:, t, 0:1],
                                                       in1=basein[:, j, :], op0=ALU.mult, op1=ALU.add).then_inc(x1_ready, 1)
                dve.drain()
                with dve.Fori(0, NT) as t:
                    nc.vector.bn_stats(stats[:, t, :], x1[:, t, :])
                dve.drain()
                nc.vector.tensor_tensor(mean[:, :], stats[:, :, 1], stats[:, :, 4], ALU.add)
                nc.vector.tensor_tensor(half[:, :], stats[:, :, 1], stats[:, :, 4], ALU.subtract)
                nc.vector.tensor_tensor(var[:, :], stats[:, :, 2], stats[:, :, 5], ALU.add)
                dve.drain()
                nc.vector.tensor_scalar(mean[:, :], mean[:, :], 0.5, None, ALU.mult)
                nc.vector.tensor_tensor(half[:, :], half[:, :], half[:, :], ALU.mult)
                nc.vector.tensor_scalar(var[:, :], var[:, :], 1.0 / D, None, ALU.mult)
                dve.drain()
                nc.vector.scalar_tensor_tensor(out=var[:, :], in0=half[:, :], scalar=0.25, in1=var[:, :],
                                               op0=ALU.mult, op1=ALU.add).then_inc(stats_done, 1)
                dve.wait_ge(root_done, 1)
                newton(nc, dve, rstd, half, var)
                with dve.Fori(0, TRIPS) as i:
                    for j in range(U):
                        t = i * U + j
                        after(dve, y_turned, i * U + max(j - 1, 0))
                        nc.vector.tensor_scalar(y[:, t, :], x1[:, t, :], mean[:, bass.ds(t, 1)], rstd[:, bass.ds(t, 1)],
                                                ALU.subtract, ALU.mult)
                        dve.drain()
                        nc.vector.tensor_copy(ycur[:, j % 2, :], y[:, t, :]).then_inc(y_ready, 1)
                        if j == 0:
                            dve.wait_ge(loads_in, 48)
                        else:
                            dve.wait_ge(gated, t)
                            nc.vector.tensor_tensor(logits[:, t - 1, :], pG[:, (j - 1) % 2, 0:NEXP], bg[:, :], ALU.add).then_inc(logits_ready, 1)
                    dve.wait_ge(gated, i * U + U)
                    nc.vector.tensor_tensor(logits[:, i * U + U - 1, :], pG[:, (U - 1) % 2, 0:NEXP], bg[:, :], ALU.add).then_inc(logits_ready, 1)
                nc.vector.tensor_scalar(rank8[:, :], k["count"][:, 0:NEXP], -1.0, float(NEXP), ALU.mult, ALU.add)
                dve.drain()
                for s, to in enumerate((first, second)):
                    nc.vector.tensor_reduce(top[:, s, :], logits[:, :, :], AX_X, ALU.max)
                    dve.drain()
                    nc.vector.tensor_tensor(code[:, :, :], logits[:, :, :], spread(top[:, s, :], 2, NEXP), ALU.is_equal)
                    dve.drain()
                    nc.vector.tensor_tensor(code[:, :, :], code[:, :, :], spread(rank8[:, :], 1, NT), ALU.mult)
                    dve.drain()
                    nc.vector.tensor_reduce(best[:, :], code[:, :, :], AX_X, ALU.max)
                    dve.drain()
                    nc.vector.tensor_tensor(to[:, :, :], code[:, :, :], spread(best[:, :], 2, NEXP), ALU.is_equal)
                    dve.drain()
                    if s == 0:
                        nc.vector.scalar_tensor_tensor(out=logits[:, :, :], in0=to[:, :, :], scalar=-BIG, in1=logits[:, :, :],
                                                       op0=ALU.mult, op1=ALU.add)
                        dve.drain()
                nc.vector.tensor_tensor(best[:, :], top[:, 1, :], top[:, 0, :], ALU.subtract).then_inc(gap_ready, 1)
                nc.vector.tensor_tensor(work[:, :, :], first[:, :, :], second[:, :, :], ALU.add)
                dve.drain()
                nc.vector.tensor_tensor(work[:, :, :], work[:, :, :], spread(valid[:, :], 2, NEXP), ALU.mult).then_inc(chosen, 1)
                dve.wait_ge(gap_done, 1)
                nc.vector.tensor_scalar(half[:, :], best[:, :], 1.0, None, ALU.add)
                dve.drain()
                nc.vector.reciprocal(k["mix_weight"][:, 0, :], half[:, :])
                dve.drain()
                nc.vector.tensor_tensor(k["mix_weight"][:, 1, :], k["mix_weight"][:, 0, :], best[:, :], ALU.mult)
                dve.wait_ge(counted, 1)
                nc.vector.tensor_copy(code[:, :, :].rearrange("p t e -> p (t e)"), pC[:, 0:NT * NEXP])
                nc.vector.tensor_copy(before[:, :, :].rearrange("p t e -> p (t e)"), pB[:, 0:NT * NEXP])
                dve.drain()
                for e in range(NEXP):
                    nc.vector.tensor_tensor_scan(total[:, :, e], ones_row[:, :], code[:, :, e], 0.0, ALU.mult, ALU.add)
                dve.drain()
                nc.vector.tensor_scalar(tiles_f[:, :], total[:, NT - 1, :], float(P - 1), None, ALU.add)
                nc.vector.tensor_tensor(before[:, :, :], before[:, :, :], total[:, :, :], ALU.add)
                dve.drain()
                nc.vector.tensor_tensor(before[:, :, :], before[:, :, :], code[:, :, :], ALU.subtract)
                nc.vector.tensor_copy(tiles_i[:, :], tiles_f[:, :])
                dve.drain()
                nc.vector.tensor_scalar(tiles_i[:, :], tiles_i[:, :], 7, None, ALU.arith_shift_right)
                dve.drain()
                nc.vector.tensor_copy(tiles_f[:, :], tiles_i[:, :])
                dve.drain()
                nc.vector.tensor_tensor_scan(tile_start[:, :], ones_row[:, 0:NEXP], tiles_f[:, :], 0.0, ALU.mult, ALU.add)
                dve.drain()
                nc.vector.tensor_tensor(tile_start[:, :], tile_start[:, :], tiles_f[:, :], ALU.subtract)
                dve.drain()
                nc.vector.scalar_tensor_tensor(out=before[:, :, :], in0=spread(tile_start[:, :], 1, NT), scalar=float(P),
                                               in1=before[:, :, :], op0=ALU.mult, op1=ALU.add)
                nc.vector.memset(expert[:, :], 0.0)
                nc.vector.tensor_scalar(half[:, :], valid[:, :], -float(OUT_OF_RANGE), float(OUT_OF_RANGE), ALU.mult, ALU.add)
                dve.drain()
                for s, of in enumerate((first, second)):
                    nc.vector.tensor_tensor(code[:, :, :], of[:, :, :], before[:, :, :], ALU.mult)
                    dve.drain()
                    nc.vector.tensor_reduce(mean[:, :], code[:, :, :], AX_X, ALU.add)
                    dve.drain()
                    nc.vector.tensor_tensor(mean[:, :], mean[:, :], half[:, :], ALU.add)
                    dve.drain()
                    nc.vector.tensor_copy(k["slot_out"][:, s, :], mean[:, :])
                    nc.vector.tensor_scalar(var[:, :], mean[:, :], float(SLOTS - 1), None, ALU.min)
                    dve.drain()
                    nc.vector.tensor_copy(k["slot_in"][:, s, :], var[:, :])
                dve.drain()
                dve.sem_inc(slots_ready, 1)
                for e in range(1, NEXP):
                    nc.vector.scalar_tensor_tensor(out=expert[:, :], in0=k["count"][0:1, 0:TT], scalar=tile_start[0:1, e:e + 1],
                                                   in1=expert[:, :], op0=ALU.is_ge, op1=ALU.add)
                    dve.drain()
                nc.vector.tensor_copy(k["expert"][:, :], expert[:, :])


def newton(nc, dve, rstd, root, var):
    nc.vector.reciprocal(rstd[:, :], root[:, :])
    nc.vector.tensor_scalar(var[:, :], var[:, :], EPS, None, ALU.add)
    dve.drain()
    nc.vector.tensor_tensor(root[:, :], rstd[:, :], rstd[:, :], ALU.mult)
    dve.drain()
    nc.vector.tensor_tensor(root[:, :], root[:, :], var[:, :], ALU.mult)
    dve.drain()
    nc.vector.tensor_scalar(root[:, :], root[:, :], -0.5, 1.5, ALU.mult, ALU.add)
    dve.drain()
    nc.vector.tensor_tensor(rstd[:, :], rstd[:, :], root[:, :], ALU.mult)
    dve.drain()


def expert_pass(nc, k, d):
    HC = HID // P
    ETRIPS = TT // U
    assert ETRIPS * U == TT
    with ExitStack() as ctx:
        m = Memory(nc, ctx, "expert")
        w1 = m.sb("w1", [P, NEXP, DK, HID])
        w2 = m.sb("w2", [P, NEXP, HC, D])
        b1 = m.sb("b1", [P, NEXP, HC])
        b2 = m.sb("b2", [P, NEXP, D])
        xin = m.sb("xin", [P, U, D])
        xT = m.sb("xT", [P, DK, P])
        pre = m.sb("pre", [P, HID])
        hT = m.sb("hT", [P, HC, P])
        out = m.sb("out", [P, U, D])
        pX = m.ps("pX", [P, 512])
        pH = m.ps("pH", [P, 2, 512])
        pG = m.ps("pG", [P, HC, P])
        pO = m.ps("pO", [P, 2, 512])
        weights_in = m.sem("weights_in")
        x_in = [m.sem(f"x_in{j}") for j in range(U)]
        x_turned = m.sem("x_turned", starts=1)
        xT_ready = m.sem("xT_ready")
        up_done = m.sem("up_done")
        pre_ready = m.sem("pre_ready", starts=1)
        pre_turned = m.sem("pre_turned")
        h_ready = m.sem("h_ready")
        down_done = m.sem("down_done")
        out_ready = m.sem("out_ready", starts=1)
        out_free = m.sem("out_free", starts=U)
        out_stored = [m.swdge_sem(f"out_stored{j}") for j in range(U)]

        m.clear_semaphores()
        with nc.Block() as block:

            @block.sync
            def _(sp):
                with sp.Fori(0, ETRIPS) as i:
                    for j in range(U):
                        after(sp, x_turned, i * U)
                        sp.dma_start(xin[:, j, :], d["xs"][bass.ds((i * U + j) * P, P), :]).then_inc(x_in[j], 16)

            @block.scalar
            def _(act):
                for e in range(NEXP):
                    act.dma_start(w1[:, e, :, :], d["fw1"][e].rearrange("(k p) h -> p k h", p=P)).then_inc(weights_in, 16)
                    act.dma_start(w2[:, e, :, :], d["fw2"][e].rearrange("(c p) o -> p c o", p=P)).then_inc(weights_in, 16)
                act.dma_start(b1[:, :, :], d["fb1_t"]).then_inc(weights_in, 16)
                act.dma_start(b2[:, :, :], d["fb2"].partition_broadcast(P)).then_inc(weights_in, 16)
                act.wait_ge(weights_in, 16 * 18)
                with act.Fori(0, ETRIPS) as i:
                    for j in range(U):
                        t = i * U + j
                        e = act.value_load(k["expert"][0:1, bass.ds(t, 1)], min_val=0, max_val=NEXP - 1)
                        after(act, x_turned, t + 1)
                        nc.scalar.copy(xT[:, :, :].rearrange("p k n -> p (k n)"), pX[:, 0:D]).then_inc(xT_ready, 1)
                        act.wait_ge(pre_turned, t + 1)
                        for c in range(HC):
                            nc.scalar.activation(hT[:, c, :], pG[:, c, :], ACT.Gelu, bias=b1[:, e, c:c + 1]).then_inc(h_ready, 1)

            @block.vector
            def _(dve):
                dve.wait_ge(weights_in, 16 * 18)

                def take_out(t, j, i):
                    e = dve.value_load(k["expert"][0:1, bass.ds(t, 1)], min_val=0, max_val=NEXP - 1)
                    dve.wait_ge(out_free, t + 1)
                    dve.wait_ge(down_done, t + 1)
                    nc.vector.tensor_tensor(out[:, j, :], pO[:, j % 2, 0:D], b2[:, e, :], ALU.add).then_inc(out_ready, 1)

                with dve.Fori(0, ETRIPS) as i:
                    for j in range(U):
                        t = i * U + j
                        dve.wait_ge(up_done, t + 1)
                        nc.vector.tensor_copy(pre[:, :], pH[:, :, :].rearrange("p a b -> p (a b)")).then_inc(pre_ready, 1)
                        if j:
                            take_out(t - 1, j - 1, i)
                    take_out(i * U + U - 1, U - 1, i)

            @block.tensor
            def _(pe):
                def up(t, j, i):
                    e = pe.value_load(k["expert"][0:1, bass.ds(t, 1)], min_val=0, max_val=NEXP - 1)
                    pe.wait_ge(x_in[j], 16 * (i + 1))
                    for kk in range(DK):
                        last = nc.tensor.transpose(pX[:, kk * P:(kk + 1) * P], xin[:, j, kk * P:(kk + 1) * P], k["ident"][:, :])
                    last.then_inc(x_turned, 1)
                    pe.wait_ge(xT_ready, t + 1)
                    after(pe, pre_ready, t)
                    for a in range(2):
                        for kk in range(DK):
                            last = nc.tensor.matmul(pH[:, a, :], xT[:, kk, :], w1[:, e, kk, a * 512:(a + 1) * 512],
                                                    start=(kk == 0), stop=(kk == 1))
                    last.then_inc(up_done, 1)
                    return e

                def turn(t):
                    after(pe, pre_ready, t + 1)
                    for c in range(HC):
                        last = nc.tensor.transpose(pG[:, c, :], pre[:, c * P:(c + 1) * P], k["ident"][:, :])
                    last.then_inc(pre_turned, 1)

                def down(t, j, i):
                    e = pe.value_load(k["expert"][0:1, bass.ds(t, 1)], min_val=0, max_val=NEXP - 1)
                    after(pe, out_ready, i * U + max(j - 1, 0))
                    for c in range(HC):
                        pe.wait_ge(h_ready, t * HC + c + 1)
                        last = nc.tensor.matmul(pO[:, j % 2, 0:D], hT[:, c, :], w2[:, e, c, :], start=(c == 0), stop=(c == HC - 1))
                    last.then_inc(down_done, 1)

                pe.wait_ge(weights_in, 16 * 18)
                with pe.Fori(0, ETRIPS) as i:
                    up(i * U, 0, i)
                    turn(i * U)
                    for j in range(U):
                        t = i * U + j
                        if j + 1 < U:
                            up(t + 1, j + 1, i)
                        down(t, j, i)
                        if j + 1 < U:
                            turn(t + 1)

            @block.gpsimd
            def _(pool):
                with pool.Fori(0, ETRIPS) as i:
                    for j in range(U):
                        after(pool, out_ready, i * U + j + 1)
                        pool.dma_start(d["ys"][bass.ds((i * U + j) * P, P), :], out[:, j, :]).then_inc(out_stored[j], 16)
                        pool.wait_ge(out_stored[j], 16 * (i + 1))
                        pool.sem_inc(out_free, 1)
                for j in range(U):
                    pool.wait_ge(out_stored[j], 16 * ETRIPS)


def combine_pass(nc, k, d):
    with ExitStack() as ctx:
        m = Memory(nc, ctx, "combine")
        x1 = m.sb("x1", [P, 2, U, D])
        rows = m.sb("rows", [P, 2, 2, U, D])
        x_in = [m.sem("x_in0"), m.sem("x_in1")]
        rows_in = [m.swdge_sem("rows_in0"), m.swdge_sem("rows_in1")]
        out_ready = m.sem("out_ready")
        out_stored = [m.sem("out_stored0"), m.sem("out_stored1")]
        m.clear_semaphores()
        with nc.Block() as block:

            @block.gpsimd
            def _(pool):
                for i in range(TRIPS):
                    if i >= 2:
                        pool.wait_ge(out_ready, i - 1)
                    for j in range(U):
                        for s in range(2):
                            pool.indirect_dma_start(rows[:, i % 2, s, j, :], None, d["ys"],
                                                    bass.IndirectOffsetOnAxis(ap=k["slot_in"][:, s, i * U + j:i * U + j + 1], axis=0)
                                                    ).then_inc(rows_in[i % 2], 16)

            @block.sync
            def _(sp):
                for i in range(TRIPS):
                    if i >= 2:
                        sp.wait_ge(out_stored[i % 2], 16 * (i // 2) if i < TRIPS else 0)
                    sp.dma_start(x1[:, i % 2, :, :], d["x1"].rearrange("(t p) c -> p t c", p=P)[:, i * U:(i + 1) * U, :]).then_inc(x_in[i % 2], 16)

            @block.scalar
            def _(act):
                for i in range(TRIPS):
                    act.wait_ge(out_ready, i + 1)
                    if i < TRIPS - 1:
                        act.dma_start(d["out"][i * U * P:(i + 1) * U * P, :].rearrange("(t p) c -> p t c", p=P),
                                      x1[:, i % 2, :, :]).then_inc(out_stored[i % 2], 16)
                    else:
                        act.dma_start(d["out"][i * U * P:(NT - 1) * P, :].rearrange("(t p) c -> p t c", p=P),
                                      x1[:, i % 2, 0:U - 1, :]).then_inc(out_stored[i % 2], 16)
                        act.dma_start(d["out"][(NT - 1) * P:N, :], x1[0:LAST, i % 2, U - 1, :]).then_inc(out_stored[i % 2], 16)
                act.wait_ge(out_stored[0], 16 * 5)
                act.wait_ge(out_stored[1], 16 * 3)

            @block.vector
            def _(dve):
                for i in range(TRIPS):
                    dve.wait_ge(x_in[i % 2], 16 * (i // 2 + 1))
                    dve.wait_ge(rows_in[i % 2], 16 * 2 * U * (i // 2 + 1))
                    for s in range(2):
                        for j in range(U):
                            t = i * U + j
                            last = nc.vector.scalar_tensor_tensor(out=x1[:, i % 2, j, :], in0=rows[:, i % 2, s, j, :],
                                                                  scalar=k["mix_weight"][:, s, t:t + 1], in1=x1[:, i % 2, j, :],
                                                                  op0=ALU.mult, op1=ALU.add)
                        dve.drain()
                    dve.sem_inc(out_ready, 1)


def build_program(nc, d, until=99):
    with ExitStack() as ctx:
        Memory.program = ctx
        m = Memory(nc, ctx, "all")
        k = dict(
            ident=m.sb("ident", [P, P]), ones=m.sb("ones", [P, P]), node_i=m.sb("node_i", [P, NT], I32),
            count_i=m.sb("count_i", [P, P], I32), node=m.sb("node", [P, NT]), count=m.sb("count", [P, P]),
            attn1=m.sb("attn1", [P, NT, 2 * HEADS1]), attn2=m.sb("attn2", [P, NT, 2]),
            no_edges=m.sb("no_edges", [P, NT]), last_i=m.sb("last_i", [P, NT], I32),
            start_i=m.sb("start_i", [P, NT], I32), etile_i=m.sb("etile_i", [P, SJ], I32),
            offset=m.sb("offset", [1, SP], I32), src_step=m.sb("src_step", [P, SP, TPS], I32),
            place=m.sb("place", [P, SP, TPS]), self_weight=m.sb("self_weight", [P, NT, HEADS1]),
            rdenom=m.sb("rdenom", [P, NT, HEADS1]), slot_out=m.sb("slot_out", [P, 2, NT], I32),
            slot_in=m.sb("slot_in", [P, 2, NT], I32), mix_weight=m.sb("mix_weight", [P, 2, NT]),
            expert=m.sb("expert", [1, TT], I32))

        def scratch(name, shape, dt=F32):
            return nc.dram_tensor(f"s_{name}", shape, dt, kind="Internal").ap()

        d["h1"] = scratch("h1", [NP, F1])
        d["base"] = scratch("base", [NP, D])
        constants(nc, k)
        d["offsets"] = scratch("offsets", [SP], I32)
        if until != 2:
            node_pass(nc, k, d)
        edge_pass(nc, k, d)
        d["spread"], d["scanned"], d["weights"], d["sums"], d["step_weights"] = {}, {}, {}, {}, {}
        for H in (HEADS1, 1):
            d["spread"][H] = scratch(f"spread{H}", [EP, 2 * H])
            d["scanned"][H] = scratch(f"scanned{H}", [EP, H])
            d["weights"][H] = scratch(f"weights{H}", [EP, H])
            d["sums"][H] = scratch(f"sums{H}", [EP, H])
            d["step_weights"][H] = scratch(f"step_weights{H}", [P, SP * TPS * H])
        d["h2"] = scratch("h2", [NP, D])
        attention_pass(nc, k, d, 1, HEADS1, k["attn1"])
        weight_table(nc, k, d, 1, HEADS1)
        with nc.sbuf_tensor("acc1", [P, F1 // P, NP], F32) as acc:
            self_messages(nc, k, d, 1, HEADS1, F1, acc, d["h1"])
            message_pass(nc, k, d, 1, HEADS1, F1, acc, d["h1"])
            finish_layer1(nc, k, d, acc)
        attention_pass(nc, k, d, 2, 1, k["attn2"])
        weight_table(nc, k, d, 2, 1)
        d["x1"] = scratch("x1", [NP, D])
        d["xs"] = scratch("xs", [SLOTS, D])
        d["ys"] = scratch("ys", [SLOTS, D])
        with nc.sbuf_tensor("acc2", [P, DK, NP], F32) as acc:
            self_messages(nc, k, d, 2, 1, D, acc, d["h2"])
            message_pass(nc, k, d, 2, 1, D, acc, d["h2"])
            finish_layer2(nc, k, d, acc)
        expert_pass(nc, k, d)
        combine_pass(nc, k, d)


def lay_out(inputs):
    import numpy as np

    g = {n: np.asarray(v) for n, v in inputs.items()}
    dst, src = g["dst"].astype(np.int32, copy=False), g["src"].astype(np.int32, copy=False)
    pad = EP - EDGES
    dst_ext = np.concatenate([np.full(1, -1, np.int32), dst, np.full(pad, N, np.int32)])
    src_pad = np.concatenate([src, np.zeros(pad, np.int32)])
    valid = np.ones((P, NT), np.float32)
    valid[LAST:, NT - 1] = 0.0
    c = np.ascontiguousarray
    return {
        "x": np.concatenate([g["x"], np.zeros((NP - N, D), np.float32)]),
        "src": c(src_pad), "dst": c(dst_ext[1:]), "dst_ext": c(dst_ext), "valid": valid,
        "w1": c(g["L0_gnn_W1"]), "a_src1": c(g["L0_gnn_a_src1"]), "a_dst1": c(g["L0_gnn_a_dst1"]),
        "b1": c(g["L0_gnn_b1"]), "prelu_w": c(g["L0_gnn_prelu_w"].reshape(1)), "w2": c(g["L0_gnn_W2"]),
        "a_src2": c(g["L0_gnn_a_src2"]), "a_dst2": c(g["L0_gnn_a_dst2"]), "b2": c(g["L0_gnn_b2"]),
        "wq": c(g["L0_mix_wq"]), "wk_t": c(g["L0_mix_wk"].T), "wv_t": c(g["L0_mix_wv"].T),
        "wo_t": c(g["L0_mix_wo"].T), "bo": c(g["L0_mix_bo"]),
        "ln_k_g": c(g["L0_mix_ln_k_g"]), "ln_k_b": c(g["L0_mix_ln_k_b"]),
        "ln_v_g": c(g["L0_mix_ln_v_g"]), "ln_v_b": c(g["L0_mix_ln_v_b"]),
        "wg": c(g["L0_ffn_Wg"]), "bg": c(g["L0_ffn_bg"]), "fw1": c(g["L0_ffn_W1"]), "fb1_t": c(g["L0_ffn_b1"].reshape(NEXP, HID // P, P).transpose(2, 0, 1)),
        "fw2": c(g["L0_ffn_W2"]), "fb2": c(g["L0_ffn_b2"]),
    }


def kernel(**inputs):
    import numpy as np
    import concourse.bacc as bacc
    from concourse.bass_utils import run_bass_kernel_spmd

    nc = bacc.Bacc("TRN2", target_bir_lowering=False, num_devices=1)
    arrays = {f"in_{n}_dram": a for n, a in lay_out(inputs).items()}
    d = {n[3:-5]: nc.dram_tensor(n, a.shape, mybir.dt.from_np(a.dtype), kind="ExternalInput").ap()
         for n, a in arrays.items()}
    d["out"] = nc.dram_tensor("out_dram", (N, D), F32, kind="ExternalOutput").ap()
    build_program(nc, d)
    return np.asarray(run_bass_kernel_spmd(nc, [arrays], core_ids=[0]).results[0]["out_dram"])
```

```python
from contextlib import ExitStack

import concourse.bass as bass
from concourse import mybir

ALU = mybir.AluOpType
ACT = mybir.ActivationFunctionType
F32 = mybir.dt.float32
I32 = mybir.dt.int32
BF16 = mybir.dt.bfloat16
AX_X = mybir.AxisListType.X

P = 128
N = 6250
D = 256
DK = D // P
NT = -(-N // P)
NP = NT * P
LAST = N - (NT - 1) * P
U = 7
TRIPS = NT // U
UPARTS = ((0, 4), (4, U))
assert TRIPS * U == NT
EDGES = 200000
TPS = 2
BLOCK_BITS = (P * TPS).bit_length() - 1
BLOCKS = -(-EDGES // (P * TPS))
C = BLOCKS * TPS
EP = C * P
HEADS1 = 4
F1 = 512
MIX_HEADS = 8
HD = 64
EPS = 1e-5
SLOPE = 0.2
BIG = 1e30
W = P
NW = NP // W
STEPS = BLOCKS + NW - 1
SJ = -(-STEPS // P)
SP = SJ * P
G = 2
RING = 6
SETS = 3
AHEAD = 2
ROW_TILES = -(-C // P)
GATHERS = 4
LANDINGS = 4
CHUNK = 4
FAR = 2.0 ** 100
OUT_OF_RANGE = 1 << 20
NEXP = 8
HID = 1024
TT = (2 * N + NEXP * (P - 1)) // P
SLOTS = TT * P


class Memory:

    program = None

    def __init__(self, nc, ctx, stage):
        self.nc, self.ctx, self.stage = nc, ctx, stage
        self.sems = []
        self.starts = []
        Memory.program = Memory.program or ctx

    def sb(self, name, shape, dt=F32):
        return self.ctx.enter_context(self.nc.sbuf_tensor(f"{self.stage}_{name}", shape, dt))

    def ps(self, name, shape, dt=F32):
        return self.ctx.enter_context(self.nc.psum_tensor(f"{self.stage}_{name}", shape, dt))

    def swdge_sem(self, name):
        self.sems.append(self.program.enter_context(self.nc.semaphore(f"{self.stage}_{name}")))
        return self.sems[-1]

    def sem(self, name, starts=0):
        self.sems.append(self.ctx.enter_context(self.nc.semaphore(f"{self.stage}_{name}")))
        self.starts.append((self.sems[-1], starts))
        return self.sems[-1]

    def clear_semaphores(self):
        with self.nc.Block() as block:

            @block.sync
            def _(sp):
                for sem in self.sems:
                    sp.sem_clear(sem)
                for sem, starts in self.starts:
                    if starts:
                        sp.sem_inc(sem, starts)


def after(engine, sem, n):
    engine.wait_ge(sem, n + 1)


def part_of(j):
    return 0 if j < UPARTS[0][1] else 1


def spread(ap, axis, n):
    shape = list(ap.shape)
    return ap.unsqueeze(axis).to_broadcast(shape[:axis] + [n] + shape[axis:])


def constants(nc, k):
    with nc.Block() as block:

        @block.gpsimd
        def _(pool):
            nc.gpsimd.memset(k["ident"][:, :], 0.0)
            nc.gpsimd.memset(k["ones"][:, :], 1.0)
            nc.gpsimd.iota(k["node_i"][:, :], [[P, NT]], base=0, channel_multiplier=1)
            nc.gpsimd.iota(k["count_i"][:, :], [[1, P]], base=0, channel_multiplier=0)
            pool.drain()
            nc.gpsimd.affine_select(out=k["ident"][:, :], in_=k["ident"][:, :], compare_op=ALU.not_equal, fill=1.0,
                                    base=0, pattern=[[-1, P]], channel_multiplier=1)
            nc.gpsimd.tensor_copy(k["node"][:, :], k["node_i"][:, :])
            nc.gpsimd.tensor_copy(k["count"][:, :], k["count_i"][:, :])


def node_pass(nc, k, d):
    with ExitStack() as ctx:
        m = Memory(nc, ctx, "node")
        x = m.sb("x", [P, NT, D])
        w1 = m.sb("w1", [P, DK, F1])
        avec = m.sb("avec", [P, 2 * HEADS1, P])
        aprod = m.sb("aprod", [P, HEADS1, P])
        wa = m.sb("wa", [P, DK, 2 * HEADS1])
        wkv = m.sb("wkv", [P, DK, MIX_HEADS, HD])
        wkv_mean = m.sb("wkv_mean", [P, DK * MIX_HEADS])
        wq = m.sb("wq", [P, DK, D])
        wo = m.sb("wo", [P, DK, D])
        gains = m.sb("gains", [P, 2, HD])
        shifts = m.sb("shifts", [P, 2, HD])
        rbias = m.sb("rbias", [P, 2, D])
        valid = m.sb("valid", [P, NT])
        stats = m.sb("stats", [P, NT, 6])
        mean = m.sb("mean", [P, NT])
        half = m.sb("half", [P, NT])
        var = m.sb("var", [P, NT])
        rstd = m.sb("rstd", [P, NT])
        eps = m.sb("eps", [P, 1])
        xn = m.sb("xn", [P, U, D])
        xT = m.sb("xT", [P, 2, DK, P])
        h_out = m.sb("h_out", [P, U, F1])
        square = m.sb("square", [P, 2, F1])
        ssum = m.sb("ssum", [P, 2, MIX_HEADS])
        sroot = m.sb("sroot", [P, 2, MIX_HEADS])
        srec = m.sb("srec", [P, 2, MIX_HEADS])
        kvn = m.sb("kvn", [P, 2, F1])
        kvg = m.sb("kvg", [P, 2, F1])
        kv = m.sb("kv", [P, U, F1])
        zero = m.sb("zero", [P, D])
        kvT = m.sb("kvT", [P, 2, P])
        kvo = m.sb("kvo", [P, 2, D])
        mix = m.sb("mix", [P, DK, D])
        pT = m.ps("pT", [P, 2, 512])
        pH = m.ps("pH", [P, 2, F1])
        pKV = m.ps("pKV", [P, 2, F1])
        pA = m.ps("pA", [P, 512])
        pS = m.ps("pS", [P, 4, P])
        first_i = m.sb("first_i", [1, C], I32)
        first_f = m.sb("first_f", [1, C])
        firsts = m.sb("firsts", [P, C])
        leq = m.sb("leq", [P, C], BF16)
        first_in = m.sem("first_in")
        first_ready = m.sem("first_ready")
        firsts_out = m.sem("firsts_out")
        counted = m.sem("counted", starts=1)
        XPARTS = [(c, min(c + 10, NT)) for c in range(0, NT, 10)]
        loaded = [m.sem(f"loaded{c}") for c in range(len(XPARTS))]
        weights_in = m.sem("weights_in")
        weights_ready = m.sem("weights_ready")
        stats_done = m.sem("stats_done")
        root_done = m.sem("root_done")
        normed = m.sem("normed")
        turned = m.sem("turned")
        turned_out = m.sem("turned_out")
        multiplied = m.sem("multiplied")
        h_copied = m.sem("h_copied", starts=1)
        squared = m.sem("squared")
        summed = m.sem("summed", starts=1)
        rooted = m.sem("rooted")
        a_copied = m.sem("a_copied", starts=1)
        kv_normed = m.sem("kv_normed", starts=1)
        kv_scaled = m.sem("kv_scaled", starts=1)
        k_ready = m.sem("k_ready")
        v_ready = m.sem("v_ready")
        kv_used = m.sem("kv_used", starts=1)
        h_stored = [m.sem("h_stored0"), m.sem("h_stored1")]
        h_free = [m.sem("h_free0", starts=1), m.sem("h_free1", starts=1)]
        mix_step = m.sem("mix_step")
        mix_copied = m.sem("mix_copied")
        biased = m.sem("biased")
        normed2 = m.sem("normed2")
        turned2 = m.sem("turned2")
        turned2_out = m.sem("turned2_out")
        mixed = m.sem("mixed")
        base_ready = m.sem("base_ready", starts=1)
        base_stored = m.sem("base_stored")
        WLOADS = 14

        m.clear_semaphores()
        with nc.Block() as block:

            @block.sync
            def _(sp):
                sp.dma_start(first_i[:, :], d["dst"].rearrange("(c e) -> e c", e=P)[0:1, :],
                             allow_slow_non_contiguous=True).then_inc(first_in, 16)
                for (lo, hi), sem in zip(XPARTS, loaded):
                    sp.dma_start(x[:, lo:hi, :], d["x"].rearrange("(t p) c -> p t c", p=P)[:, lo:hi, :]).then_inc(sem, 16)
                with sp.Fori(0, TRIPS) as i:
                    for s, (lo, hi) in enumerate(UPARTS):
                        after(sp, h_copied, i * U + hi)
                        sp.dma_start(d["h1"].rearrange("(t p) c -> p t c", p=P)[:, bass.ds(i * U + lo, hi - lo), :],
                                     h_out[:, lo:hi, :]).then_inc(h_stored[s], 16)
                        sp.wait_ge(h_stored[s], 16 * (i + 1))
                        sp.sem_inc(h_free[s], 1)
                with sp.Fori(0, TRIPS) as i:
                    after(sp, base_ready, (i + 1) * U)
                    sp.dma_start(d["base"].rearrange("(t p) c -> p t c", p=P)[:, bass.ds(i * U, U), :],
                                 x[:, bass.ds(i * U, U), :]).then_inc(base_stored, 16)
                sp.wait_ge(base_stored, 16 * TRIPS)

            @block.scalar
            def _(act):
                loads = [
                    (w1[:, :, :], d["w1"].rearrange("(k p) f -> p k f", p=P)),
                    (avec[:, 0:HEADS1, :], d["a_src1"].partition_broadcast(P)),
                    (avec[:, HEADS1:, :], d["a_dst1"].partition_broadcast(P)),
                    (wkv[:, :, 0:4, :], d["wk_t"].rearrange("(k p) (h e) -> p k h e", p=P, e=HD)),
                    (wkv[:, :, 4:8, :], d["wv_t"].rearrange("(k p) (h e) -> p k h e", p=P, e=HD)),
                    (wq[:, :, :], d["wq"].rearrange("(k p) i -> p k i", p=P)),
                    (wo[:, :, :], d["wo_t"].rearrange("(k p) o -> p k o", p=P)),
                    (gains[:, 0, :], d["ln_k_g"].partition_broadcast(P)),
                    (gains[:, 1, :], d["ln_v_g"].partition_broadcast(P)),
                    (shifts[:, 0, :], d["ln_k_b"].partition_broadcast(P)),
                    (shifts[:, 1, :], d["ln_v_b"].partition_broadcast(P)),
                    (rbias[:, 0, :], d["bo"].partition_broadcast(P)),
                    (rbias[:, 1, :], d["b2"].partition_broadcast(P)),
                    (valid[:, :], d["valid"]),
                ]
                assert len(loads) == WLOADS
                for to, of in loads:
                    act.dma_start(to, of).then_inc(weights_in, 16)
                act.wait_ge(stats_done, 1)
                nc.scalar.activation(half[:, :], var[:, :], ACT.Sqrt, bias=eps[:, 0:1]).then_inc(root_done, 1)


                def copy_turned(t, j, done, copied):
                    act.wait_ge(done, t + 1)
                    nc.scalar.copy(xT[:, j % 2, :, :].rearrange("p k n -> p (k n)"), pT[:, j % 2, 0:D]).then_inc(copied, 1)

                with act.Fori(0, TRIPS) as i:
                    copy_turned(i * U, 0, turned, turned_out)
                    for j in range(U):
                        t = i * U + j
                        if j + 1 < U:
                            copy_turned(t + 1, j + 1, turned, turned_out)
                        act.wait_ge(multiplied, t + 1)
                        act.wait_ge(h_free[part_of(j)], i + 1)
                        nc.scalar.copy(h_out[:, j, :], pH[:, j % 2, :]).then_inc(h_copied, 1)
                        after(act, summed, t)
                        nc.scalar.activation(square[:, j % 2, :], pKV[:, j % 2, :], ACT.Square).then_inc(squared, 1)
                        after(act, summed, t + 1)
                        nc.scalar.activation(sroot[:, j % 2, :], ssum[:, j % 2, :], ACT.Sqrt, bias=eps[:, 0:1],
                                             scale=1.0 / HD).then_inc(rooted, 1)
                with act.Fori(0, TRIPS) as i:
                    for j in range(U):
                        copy_turned(i * U + j, j, turned2, turned2_out)

            @block.vector
            def _(dve):
                dve.wait_ge(first_in, 16)
                nc.vector.tensor_copy(first_f[:, :], first_i[:, :]).then_inc(first_ready, 1)
                for (lo, hi), sem in zip(XPARTS, loaded):
                    dve.wait_ge(sem, 16)
                    with dve.Fori(lo, hi) as t:
                        nc.vector.bn_stats(stats[:, t, :], x[:, t, :])
                nc.vector.memset(eps[:, :], EPS)
                nc.vector.memset(zero[:, :], 0.0)
                nc.vector.memset(kvT[:, :, :], 0.0)
                dve.drain()
                nc.vector.tensor_tensor(mean[:, :], stats[:, :, 1], stats[:, :, 4], ALU.add)
                nc.vector.tensor_tensor(half[:, :], stats[:, :, 1], stats[:, :, 4], ALU.subtract)
                nc.vector.tensor_tensor(var[:, :], stats[:, :, 2], stats[:, :, 5], ALU.add)
                dve.drain()
                nc.vector.tensor_scalar(mean[:, :], mean[:, :], 0.5, None, ALU.mult)
                nc.vector.tensor_tensor(half[:, :], half[:, :], half[:, :], ALU.mult)
                nc.vector.tensor_scalar(var[:, :], var[:, :], 1.0 / D, None, ALU.mult)
                dve.drain()
                nc.vector.scalar_tensor_tensor(out=var[:, :], in0=half[:, :], scalar=0.25, in1=var[:, :],
                                               op0=ALU.mult, op1=ALU.add).then_inc(stats_done, 1)
                dve.wait_ge(firsts_out, 1)
                for q, of in enumerate((pH, pKV)):
                    n = min(2 * F1, C - q * 2 * F1)
                    nc.vector.tensor_copy(firsts[:, q * 2 * F1:q * 2 * F1 + n], of[:, :, :].rearrange("p a b -> p (a b)")[:, 0:n])
                dve.wait_ge(weights_in, 16 * WLOADS)
                for kk in range(DK):
                    for s in range(2):
                        nc.vector.tensor_tensor(aprod[:, :, :], w1[:, kk, :].rearrange("p (h f) -> p h f", f=P),
                                                avec[:, s * HEADS1:(s + 1) * HEADS1, :], ALU.mult)
                        dve.drain()
                        nc.vector.tensor_reduce(wa[:, kk, s * HEADS1:(s + 1) * HEADS1], aprod[:, :, :], AX_X, ALU.add)
                        dve.drain()
                wkv_v = wkv[:, :, :, :].rearrange("p k h e -> p (k h) e")
                nc.vector.tensor_reduce(wkv_mean[:, :], wkv_v, AX_X, ALU.add)
                dve.drain()
                nc.vector.tensor_scalar(wkv_mean[:, :], wkv_mean[:, :], 1.0 / HD, None, ALU.mult)
                dve.drain()
                nc.vector.tensor_tensor(wkv_v, wkv_v, spread(wkv_mean[:, :], 2, HD), ALU.subtract)
                nc.vector.tensor_tensor(rbias[:, 0, :], rbias[:, 0, :], rbias[:, 1, :], ALU.add)
                dve.drain()
                dve.sem_inc(weights_ready, 1)
                dve.wait_ge(root_done, 1)
                nc.vector.reciprocal(rstd[:, :], half[:, :])
                nc.vector.tensor_scalar(var[:, :], var[:, :], EPS, None, ALU.add)
                dve.drain()
                nc.vector.tensor_tensor(half[:, :], rstd[:, :], rstd[:, :], ALU.mult)
                dve.drain()
                nc.vector.tensor_tensor(half[:, :], half[:, :], var[:, :], ALU.mult)
                dve.drain()
                nc.vector.tensor_scalar(half[:, :], half[:, :], -0.5, 1.5, ALU.mult, ALU.add)
                dve.drain()
                nc.vector.tensor_tensor(rstd[:, :], rstd[:, :], half[:, :], ALU.mult)
                dve.drain()

                def norm(t, j, of, done):
                    nc.vector.tensor_scalar(xn[:, j, :], of, mean[:, bass.ds(t, 1)], rstd[:, bass.ds(t, 1)],
                                            ALU.subtract, ALU.mult).then_inc(done, 1)

                with dve.Fori(0, TRIPS) as i:
                    for j in range(U):
                        norm(i * U + j, j, x[:, i * U + j, :], normed)
                    for j in range(U):
                        t = i * U + j
                        b = j % 2
                        dve.wait_ge(squared, t + 1)
                        nc.vector.tensor_reduce(ssum[:, b, :], square[:, b, :].rearrange("p (h e) -> p h e", e=HD),
                                                AX_X, ALU.add).then_inc(summed, 1)
                        nc.vector.tensor_copy(k["attn1"][:, t, :], pA[:, 0:2 * HEADS1]).then_inc(a_copied, 1)
                        after(dve, counted, t)
                        nc.vector.tensor_scalar(leq[:, :], firsts[:, :], k["node"][:, bass.ds(t, 1)], 0.0, ALU.is_le, ALU.add,
                                                accum_out=k["tiles_leq"][:, bass.ds(t, 1)]).then_inc(counted, 1)
                        dve.wait_ge(rooted, t + 1)
                        nc.vector.reciprocal(srec[:, b, :], sroot[:, b, :])
                        dve.drain()
                        after(dve, kv_scaled, t)
                        nc.vector.tensor_tensor(kvn[:, b, :].rearrange("p (h e) -> p h e", e=HD),
                                                pKV[:, b, :].rearrange("p (h e) -> p h e", e=HD),
                                                spread(srec[:, b, :], 2, HD), ALU.mult).then_inc(kv_normed, 1)
                        after(dve, kv_scaled, t + 1)
                        nc.vector.scalar_tensor_tensor(
                            out=kv[:, j, D:].rearrange("p (h e) -> p h e", e=HD),
                            in0=spread(shifts[:, 1, :], 1, 4), scalar=valid[:, bass.ds(t, 1)],
                            in1=kvg[:, b, D:].rearrange("p (h e) -> p h e", e=HD),
                            op0=ALU.mult, op1=ALU.add).then_inc(v_ready, 1)
                dve.wait_ge(mix_step, 1)
                for q in range(2):
                    for s in range(2):
                        r = slice(s * HD, (s + 1) * HD)
                        nc.vector.tensor_scalar(kvT[r, q, r], pS[r, q, r], 1.0 / N, None, ALU.mult)
                dve.drain()
                dve.sem_inc(mix_copied, 1)
                for q in range(2):
                    dve.wait_ge(mix_step, 2 + q)
                    nc.vector.tensor_copy(kvo[:, q, :], pH[:, q, 0:D]).then_inc(mix_copied, 1)
                for q in range(2):
                    dve.wait_ge(mix_step, 4 + q)
                    nc.vector.tensor_copy(mix[:, q, :], pKV[:, q, 0:D]).then_inc(mix_copied, 1)
                def norm2(t, j):
                    norm(t, j, x[:, t, :], normed2)
                    nc.vector.tensor_tensor(x[:, t, :], x[:, t, :], rbias[:, 0, :], ALU.add).then_inc(biased, 1)

                with dve.Fori(0, TRIPS) as i:
                    norm2(i * U, 0)
                    norm2(i * U + 1, 1)
                    for j in range(U):
                        t = i * U + j
                        if j + 2 < U:
                            norm2(t + 2, j + 2)
                        dve.wait_ge(mixed, t + 1)
                        dve.wait_ge(biased, t + 1)
                        nc.vector.tensor_tensor(x[:, t, :], pH[:, j % 2, 0:D], x[:, t, :], ALU.add).then_inc(base_ready, 1)

            @block.gpsimd
            def _(pool):
                pool.wait_ge(weights_ready, 1)
                with pool.Fori(0, TRIPS) as i:
                    for j in range(U):
                        t = i * U + j
                        after(pool, kv_normed, t + 1)
                        for s in range(2):
                            last = nc.gpsimd.tensor_tensor(
                                kvg[:, j % 2, s * D:(s + 1) * D].rearrange("p (h e) -> p h e", e=HD),
                                kvn[:, j % 2, s * D:(s + 1) * D].rearrange("p (h e) -> p h e", e=HD),
                                spread(gains[:, s, :], 1, 4), ALU.mult)
                        last.then_inc(kv_scaled, 1)
                        after(pool, kv_scaled, t + 1)
                        after(pool, kv_used, i)
                        nc.gpsimd.tensor_tensor(kv[:, j, 0:D].rearrange("p (h e) -> p h e", e=HD),
                                                kvg[:, j % 2, 0:D].rearrange("p (h e) -> p h e", e=HD),
                                                spread(shifts[:, 0, :], 1, 4), ALU.add).then_inc(k_ready, 1)

            @block.tensor
            def _(pe):
                pe.wait_ge(first_ready, 1)
                for a in range(-(-C // F1)):
                    w = min(F1, C - F1 * a)
                    last = nc.tensor.matmul((pH if a < 2 else pKV)[:, a % 2, 0:w], k["ones"][0:1, :], first_f[:, F1 * a:F1 * a + w],
                                            start=True, stop=True)
                last.then_inc(firsts_out, 1)
                pe.wait_ge(weights_ready, 1)
                nc.tensor.matmul(pS[:, 0:2, :].rearrange("p q n -> p (q n)"), zero[:, 0:P], zero[:, :], start=True, stop=False,
                                 skip_group_check=True)

                def turn(t, j, ready, done):
                    pe.wait_ge(ready, t + 1)
                    for kk in range(DK):
                        last = nc.tensor.transpose(pT[:, j % 2, kk * P:(kk + 1) * P], xn[:, j, kk * P:(kk + 1) * P],
                                                   k["ident"][:, :])
                    last.then_inc(done, 1)

                with pe.Fori(0, TRIPS) as i:
                    turn(i * U, 0, normed, turned)
                    for j in range(U):
                        t = i * U + j
                        b = j % 2
                        if j + 1 < U:
                            turn(t + 1, j + 1, normed, turned)
                        pe.wait_ge(turned_out, t + 1)
                        if j >= 2:
                            after(pe, h_copied, t - 1)
                            after(pe, kv_normed, t - 1)
                        else:
                            after(pe, h_copied, i * U)
                            after(pe, kv_normed, i * U)
                        for kk in range(DK):
                            nc.tensor.matmul(pH[:, b, :], xT[:, b, kk, :], w1[:, kk, :], start=(kk == 0), stop=(kk == 1))
                        for kk in range(DK):
                            nc.tensor.matmul(pKV[:, b, :], xT[:, b, kk, :], wkv[:, kk, :, :].rearrange("p h e -> p (h e)"),
                                             start=(kk == 0), stop=(kk == 1))
                        after(pe, a_copied, t)
                        for kk in range(DK):
                            last = nc.tensor.matmul(pA[:, 0:2 * HEADS1], xT[:, b, kk, :], wa[:, kk, :],
                                                    start=(kk == 0), stop=(kk == 1))
                        last.then_inc(multiplied, 1)
                    for j in range(U):
                        pe.wait_ge(k_ready, i * U + j + 1)
                        pe.wait_ge(v_ready, i * U + j + 1)
                        for q in range(2):
                            last = nc.tensor.matmul(pS[:, q, :], kv[:, j, D + q * P:D + (q + 1) * P],
                                                    kv[:, j, q * P:(q + 1) * P], start=False, stop=False,
                                                    skip_group_check=True)
                    last.then_inc(kv_used, 1)
                nc.tensor.matmul(pS[:, 0:2, :].rearrange("p q n -> p (q n)"), zero[:, 0:P], zero[:, :], start=False, stop=True,
                                 skip_group_check=True).then_inc(mix_step, 1)
                pe.wait_ge(mix_copied, 1)
                for q in range(2):
                    nc.tensor.matmul(pH[:, q, 0:D], kvT[:, q, :], wo[:, q, :], start=True, stop=True).then_inc(mix_step, 1)
                pe.wait_ge(mix_copied, 3)
                for c in range(DK):
                    for q in range(2):
                        last = nc.tensor.matmul(pKV[:, c, 0:D], wq[:, q, c * P:(c + 1) * P], kvo[:, q, :],
                                                start=(q == 0), stop=(q == 1))
                    last.then_inc(mix_step, 1)
                pe.wait_ge(mix_copied, 5)
                with pe.Fori(0, TRIPS) as i:
                    turn(i * U, 0, normed2, turned2)
                    for j in range(U):
                        t = i * U + j
                        if j + 1 < U:
                            turn(t + 1, j + 1, normed2, turned2)
                        pe.wait_ge(turned2_out, t + 1)
                        after(pe, base_ready, i * U + max(j - 1, 0))
                        for kk in range(DK):
                            last = nc.tensor.matmul(pH[:, j % 2, 0:D], xT[:, j % 2, kk, :], mix[:, kk, :],
                                                    start=(kk == 0), stop=(kk == 1))
                        last.then_inc(mixed, 1)


def edge_pass(nc, k, d):
    with ExitStack() as ctx:
        m = Memory(nc, ctx, "edge")
        tiles_leq = k["tiles_leq"]
        tile_i = m.sb("tile_i", [P, NT], I32)
        run_i = m.sb("run_i", [P, NT, P], I32)
        run_f = m.sb("run_f", [P, NT, P])
        rowend = m.sb("rowend", [P, NT])
        rowstart = m.sb("rowstart", [P, NT])
        tmp = m.sb("tmp", [P, NT])
        follow = m.sb("follow", [P, P])
        carry = m.sb("carry", [P, P])
        pick = m.sb("pick", [P, P])
        bound_i = m.sb("bound_i", [P, NW], I32)
        bound = m.sb("bound", [P, NW])
        window_i = m.sb("window_i", [P, NW], I32)
        window = m.sb("window", [P, NW])
        leq_w = m.sb("leq_w", [P, NW])
        at_window = m.sb("at_window", [P, SJ])
        etile = m.sb("etile", [P, SJ])
        over = m.sb("over", [P, SJ])
        lift = m.sb("lift", [P, SJ])
        offset_f = m.sb("offset_f", [P, SJ])
        off_t = m.sb("off_t", [SJ, P], I32)
        src_i = m.sb("src_i", [P, SJ, TPS * P], I32)
        dst_i = m.sb("dst_i", [P, SJ, TPS * P], I32)
        src_f = m.sb("src_f", [P, SJ, TPS * P])
        dst_f = m.sb("dst_f", [P, SJ, TPS * P])
        pT = m.ps("pT", [P, 2, 4, P])
        pR = m.ps("pR", [P, 512])
        pO = m.ps("pO", [P, 512])
        tiles_ready = m.sem("tiles_ready")
        runs_in = m.swdge_sem("runs_in")
        masks_ready = m.sem("masks_ready")
        ends_ready = m.sem("ends_ready")
        starts_out = m.sem("starts_out")
        walk_ready = m.sem("walk_ready")
        rows_in = m.swdge_sem("rows_in")
        rows_ready = m.sem("rows_ready")
        turned = m.sem("turned")
        copied = m.sem("copied")
        offsets_turned = m.sem("offsets_turned")
        offsets_ready = m.sem("offsets_ready")
        offsets_out = m.sem("offsets_out")
        offsets_in = m.sem("offsets_in")
        QUADS = SJ * TPS // 2

        m.clear_semaphores()
        with nc.Block() as block:

            @block.sync
            def _(sp):
                sp.wait_ge(offsets_ready, 1)
                sp.dma_start(d["offsets"].rearrange("(j p) -> j p", p=P), off_t[:, :]).then_inc(offsets_out, 16)
                sp.wait_ge(offsets_out, 16)
                sp.dma_start(k["offset"][:, :], d["offsets"].unsqueeze(0)).then_inc(offsets_in, 16)
                sp.wait_ge(offsets_in, 16)

            @block.gpsimd
            def _(pool):
                nc.gpsimd.memset(follow[:, :], 0.0)
                nc.gpsimd.memset(carry[:, :], 0.0)
                nc.gpsimd.memset(pick[:, :], 0.0)
                nc.gpsimd.iota(window_i[:, :], [[1, NW]], base=1, channel_multiplier=0)
                pool.drain()
                nc.gpsimd.affine_select(out=follow[:, :], in_=follow[:, :], compare_op=ALU.not_equal, fill=1.0,
                                        base=1, pattern=[[-1, P]], channel_multiplier=1)
                nc.gpsimd.affine_select(out=carry[:, :], in_=carry[:, :], compare_op=ALU.not_equal, fill=1.0,
                                        base=1 - P, pattern=[[-P, P]], channel_multiplier=1)
                nc.gpsimd.affine_select(out=pick[:, :], in_=pick[:, :], compare_op=ALU.not_equal, fill=1.0,
                                        base=1 - P, pattern=[[0, P]], channel_multiplier=1)
                nc.gpsimd.tensor_copy(window[:, :], window_i[:, :])
                pool.drain()
                pool.sem_inc(masks_ready, 1)
                pool.wait_ge(tiles_ready, 1)
                for t in range(NT):
                    pool.indirect_dma_start(run_i[:, t, :], None, d["dst"].rearrange("(c e) -> c e", e=P),
                                            bass.IndirectOffsetOnAxis(ap=tile_i[:, t:t + 1], axis=0)).then_inc(runs_in, 16)
                pool.wait_ge(walk_ready, 1)
                for j in range(SJ):
                    for to, of in ((src_i, d["src"]), (dst_i, d["dst"])):
                        pool.indirect_dma_start(to[:, j, :], None, of.rearrange("(c e) -> c e", e=TPS * P),
                                                bass.IndirectOffsetOnAxis(ap=k["etile_i"][:, j:j + 1], axis=0)).then_inc(rows_in, 16)

            @block.vector
            def _(dve):
                nc.vector.tensor_scalar(tiles_leq[:, :], tiles_leq[:, :], -1.0, 0.0, ALU.add, ALU.max)
                dve.drain()
                nc.vector.tensor_copy(tile_i[:, :], tiles_leq[:, :]).then_inc(tiles_ready, 1)
                dve.wait_ge(runs_in, 16 * NT)
                nc.vector.tensor_tensor(run_f[:, :, :], run_i[:, :, :], spread(k["node"][:, :], 2, P), ALU.is_le)
                dve.drain()
                nc.vector.tensor_reduce(rowend[:, :], run_f[:, :, :], AX_X, ALU.add)
                dve.drain()
                nc.vector.scalar_tensor_tensor(out=rowend[:, :], in0=tiles_leq[:, :], scalar=float(P), in1=rowend[:, :],
                                               op0=ALU.mult, op1=ALU.add).then_inc(ends_ready, 1)
                dve.wait_ge(starts_out, 1)
                nc.vector.tensor_copy(rowstart[:, :], pR[:, 0:NT])
                nc.vector.tensor_copy(bound_i[:, :], pO[:, 0:NW])
                dve.drain()
                nc.vector.tensor_tensor(k["no_edges"][:, :], rowstart[:, :], rowend[:, :], ALU.is_equal)
                nc.vector.tensor_scalar(tmp[:, :], rowend[:, :], -1.0, 0.0, ALU.add, ALU.max)
                nc.vector.tensor_scalar(bound_i[:, :], bound_i[:, :], BLOCK_BITS, None, ALU.arith_shift_right)
                dve.drain()
                nc.vector.tensor_copy(k["last_i"][:, :], tmp[:, :])
                nc.vector.scalar_tensor_tensor(out=rowstart[:, :], in0=k["no_edges"][:, :], scalar=float(OUT_OF_RANGE),
                                               in1=rowstart[:, :], op0=ALU.mult, op1=ALU.add)
                nc.vector.tensor_tensor(bound[:, :], bound_i[:, :], window[:, :], ALU.add)
                dve.drain()
                nc.vector.tensor_copy(k["start_i"][:, :], rowstart[:, :])
                for j in range(SJ):
                    nc.vector.tensor_scalar(leq_w[:, 0:NW - 1], bound[:, 0:NW - 1], k["node"][:, j:j + 1], 0.0, ALU.is_le,
                                            ALU.add, accum_out=at_window[:, j:j + 1])
                    dve.drain()
                nc.vector.tensor_tensor(etile[:, :], k["node"][:, 0:SJ], at_window[:, :], ALU.subtract)
                nc.vector.tensor_scalar(offset_f[:, :], at_window[:, :], float(W), None, ALU.mult)
                dve.drain()
                nc.vector.tensor_scalar(over[:, :], etile[:, :], float(BLOCKS - 1), float(OUT_OF_RANGE), ALU.is_gt, ALU.mult)
                nc.vector.tensor_scalar(etile[:, :], etile[:, :], float(BLOCKS - 1), None, ALU.min)
                dve.drain()
                nc.vector.tensor_tensor(lift[:, :], offset_f[:, :], over[:, :], ALU.subtract)
                nc.vector.tensor_copy(k["etile_i"][:, :], etile[:, :])
                dve.drain()
                dve.sem_inc(walk_ready, 1)
                dve.wait_ge(offsets_turned, 1)
                nc.vector.tensor_copy(off_t[:, :], pR[0:SJ, 0:P]).then_inc(offsets_ready, 1)
                dve.wait_ge(rows_in, 2 * 16 * SJ)
                nc.vector.tensor_copy(src_f[:, :, :], src_i[:, :, :])
                nc.vector.tensor_tensor(dst_f[:, :, :], dst_i[:, :, :], spread(lift[:, :], 2, TPS * P), ALU.subtract)
                dve.drain()
                dve.sem_inc(rows_ready, 1)
                for a in range(QUADS):
                    dve.wait_ge(turned, a + 1)
                    for n, to in enumerate((k["src_step"], k["place"])):
                        last = nc.vector.tensor_copy(to[:, a * P:(a + 1) * P, :],
                                                     pT[:, a % 2, n * TPS:(n + 1) * TPS, :].rearrange("p u s -> p s u"))
                    last.then_inc(copied, 1)

            @block.tensor
            def _(pe):
                pe.wait_ge(masks_ready, 1)
                pe.wait_ge(ends_ready, 1)
                nc.tensor.matmul(pR[:, 0:NT], follow[:, :], rowend[:, :], start=True, stop=False, skip_group_check=True)
                nc.tensor.matmul(pR[:, 1:NT], carry[:, :], rowend[:, 0:NT - 1], start=False, stop=True, skip_group_check=True)
                nc.tensor.matmul(pO[:, 0:NW], pick[:, :], rowend[:, :], start=True, stop=True).then_inc(starts_out, 1)
                pe.wait_ge(walk_ready, 1)
                nc.tensor.transpose(pR[0:SJ, 0:P], offset_f[:, :], k["ident"][:, :]).then_inc(offsets_turned, 1)
                pe.wait_ge(rows_ready, 1)
                for a in range(QUADS):
                    if a >= 2:
                        pe.wait_ge(copied, a - 1)
                    for n, of in enumerate((src_f, dst_f)):
                        for u in range(TPS):
                            last = nc.tensor.transpose(pT[:, a % 2, n * TPS + u, :], of[:, a, u * P:(u + 1) * P], k["ident"][:, :])
                    last.then_inc(turned, 1)


def attention_pass(nc, k, d, layer, H, attn):
    with ExitStack() as ctx:
        m = Memory(nc, ctx, f"attn{layer}")
        LOOKED = ROW_TILES if H == 1 else 2 * CHUNK
        GROUPS = (C - LOOKED * P) // GATHERS if LOOKED < ROW_TILES else 0
        assert not GROUPS or LOOKED * P + GROUPS * GATHERS == C and P % LANDINGS == 0
        CHUNKS = [range(t, min(t + CHUNK, LOOKED)) for t in range(0, LOOKED, CHUNK)]
        NQ = len(CHUNKS)
        src_row = m.sb("src_row", [P, C], I32)
        part_i = m.sb("part_i", [P, C], I32)
        place_in_tile = m.sb("place_in_tile", [P, LOOKED * P], BF16)
        node_tile = m.sb("node_tile", [P, LOOKED * P], BF16)
        eye = m.sb("eye", [P, P], BF16)
        far = m.sb("far", [NT, H, NT], BF16)
        minus = m.sb("minus", [P, 1])
        index = m.sb("index", [P, LANDINGS, GATHERS], I32)
        landing = m.sb("landing", [P, LANDINGS, GATHERS, H])
        left = m.sb("left", [P, H, NT])
        table = m.sb("table", [P, 3, H, NT], BF16)
        one_hot = m.sb("one_hot", [P, 2, CHUNK * P], BF16)
        distance = m.sb("distance", [NT, 2, CHUNK * P], BF16)
        dst_row = m.sb("dst_row", [P, C], I32)
        dst_before = m.sb("dst_before", [P, C], I32)
        same = m.sb("same", [P, C])
        reset = m.sb("reset", [P, C])
        zero = m.sb("zero", [P, C])
        first_scan = m.sb("first_scan", [P, C])
        term = m.sb("term", [P, C, H])
        scan = m.sb("scan", [P, C, H])
        target = m.sb("target", [P, C, 2 * H])
        node_in = m.sb("node_in", [P, NT, H])
        node_out = m.sb("node_out", [P, NT, 2 * H])
        logit = m.sb("logit", [P, NT, H])
        peak = m.sb("peak", [P, NT, H])
        through = m.sb("through", [P, 1])
        flags = m.sb("flags", [P, 2, 2 * H])
        ends = m.sb("ends", [P, 2 * H])
        row_flags = m.sb("row_flags", [2 * H, P])
        row_ends = m.sb("row_ends", [2 * H, P])
        row_scan = m.sb("row_scan", [2 * H, P + 1])
        carried = m.sb("carried", [P, 2 * H])
        pPlace = m.ps("pPlace", [P, 2, 512])
        pTile = m.ps("pTile", [P, 2, 512])
        pTerm = m.ps("pTerm", [P, 2, CHUNK // 2, 512])
        pF, pE, pK = pPlace[:, 0, :], pPlace[:, 1, :], pTile[:, 0, :]
        by_place = target[:, :, :].rearrange("p c h -> p (c h)")[:, 0:P * LOOKED * H].rearrange("p (r j h) -> p r j h", r=P, h=H)
        terms_stored = m.sem("terms_stored")
        index_ready = m.sem("index_ready")
        index_seen = m.sem("index_seen")
        gathered = [m.swdge_sem(f"gathered{r}") for r in range(LANDINGS if GROUPS else 0)]
        landed = m.sem("landed", starts=LANDINGS)
        lookup_ready = m.sem("lookup_ready")
        spread_out = m.sem("spread_out")
        one_hot_ready = m.sem("one_hot_ready", starts=2)
        distance_ready = m.sem("distance_ready", starts=2)
        picked = m.sem("picked", starts=2)
        reduced = m.sem("reduced", starts=2)
        all_reduced = m.sem("all_reduced")
        turned = m.sem("turned")
        copied = m.sem("copied")
        rows_in = m.sem("rows_in")
        zero_ready = m.sem("zero_ready")
        zeros_stored = m.sem("zeros_stored")
        carry_in = m.sem("carry_in")
        carry_turned = m.sem("carry_turned")
        carry_scanned = m.sem("carry_scanned")
        carry_back = m.sem("carry_back")
        peaks_ready = m.sem("peaks_ready")
        peaks_stored = m.sem("peaks_stored")
        node_peaks_in = m.swdge_sem("node_peaks_in")
        self_ready = m.sem("self_ready")
        self_done = m.sem("self_done")
        node_ready = m.sem("node_ready")
        node_scattered = m.swdge_sem("node_scattered")
        target_in = m.sem("target_in")
        logits_ready = m.sem("logits_ready")
        weights_ready = m.sem("weights_ready")
        weights_stored = m.sem("weights_stored")
        sums_ready = m.sem("sums_ready")
        sums_stored = m.sem("sums_stored")
        SCANS = [(H, True), (2 * H, False), (H, False)]

        def tile_edges(t):
            return min(P, C - t * P)

        def chunk_edges(q):
            return P * len(CHUNKS[q])

        def g_half(q):
            assert NQ % 2 == 0
            return q % 2

        def flat(ap):
            return ap.rearrange("p c h -> p (c h)")

        def dram_rows(ap):
            return ap.rearrange("(p c) h -> p (c h)", p=P)

        m.clear_semaphores()
        with nc.Block() as block:

            @block.sync
            def _(sp):
                if GROUPS:
                    sp.dma_start(d["terms"].rearrange("(t p) h -> p t h", p=P), attn[:, :, 0:H],
                                 allow_slow_non_contiguous=True).then_inc(terms_stored, 16)
                sp.dma_start(src_row[:, :], d["src"].rearrange("(p c) -> p c", p=P)).then_inc(rows_in, 16)
                sp.dma_start(dst_row[:, :], d["dst"].rearrange("(p c) -> p c", p=P)).then_inc(rows_in, 16)
                sp.dma_start(dst_before[:, :], d["dst_ext"][0:EP].rearrange("(p c) -> p c", p=P)).then_inc(rows_in, 16)
                sp.wait_ge(zero_ready, 1)
                for a in range(2 * H):
                    sp.dma_start(dram_rows(d["spread"][H])[:, a * C:(a + 1) * C], zero[:, :]).then_inc(zeros_stored, 16)
                sp.wait_ge(peaks_ready, 1)
                sp.dma_start(dram_rows(d["scanned"][H]), flat(scan[:, :, :])).then_inc(peaks_stored, 16)
                sp.wait_ge(node_scattered, 16 * NT)
                sp.dma_start(flat(target[:, :, :]), dram_rows(d["spread"][H])).then_inc(target_in, 16)
                sp.wait_ge(weights_ready, 1)
                sp.dma_start(dram_rows(d["weights"][H]), flat(term[:, :, :])).then_inc(weights_stored, 16)
                sp.wait_ge(sums_ready, 1)
                sp.dma_start(dram_rows(d["sums"][H]), flat(scan[:, :, :])).then_inc(sums_stored, 16)
                sp.wait_ge(weights_stored, 16)
                sp.wait_ge(sums_stored, 16)

            @block.scalar
            def _(act):
                def distances(g, q):
                    n = chunk_edges(q)
                    act.wait_ge(spread_out, g + 1)
                    act.wait_ge(picked, g + 1)
                    nc.scalar.activation(distance[:, g_half(q), 0:n], pTile[0:NT, g_half(q), 0:n], ACT.Square,
                                         bias=minus[0:NT, 0:1]).then_inc(distance_ready, 1)

                def take_gathered(g, r, trip):
                    act.wait_ge(gathered[r], (trip + 1) * (16 * GATHERS))
                    nc.scalar.copy(term[:, bass.ds(g * GATHERS + LOOKED * P, GATHERS), :], landing[:, r, :, :]).then_inc(landed, 1)

                def bring_index(g, r):
                    nc.scalar.copy(index[:, r, :], src_row[:, bass.ds(g * GATHERS + LOOKED * P, GATHERS)]).then_inc(index_ready, 1)

                act.wait_ge(lookup_ready, 1)
                if GROUPS:
                    for r in range(LANDINGS):
                        bring_index(r, r)
                    full = GROUPS // LANDINGS - 1
                    assert full * LANDINGS <= P
                    with act.Fori(0, full) as i:
                        for r in range(LANDINGS):
                            g = i * LANDINGS + r
                            for q in range(NQ):
                                distances(g * NQ + q, q)
                            take_gathered(g, r, i)
                            bring_index(g + LANDINGS, r)
                    for g in range(full * LANDINGS, GROUPS):
                        if g < P:
                            for q in range(NQ):
                                distances(g * NQ + q, q)
                        take_gathered(g, g % LANDINGS, g // LANDINGS)
                        if g + LANDINGS < GROUPS:
                            bring_index(g + LANDINGS, g % LANDINGS)
                else:
                    with act.Fori(0, P) as row:
                        for q in range(NQ):
                            distances(row * NQ + q, q)
                act.wait_ge(self_ready, 1)
                nc.scalar.activation(k["self_weight"][:, :, 0:H], logit[:, :, :], ACT.Exp).then_inc(self_done, 1)
                act.wait_ge(logits_ready, 1)
                nc.scalar.activation(flat(term[:, :, :]), flat(term[:, :, :]), ACT.Exp).then_inc(weights_ready, 1)

            @block.gpsimd
            def _(pool):
                def gather_terms(g, r):
                    pool.wait_ge(index_ready, g + 1)
                    pool.wait_ge(landed, g + 1)
                    pool.sem_inc(index_seen, 1)
                    for a in range(GATHERS):
                        pool.indirect_dma_start(landing[:, r, a, :], None, d["terms"],
                                                bass.IndirectOffsetOnAxis(ap=index[:, r, a:a + 1], axis=0)).then_inc(gathered[r], 16)

                if GROUPS:
                    pool.wait_ge(terms_stored, 16)
                    with pool.Fori(0, GROUPS // LANDINGS) as i:
                        for r in range(LANDINGS):
                            gather_terms(i * LANDINGS + r, r)
                    for g in range(GROUPS // LANDINGS * LANDINGS, GROUPS):
                        gather_terms(g, g % LANDINGS)
                pool.wait_ge(peaks_stored, 16)
                for t in range(NT):
                    pool.indirect_dma_start(node_in[:, t, :], None, d["scanned"][H],
                                            bass.IndirectOffsetOnAxis(ap=k["last_i"][:, t:t + 1], axis=0)).then_inc(node_peaks_in, 16)
                pool.wait_ge(node_ready, 1)
                pool.wait_ge(zeros_stored, 16 * 2 * H)
                for t in range(NT):
                    pool.indirect_dma_start(d["spread"][H], bass.IndirectOffsetOnAxis(ap=k["start_i"][:, t:t + 1], axis=0),
                                            node_out[:, t, :], None, bounds_check=EP - 1, oob_is_err=False
                                            ).then_inc(node_scattered, 16)

            @block.tensor
            def _(pe):
                def spread_row(row, g, q):
                    n, first = chunk_edges(q), CHUNKS[q][0] * P
                    pe.wait_ge(one_hot_ready, g + 1)
                    pe.wait_ge(distance_ready, g + 1)
                    nc.tensor.matmul(pPlace[:, g_half(q), 0:n], eye[:, bass.ds(row, 1)].to_broadcast([P, P]),
                                     place_in_tile[:, first:first + n], start=True, stop=True)
                    nc.tensor.matmul(pTile[0:NT, g_half(q), 0:n], eye[:, bass.ds(row, 1)].to_broadcast([P, NT]),
                                     node_tile[:, first:first + n], start=True, stop=True).then_inc(spread_out, 1)

                def pick(g, q):
                    pe.wait_ge(one_hot_ready, g + 3)
                    pe.wait_ge(distance_ready, g + 3)
                    pe.wait_ge(reduced, g + 1)
                    for t in CHUNKS[q]:
                        u = t % CHUNK
                        edges = slice(u * P, (u + 1) * P)
                        to = pTerm[:, g_half(q), u // 2, u % 2 * H * NT:(u % 2 + 1) * H * NT]
                        nc.tensor.matmul(to, distance[:, g_half(q), edges], far[:, :, :].rearrange("p h t -> p (h t)"),
                                         start=True, stop=False)
                        for part in range(3):
                            last = nc.tensor.matmul(to, one_hot[:, g_half(q), edges],
                                                    table[:, part, :, :].rearrange("p h t -> p (h t)"),
                                                    start=False, stop=(part == 2))
                    last.then_inc(picked, 1)

                pe.wait_ge(lookup_ready, 1)
                spread_row(0, 0, 0)
                with pe.Fori(0, P - 1) as row:
                    for q in range(NQ):
                        spread_row(row + (q + 1) // NQ, row * NQ + q + 1, (q + 1) % NQ)
                        pick(row * NQ + q, q)
                for q in range(NQ):
                    if q + 1 < NQ:
                        spread_row(P - 1, (P - 1) * NQ + q + 1, q + 1)
                    pick((P - 1) * NQ + q, q)
                pe.wait_ge(all_reduced, 1)
                for j in range(LOOKED):
                    e = tile_edges(j)
                    if j >= 2:
                        pe.wait_ge(copied, j - 1)
                    for h in range(H):
                        last = nc.tensor.transpose(pTerm[:, j % 2, 0, h * P:h * P + e], by_place[0:e, :, j, h], k["ident"][0:e, 0:e])
                    last.then_inc(turned, 1)

                for r, (n, _) in enumerate(SCANS):
                    pe.wait_ge(carry_in, r + 1)
                    nc.tensor.transpose(pF[0:n, 0:P], flags[:, 1 if r == 0 else 0, 0:n], k["ident"][:, :])
                    nc.tensor.transpose(pE[0:n, 0:P], ends[:, 0:n], k["ident"][:, :]).then_inc(carry_turned, 1)
                    pe.wait_ge(carry_scanned, r + 1)
                    nc.tensor.transpose(pK[:, 0:n], row_scan[0:n, 0:P], k["ident"][0:n, 0:n]).then_inc(carry_back, 1)

            @block.vector
            def _(dve):
                nc.vector.memset(zero[:, :], 0.0)
                dve.drain()
                dve.sem_inc(zero_ready, 1)
                dve.wait_ge(rows_in, 48)
                nc.vector.tensor_scalar(part_i[:, :], src_row[:, :], P - 1, None, ALU.bitwise_and)
                nc.vector.tensor_copy(eye[:, :], k["ident"][:, :])
                nc.vector.tensor_scalar(far[:, :, :], spread(k["ident"][0:NT, 0:NT], 1, H), -FAR, None, ALU.mult)
                nc.vector.tensor_scalar(minus[:, :], k["node"][:, 0:1], -1.0, None, ALU.mult)
                nc.vector.tensor_copy(left[:, :, :], attn[:, :, 0:H].rearrange("p t h -> p h t"))
                dve.drain()
                n = min(C, LOOKED * P)
                nc.vector.tensor_copy(place_in_tile[:, 0:n], part_i[:, 0:n])
                dve.drain()
                nc.vector.tensor_scalar(part_i[:, :], src_row[:, :], P.bit_length() - 1, None, ALU.arith_shift_right)
                dve.drain()
                nc.vector.tensor_copy(node_tile[:, 0:n], part_i[:, 0:n])
                if n < LOOKED * P:
                    nc.vector.memset(place_in_tile[:, n:], 0.0)
                    nc.vector.memset(node_tile[:, n:], 0.0)
                for part in range(3):
                    nc.vector.tensor_copy(table[:, part, :, :], left[:, :, :])
                    dve.drain()
                    nc.vector.tensor_tensor(left[:, :, :], left[:, :, :], table[:, part, :, :], ALU.subtract)
                    dve.drain()
                dve.sem_inc(lookup_ready, 1)
                nc.vector.tensor_tensor(same[:, :], dst_row[:, :], dst_before[:, :], ALU.is_equal)
                dve.drain()
                nc.vector.tensor_scalar(reset[:, :], same[:, :], -1.0, BIG, ALU.add, ALU.mult)
                nc.vector.tensor_reduce(through[:, :], same[:, :], AX_X, ALU.min)
                dve.drain()
                nc.vector.tensor_copy(flags[:, 0, :], through[:, 0:1].to_broadcast([P, 2 * H]))
                nc.vector.tensor_scalar(flags[:, 1, :], through[:, 0:1].to_broadcast([P, 2 * H]), -1.0, BIG, ALU.add, ALU.mult)

                def one_hots(g, q):
                    n = chunk_edges(q)
                    dve.wait_ge(spread_out, g + 1)
                    dve.wait_ge(picked, g + 1)
                    nc.vector.tensor_scalar(one_hot[:, g_half(q), 0:n], pPlace[:, g_half(q), 0:n], k["node"][:, 0:1], None,
                                            ALU.is_equal).then_inc(one_hot_ready, 1)

                def reduce_terms(row, g, q):
                    tiles = CHUNKS[q]
                    dve.wait_ge(picked, g + 3)
                    banks, pair = -(-len(tiles) // 2), min(len(tiles), 2)
                    nc.vector.tensor_reduce(
                        by_place[:, bass.ds(row, 1), tiles[0]:tiles[-1] + 1, :].rearrange("p r (b u) h -> p (r b) (u h)", b=banks),
                        pTerm[:, g_half(q), 0:banks, 0:pair * H * NT].rearrange("p b (u t) -> p b u t", t=NT),
                        AX_X, ALU.max).then_inc(reduced, 1)

                one_hots(0, 0)
                with dve.Fori(0, P - 1) as row:
                    for q in range(NQ):
                        one_hots(row * NQ + q + 1, (q + 1) % NQ)
                        reduce_terms(row, row * NQ + q, q)
                for q in range(NQ):
                    if q + 1 < NQ:
                        one_hots((P - 1) * NQ + q + 1, q + 1)
                    reduce_terms(P - 1, (P - 1) * NQ + q, q)
                dve.drain()
                dve.sem_inc(all_reduced, 1)
                if GROUPS:
                    dve.wait_ge(landed, GROUPS + LANDINGS)
                for j in range(LOOKED):
                    e = tile_edges(j)
                    dve.wait_ge(turned, j + 1)
                    nc.vector.tensor_copy(term[:, j * P:j * P + e, :].rearrange("p c h -> p h c"),
                                          pTerm[:, j % 2, 0, 0:H * P].rearrange("p (h e) -> p h e", h=H)[:, :, 0:e]).then_inc(copied, 1)
                dve.drain()

                def run_scan(r, of, to):
                    n, peak_scan = SCANS[r]
                    mark, op0, op1, empty = (reset, ALU.add, ALU.max, -BIG) if peak_scan else (same, ALU.mult, ALU.add, 0.0)
                    for h in range(n):
                        nc.vector.tensor_tensor_scan(first_scan[:, :], mark[:, :], of(h), empty, op0, op1)
                        dve.drain()
                        nc.vector.tensor_copy(ends[:, h:h + 1], first_scan[:, C - 1:C])
                        dve.drain()
                    dve.sem_inc(carry_in, 1)
                    dve.wait_ge(carry_turned, r + 1)
                    nc.vector.tensor_copy(row_flags[0:n, :], pF[0:n, 0:P])
                    nc.vector.tensor_copy(row_ends[0:n, :], pE[0:n, 0:P])
                    nc.vector.memset(row_scan[0:n, 0:1], empty)
                    dve.drain()
                    nc.vector.tensor_tensor_scan(row_scan[0:n, 1:P + 1], row_flags[0:n, :], row_ends[0:n, :], empty, op0, op1)
                    dve.drain()
                    dve.sem_inc(carry_scanned, 1)
                    dve.wait_ge(carry_back, r + 1)
                    nc.vector.tensor_copy(carried[:, 0:n], pK[:, 0:n])
                    dve.drain()
                    for h in range(n):
                        nc.vector.tensor_tensor_scan(to(h), mark[:, :], of(h), carried[:, h:h + 1], op0, op1)
                    dve.drain()

                def leaky(ap):
                    nc.vector.scalar_tensor_tensor(out=ap, in0=ap, scalar=SLOPE, in1=ap, op0=ALU.mult, op1=ALU.max)
                    dve.drain()

                run_scan(0, lambda h: term[:, :, h], lambda h: scan[:, :, h])
                dve.sem_inc(peaks_ready, 1)
                dve.wait_ge(node_peaks_in, 16 * NT)
                nc.vector.scalar_tensor_tensor(out=peak[:, :, :], in0=spread(k["no_edges"][:, :], 2, H), scalar=-BIG,
                                               in1=node_in[:, :, :], op0=ALU.mult, op1=ALU.add)
                nc.vector.tensor_tensor(logit[:, :, :], attn[:, :, 0:H], attn[:, :, H:2 * H], ALU.add)
                dve.drain()
                nc.vector.tensor_tensor(peak[:, :, :], peak[:, :, :], attn[:, :, 0:H], ALU.max)
                dve.drain()
                nc.vector.tensor_tensor(peak[:, :, :], peak[:, :, :], attn[:, :, H:2 * H], ALU.add)
                dve.drain()
                leaky(logit[:, :, :])
                leaky(peak[:, :, :])
                nc.vector.tensor_tensor(logit[:, :, :], logit[:, :, :], peak[:, :, :], ALU.subtract).then_inc(self_ready, 1)
                nc.vector.tensor_copy(node_out[:, :, 0:H], attn[:, :, H:2 * H])
                nc.vector.tensor_copy(node_out[:, :, H:2 * H], peak[:, :, :])
                dve.drain()
                dve.sem_inc(node_ready, 1)
                dve.wait_ge(target_in, 16)
                run_scan(1, lambda h: target[:, :, h], lambda h: target[:, :, h])
                nc.vector.tensor_tensor(term[:, :, :], term[:, :, :], target[:, :, 0:H], ALU.add)
                dve.drain()
                leaky(term[:, :, :])
                nc.vector.tensor_tensor(term[:, :, :], term[:, :, :], target[:, :, H:2 * H], ALU.subtract).then_inc(logits_ready, 1)
                dve.wait_ge(weights_ready, 1)
                run_scan(2, lambda h: term[:, :, h], lambda h: scan[:, :, h])
                dve.sem_inc(sums_ready, 1)


def weight_table(nc, k, d, layer, H):
    with ExitStack() as ctx:
        m = Memory(nc, ctx, f"table{layer}")
        rows = m.sb("rows", [P, SJ, TPS * P * H])
        turned = m.sb("turned", [P, 2, P, TPS, H])
        pT = m.ps("pT", [P, 2, TPS, 4, P])
        rows_in = m.swdge_sem("rows_in")
        done = m.sem("done")
        copied = m.sem("copied")
        stored = [m.sem("stored0"), m.sem("stored1")]

        m.clear_semaphores()
        with nc.Block() as block:

            @block.gpsimd
            def _(pool):
                for j in range(SJ):
                    pool.indirect_dma_start(rows[:, j, :], None, d["weights"][H].rearrange("(c e) h -> c (e h)", e=TPS * P),
                                            bass.IndirectOffsetOnAxis(ap=k["etile_i"][:, j:j + 1], axis=0)).then_inc(rows_in, 16)

            @block.tensor
            def _(pe):
                pe.wait_ge(rows_in, 16 * SJ)
                for j in range(SJ):
                    if j >= 2:
                        pe.wait_ge(copied, j - 1)
                    for u in range(TPS):
                        for h in range(H):
                            last = nc.tensor.transpose(pT[:, j % 2, u, h, :],
                                                       rows[:, j, u * P * H:(u + 1) * P * H].rearrange("p (e h) -> p h e", h=H)[:, h, :],
                                                       k["ident"][:, :])
                    last.then_inc(done, 1)

            @block.vector
            def _(dve):
                for j in range(SJ):
                    dve.wait_ge(done, j + 1)
                    if j >= 2:
                        dve.wait_ge(stored[j % 2], 16 * (j // 2))
                    for u in range(TPS):
                        last = nc.vector.tensor_copy(turned[:, j % 2, :, u, :], pT[:, j % 2, u, 0:H, :].rearrange("p h s -> p s h"))
                    last.then_inc(copied, 1)

            @block.sync
            def _(sp):
                for j in range(SJ):
                    sp.wait_ge(copied, j + 1)
                    sp.dma_start(d["step_weights"][H][:, j * P * TPS * H:(j + 1) * P * TPS * H],
                                 turned[:, j % 2, :, :, :].rearrange("p s u h -> p (s u h)")).then_inc(stored[j % 2], 16)
                sp.wait_ge(stored[0], 16 * (-(-SJ // 2)))
                sp.wait_ge(stored[1], 16 * (SJ // 2))


def self_messages(nc, k, d, layer, H, F, acc, table):
    NB = F // P
    with ExitStack() as ctx:
        m = Memory(nc, ctx, f"self{layer}")
        rows = m.sb("rows", [P, U, F])
        diag = m.sb("diag", [P, 2, H, P])
        sums = m.sb("sums", [P, NT, H])
        some_edges = m.sb("some_edges", [P, NT])
        sums_in = m.swdge_sem("sums_in")
        pM = m.ps("pM", [P, 2, 512])
        rows_in = [m.sem("rows_in0"), m.sem("rows_in1")]
        diag_ready = m.sem("diag_ready")
        multiplied = m.sem("multiplied", starts=U)
        copied = m.sem("copied", starts=1)
        m.clear_semaphores()
        with nc.Block() as block:

            @block.sync
            def _(sp):
                with sp.Fori(0, TRIPS) as i:
                    for s, (lo, hi) in enumerate(UPARTS):
                        sp.wait_ge(multiplied, i * U + hi)
                        sp.dma_start(rows[:, lo:hi, :], table.rearrange("(t p) c -> p t c", p=P)[:, bass.ds(i * U + lo, hi - lo), :]
                                     ).then_inc(rows_in[s], 16)

            @block.gpsimd
            def _(pool):
                for t in range(NT):
                    pool.indirect_dma_start(sums[:, t, :], None, d["sums"][H],
                                            bass.IndirectOffsetOnAxis(ap=k["last_i"][:, t:t + 1], axis=0)).then_inc(sums_in, 16)

            @block.vector
            def _(dve):
                with dve.Fori(0, TRIPS) as i:
                    for j in range(U):
                        t = i * U + j
                        dve.wait_ge(multiplied, i * U + max(j - 1, 0) + U)
                        nc.vector.tensor_tensor(diag[:, j % 2, :, :], spread(k["ident"][:, :], 1, H),
                                                spread(k["self_weight"][:, t, 0:H], 2, P), ALU.mult).then_inc(diag_ready, 1)
                nc.vector.tensor_scalar(some_edges[:, :], k["no_edges"][:, :], -1.0, 1.0, ALU.mult, ALU.add)
                dve.drain()
                dve.wait_ge(sums_in, 16 * NT)
                nc.vector.tensor_tensor(sums[:, :, :], sums[:, :, :], spread(some_edges[:, :], 2, H), ALU.mult)
                dve.drain()
                nc.vector.tensor_tensor(sums[:, :, :], sums[:, :, :], k["self_weight"][:, :, 0:H], ALU.add)
                dve.drain()
                nc.vector.reciprocal(k["rdenom"][:, :, 0:H], sums[:, :, :])

            @block.tensor
            def _(pe):
                with pe.Fori(0, TRIPS) as i:
                    for j in range(U):
                        t = i * U + j
                        pe.wait_ge(rows_in[part_of(j)], 16 * (i + 1))
                        pe.wait_ge(diag_ready, t + 1)
                        after(pe, copied, i * U + max(j - 1, 0))
                        for b in range(NB):
                            last = nc.tensor.matmul(pM[:, j % 2, b * P:(b + 1) * P], rows[:, j, b * P:(b + 1) * P],
                                                    diag[:, j % 2, b % H, :], start=True, stop=True)
                        last.then_inc(multiplied, 1)

            @block.scalar
            def _(act):
                with act.Fori(0, TRIPS) as i:
                    for j in range(U):
                        t = i * U + j
                        act.wait_ge(multiplied, t + 1 + U)
                        nc.scalar.copy(acc[:, 0:NB, bass.ds(t * P, P)],
                                       pM[:, j % 2, 0:F].rearrange("p (b n) -> p b n", n=P)).then_inc(copied, 1)


def message_pass(nc, k, d, layer, H, F, acc, table):
    NB = F // P
    GROUPS = -(-STEPS // G)
    WTRIPS = -(-(GROUPS - AHEAD) // RING)
    HV = H if H == 1 else H - 1
    GT = G * TPS
    assert (WTRIPS * RING + AHEAD) * G <= SP and AHEAD <= SETS and 2 * SETS == RING
    with ExitStack() as ctx:
        m = Memory(nc, ctx, f"walk{layer}")
        index = m.sb("index", [P, RING, G, TPS], I32)
        rows = m.sb("rows", [P, RING, GT, F])
        stepw = m.sb("stepw", [P, 2, SETS * GT * H])
        hit = m.sb("hit", [P, 2, GT, W])
        placed = m.sb("placed", [P, SETS, GT, H, W])
        pM = m.ps("pM", [P, SETS * G, 512])
        index_ready = m.sem("index_ready")
        index_seen = m.sem("index_seen")
        rows_in = [m.swdge_sem(f"rows_in{r}") for r in range(RING)]
        stepw_in = [m.sem("stepw_in0"), m.sem("stepw_in1")]
        hit_ready = m.sem("hit_ready")
        placed_ready = m.sem("placed_ready")
        last_head_ready = m.sem("last_head_ready", starts=2)
        multiplied = m.sem("multiplied", starts=RING * G)
        added = m.sem("added", starts=SETS * G)

        def loop(eng, body):
            with eng.Fori(0, WTRIPS) as i:
                for r in range(RING):
                    body(i * RING + r, r, i)
            for r in range(AHEAD):
                body(WTRIPS * RING + r, r, WTRIPS)

        m.clear_semaphores()
        with nc.Block() as block:

            @block.sync
            def _(sp):
                def load(q, half, n):
                    sp.dma_start(stepw[:, half, 0:n * GT * H],
                                 d["step_weights"][H][:, bass.ds(q * (GT * H), n * GT * H)]).then_inc(stepw_in[half], 16)

                for half in range(2):
                    load(half * SETS, half, SETS)
                with sp.Fori(1, WTRIPS) as i:
                    for half in range(2):
                        q = i * RING + half * SETS
                        sp.wait_ge(multiplied, q * G + (RING - SETS) * G)
                        load(q, half, SETS)
                sp.wait_ge(multiplied, WTRIPS * RING * G + (RING - SETS) * G)
                load(WTRIPS * RING, 0, AHEAD)

            @block.scalar
            def _(act):
                def bring_index(q, r, trip):
                    act.wait_ge(multiplied, q * G + G)
                    nc.scalar.copy(index[:, r, :, :], k["src_step"][:, bass.ds(q * G, G), :]).then_inc(index_ready, 1)

                def place_last_head(q, r, trip):
                    s, half = r % SETS, r // SETS
                    act.wait_ge(multiplied, q * G + (RING - SETS + 1) * G)
                    act.wait_ge(stepw_in[half], 16 * (trip + 1))
                    act.wait_ge(hit_ready, q + 1)
                    for a in range(GT):
                        w = (s * GT + a) * H + HV
                        last = nc.scalar.activation(placed[:, s, a, HV, :], hit[:, r % 2, a, :], ACT.Copy,
                                                    scale=stepw[:, half, w:w + 1])
                    last.then_inc(last_head_ready, 1)

                if HV == H:
                    loop(act, bring_index)
                else:
                    for r in range(AHEAD):
                        bring_index(r, r, 0)
                    with act.Fori(0, WTRIPS) as i:
                        for r in range(RING):
                            bring_index(i * RING + r + AHEAD, (r + AHEAD) % RING, i)
                            place_last_head(i * RING + r, r, i)
                    for r in range(AHEAD):
                        place_last_head(WTRIPS * RING + r, r, WTRIPS)

            @block.gpsimd
            def _(pool):
                def gather(q, r, trip):
                    pool.wait_ge(index_ready, q + 1)
                    pool.sem_inc(index_seen, 1)
                    for a in range(G):
                        for u in range(TPS):
                            pool.indirect_dma_start(rows[:, r, a * TPS + u, :], None, table,
                                                    bass.IndirectOffsetOnAxis(ap=index[:, r, a, u:u + 1], axis=0)
                                                    ).then_inc(rows_in[r], 16)

                loop(pool, gather)

            @block.tensor
            def _(pe):
                def multiply(q, r, trip):
                    s = r % SETS
                    pe.wait_ge(placed_ready, q + 1)
                    if HV < H:
                        pe.wait_ge(last_head_ready, q + 1 + 2)
                    pe.wait_ge(rows_in[r], (trip + 1) * (16 * GT))
                    for a in range(G):
                        pe.wait_ge(added, q * G + a + 1)
                        for b in range(NB):
                            for u in range(TPS):
                                last = nc.tensor.matmul(pM[:, s * G + a, b * W:(b + 1) * W],
                                                        rows[:, r, a * TPS + u, b * P:(b + 1) * P],
                                                        placed[:, s, a * TPS + u, b % H, :], start=(u == 0), stop=(u == TPS - 1))
                        last.then_inc(multiplied, 1)

                loop(pe, multiply)

            @block.vector
            def _(dve):

                def prepare(q, r, trip):
                    s, half = r % SETS, r // SETS
                    dve.wait_ge(multiplied, (q - SETS) * G + G + RING * G)
                    if HV < H:
                        dve.wait_ge(last_head_ready, q + 1)
                    nc.vector.tensor_tensor(hit[:, r % 2, :, :], spread(k["count"][:, 0:W], 1, GT),
                                            spread(k["place"][:, bass.ds(q * G, G), :].rearrange("p g u -> p (g u)"), 2, W),
                                            ALU.is_equal).then_inc(hit_ready, 1)
                    dve.wait_ge(stepw_in[half], 16 * (trip + 1))
                    dve.wait_ge(hit_ready, q + 1)
                    nc.vector.tensor_tensor(placed[:, s, :, 0:HV, :], spread(hit[:, r % 2, :, :], 2, HV),
                                            spread(stepw[:, half, s * GT * H:(s + 1) * GT * H].rearrange("p (g h) -> p g h", h=H)[:, :, 0:HV], 3, W),
                                            ALU.mult).then_inc(placed_ready, 1)

                def add(q, r):
                    for a in range(G):
                        node = dve.value_load(k["offset"][0:1, bass.ds(q * G + a, 1)], min_val=0, max_val=NP - W)
                        dve.wait_ge(multiplied, q * G + a + 1 + RING * G)
                        dve.wait_ge(added, q * G + a + SETS * G)
                        to = acc[:, 0:NB, bass.ds(node, W)]
                        nc.vector.tensor_tensor(to, pM[:, r % SETS * G + a, 0:NB * W].rearrange("p (b w) -> p b w", w=W), to,
                                                ALU.add).then_inc(added, 1)

                for q in range(AHEAD):
                    prepare(q, q, 0)
                with dve.Fori(0, WTRIPS) as i:
                    for r in range(RING):
                        prepare(i * RING + r + AHEAD, (r + AHEAD) % RING, i + (r + AHEAD) // RING)
                        add(i * RING + r, r)
                for r in range(AHEAD):
                    add(WTRIPS * RING + r, r)


def finish_layer1(nc, k, d, acc):
    NB = F1 // P
    with ExitStack() as ctx:
        m = Memory(nc, ctx, "finish1")
        w2 = m.sb("w2", [P, NB, D + 2])
        avec = m.sb("avec", [P, 2, D])
        aprod = m.sb("aprod", [P, NB, D])
        bias = m.sb("bias", [P, NB])
        slope = m.sb("slope", [P, 1])
        diag = m.sb("diag", [P, 2, HEADS1, P])
        norm = m.sb("norm", [P, 2, NB, P])
        pos = m.sb("pos", [P, 2, NB, P])
        neg = m.sb("neg", [P, 2, NB, P])
        z = m.sb("z", [P, 2, NB, P])
        h_out = m.sb("h_out", [P, U, D])
        pR = m.ps("pR", [P, 2, 512])
        pH = m.ps("pH", [P, 2, 512])
        weights_in = m.sem("weights_in")
        weights_ready = m.sem("weights_ready")
        diag_ready = m.sem("diag_ready")
        spread_out = m.sem("spread_out", starts=1)
        normed = m.sem("normed", starts=1)
        pos_ready = m.sem("pos_ready")
        z_ready = m.sem("z_ready", starts=1)
        multiplied = m.sem("multiplied", starts=1)
        h_copied = m.sem("h_copied", starts=1)
        h_stored = [m.sem("h_stored0"), m.sem("h_stored1")]
        h_free = [m.sem("h_free0", starts=1), m.sem("h_free1", starts=1)]
        zero = m.sb("zero", [P, SLOTS * D // P // 30])
        zeros_stored = m.swdge_sem("zeros_stored")
        m.clear_semaphores()
        with nc.Block() as block:

            @block.gpsimd
            def _(pool):
                nc.gpsimd.memset(zero[:, :], 0.0)
                pool.drain()
                for a in range(30):
                    w = SLOTS * D // P // 30
                    pool.dma_start(d["xs"].rearrange("(p s) c -> p (s c)", p=P)[:, a * w:(a + 1) * w], zero[:, :]).then_inc(zeros_stored, 16)
                pool.wait_ge(zeros_stored, 16 * 30)

            @block.sync
            def _(sp):
                loads = [(w2[:, :, 0:D], d["w2"].rearrange("(b p) c -> p b c", p=P)), (avec[:, 0:1, :], d["a_src2"].partition_broadcast(P)),
                         (avec[:, 1:2, :], d["a_dst2"].partition_broadcast(P)), (slope[:, :], d["prelu_w"].partition_broadcast(P))]
                for to, of in loads:
                    sp.dma_start(to, of).then_inc(weights_in, 16)
                sp.dma_start(bias[:, :], d["b1"].rearrange("(b p) -> p b", p=P), allow_slow_non_contiguous=True).then_inc(weights_in, 16)
                with sp.Fori(0, TRIPS) as i:
                    for s, (lo, hi) in enumerate(UPARTS):
                        after(sp, h_copied, i * U + hi)
                        sp.dma_start(d["h2"].rearrange("(t p) c -> p t c", p=P)[:, bass.ds(i * U + lo, hi - lo), :],
                                     h_out[:, lo:hi, :]).then_inc(h_stored[s], 16)
                        sp.wait_ge(h_stored[s], 16 * (i + 1))
                        sp.sem_inc(h_free[s], 1)

            @block.vector
            def _(dve):
                dve.wait_ge(weights_in, 16 * 5)
                for s in range(2):
                    nc.vector.tensor_tensor(aprod[:, :, :], w2[:, :, 0:D], spread(avec[:, s, :], 1, NB), ALU.mult)
                    dve.drain()
                    nc.vector.tensor_reduce(w2[:, :, D + s], aprod[:, :, :], AX_X, ALU.add)
                    dve.drain()
                dve.sem_inc(weights_ready, 1)
                nc.vector.tensor_scalar(slope[:, :], slope[:, :], -1.0, None, ALU.mult)
                dve.drain()

                def diagonal(i, t, j):
                    after(dve, spread_out, i * U + max(j - 1, 0))
                    nc.vector.tensor_tensor(diag[:, j % 2, :, :], spread(k["ident"][:, :], 1, HEADS1),
                                            spread(k["rdenom"][:, t, :], 2, P), ALU.mult).then_inc(diag_ready, 1)

                def normalise(t, j):
                    b = j % 2
                    after(dve, spread_out, t + 1)
                    nc.vector.tensor_tensor(norm[:, b, :, :], acc[:, 0:NB, bass.ds(t * P, P)],
                                            pR[:, b, :].rearrange("p (b n) -> p b n", n=P), ALU.mult)
                    dve.drain()
                    nc.vector.tensor_tensor(norm[:, b, :, :], norm[:, b, :, :], spread(bias[:, :], 2, P), ALU.add).then_inc(normed, 1)

                def prelu(i, t, j):
                    dve.wait_ge(pos_ready, t + 1)
                    after(dve, multiplied, i * U + max(j - 1, 0))
                    nc.vector.scalar_tensor_tensor(out=z[:, j % 2, :, :], in0=neg[:, j % 2, :, :], scalar=slope[:, 0:1],
                                                   in1=pos[:, j % 2, :, :], op0=ALU.mult, op1=ALU.add).then_inc(z_ready, 1)

                with dve.Fori(0, TRIPS) as i:
                    diagonal(i, i * U, 0)
                    for j in range(U):
                        t = i * U + j
                        if j + 1 < U:
                            diagonal(i, t + 1, j + 1)
                        normalise(t, j)
                        if j:
                            prelu(i, t - 1, j - 1)
                    prelu(i, i * U + U - 1, U - 1)

            @block.scalar
            def _(act):
                def parts(i, t, j):
                    after(act, normed, t + 1)
                    after(act, z_ready, i * U + max(j - 1, 0))
                    nc.scalar.activation(pos[:, j % 2, :, :], norm[:, j % 2, :, :], ACT.Relu)
                    nc.scalar.activation(neg[:, j % 2, :, :], norm[:, j % 2, :, :], ACT.Relu, scale=-1.0).then_inc(pos_ready, 1)

                def copy_out(i, t, j):
                    after(act, multiplied, t + 1)
                    act.wait_ge(h_free[part_of(j)], i + 1)
                    nc.scalar.copy(k["attn2"][:, t, :], pH[:, j % 2, D:D + 2])
                    nc.scalar.copy(h_out[:, j, :], pH[:, j % 2, 0:D]).then_inc(h_copied, 1)

                with act.Fori(0, TRIPS) as i:
                    for j in range(U):
                        parts(i, i * U + j, j)
                        if j:
                            copy_out(i, i * U + j - 1, j - 1)
                    copy_out(i, i * U + U - 1, U - 1)

            @block.tensor
            def _(pe):
                pe.wait_ge(weights_ready, 1)

                def spread_norm(i, t, j):
                    pe.wait_ge(diag_ready, t + 1)
                    after(pe, normed, i * U + max(j - 1, 0))
                    nc.tensor.matmul(pR[:, j % 2, :], k["ones"][:, :], diag[:, j % 2, :, :].rearrange("p h n -> p (h n)"),
                                     start=True, stop=True).then_inc(spread_out, 1)

                def multiply(i, t, j):
                    after(pe, z_ready, t + 1)
                    after(pe, h_copied, i * U + max(j - 1, 0))
                    for b in range(NB):
                        last = nc.tensor.matmul(pH[:, j % 2, 0:D + 2], z[:, j % 2, b, :], w2[:, b, :], start=(b == 0), stop=(b == NB - 1))
                    last.then_inc(multiplied, 1)

                with pe.Fori(0, TRIPS) as i:
                    spread_norm(i, i * U, 0)
                    for j in range(U):
                        if j + 1 < U:
                            spread_norm(i, i * U + j + 1, j + 1)
                        if j:
                            multiply(i, i * U + j - 1, j - 1)
                    multiply(i, i * U + U - 1, U - 1)


def finish_layer2(nc, k, d, acc):
    with ExitStack() as ctx:
        m = Memory(nc, ctx, "finish2")
        x1 = m.sb("x1", [P, NT, D])
        y = m.sb("y", [P, NT, D])
        part = m.sb("part", [P, 2, DK, P])
        basein = m.sb("basein", [P, U, D])
        stats = m.sb("stats", [P, NT, 6])
        mean = m.sb("mean", [P, NT])
        half = m.sb("half", [P, NT])
        var = m.sb("var", [P, NT])
        rstd = m.sb("rstd", [P, NT])
        eps = m.sb("eps", [P, 1])
        yT = m.sb("yT", [P, 2, DK, P])
        ycur = m.sb("ycur", [P, 2, D])
        wg = m.sb("wg", [P, DK, NEXP])
        bg = m.sb("bg", [P, NEXP])
        logits = m.sb("logits", [P, NT, NEXP])
        code = m.sb("code", [P, NT, NEXP])
        first = m.sb("first", [P, NT, NEXP])
        second = m.sb("second", [P, NT, NEXP])
        work = m.sb("work", [P, NT, NEXP])
        rank8 = m.sb("rank8", [P, NEXP])
        top = m.sb("top", [P, 2, NT])
        best = m.sb("best", [P, NT])
        valid = m.sb("valid", [P, NT])
        tri = m.sb("tri", [P, P])
        before = m.sb("before", [P, NT, NEXP])
        total = m.sb("total", [P, NT, NEXP])
        ones_row = m.sb("ones_row", [P, NT])
        tiles_i = m.sb("tiles_i", [P, NEXP], I32)
        tiles_f = m.sb("tiles_f", [P, NEXP])
        tile_start = m.sb("tile_start", [P, NEXP])
        expert = m.sb("expert", [1, TT])
        pT = m.ps("pT", [P, 2, 512])
        pG = m.ps("pG", [P, 2, 512])
        pB = m.ps("pB", [P, 512])
        pC = m.ps("pC", [P, 512])
        loads_in = m.sem("loads_in")
        tri_ready = m.sem("tri_ready")
        base_in = m.sem("base_in")
        part_ready = m.sem("part_ready")
        turned = m.sem("turned", starts=1)
        x1_ready = m.sem("x1_ready", starts=1)
        x1_stored = m.sem("x1_stored")
        stats_done = m.sem("stats_done")
        root_done = m.sem("root_done")
        y_ready = m.sem("y_ready")
        y_kept = m.sem("y_kept", starts=1)
        y_turned = m.sem("y_turned", starts=1)
        yT_ready = m.sem("yT_ready")
        gated = m.sem("gated", starts=1)
        logits_ready = m.sem("logits_ready", starts=1)
        gap_ready = m.sem("gap_ready")
        gap_done = m.sem("gap_done")
        chosen = m.sem("chosen")
        counted = m.sem("counted")
        slots_ready = m.sem("slots_ready")
        scattered = m.swdge_sem("scattered")

        m.clear_semaphores()
        with nc.Block() as block:

            @block.sync
            def _(sp):
                sp.dma_start(wg[:, :, :], d["wg"].rearrange("(k p) e -> p k e", p=P)).then_inc(loads_in, 16)
                sp.dma_start(bg[:, :], d["bg"].partition_broadcast(P)).then_inc(loads_in, 16)
                sp.dma_start(valid[:, :], d["valid"]).then_inc(loads_in, 16)
                with sp.Fori(0, TRIPS) as i:
                    after(sp, x1_ready, i * U)
                    sp.dma_start(basein[:, :, :], d["base"].rearrange("(t p) c -> p t c", p=P)[:, bass.ds(i * U, U), :]).then_inc(base_in, 16)
                after(sp, x1_ready, NT)
                sp.dma_start(d["x1"].rearrange("(t p) c -> p t c", p=P), x1[:, :, :]).then_inc(x1_stored, 16)
                sp.wait_ge(x1_stored, 16)

            @block.gpsimd
            def _(pool):
                nc.gpsimd.memset(tri[:, :], 1.0)
                pool.drain()
                nc.gpsimd.affine_select(out=tri[:, :], in_=tri[:, :], compare_op=ALU.is_gt, fill=0.0,
                                        base=0, pattern=[[1, P]], channel_multiplier=-1)
                pool.drain()
                pool.sem_inc(tri_ready, 1)
                pool.wait_ge(slots_ready, 1)
                after(pool, y_kept, NT)
                for s in range(2):
                    for t in range(NT):
                        pool.indirect_dma_start(d["xs"], bass.IndirectOffsetOnAxis(ap=k["slot_out"][:, s, t:t + 1], axis=0),
                                                y[:, t, :], None, bounds_check=SLOTS - 1, oob_is_err=False).then_inc(scattered, 16)
                pool.wait_ge(scattered, 16 * 2 * NT)

            @block.scalar
            def _(act):
                with act.Fori(0, TRIPS) as i:
                    for j in range(U):
                        t = i * U + j
                        after(act, turned, i * U + max(j - 1, 0))
                        nc.scalar.copy(part[:, j % 2, :, :], acc[:, 0:DK, bass.ds(t * P, P)]).then_inc(part_ready, 1)
                act.wait_ge(stats_done, 1)
                nc.scalar.activation(half[:, :], var[:, :], ACT.Sqrt, bias=eps[:, 0:1]).then_inc(root_done, 1)
                with act.Fori(0, TRIPS) as i:
                    for j in range(U):
                        act.wait_ge(y_ready, i * U + j + 1)
                        nc.scalar.copy(y[:, i * U + j, :], ycur[:, j % 2, :]).then_inc(y_kept, 1)
                        after(act, y_turned, i * U + j + 1)
                        after(act, gated, i * U + max(j - 1, 0))
                        nc.scalar.copy(yT[:, j % 2, :, :].rearrange("p k n -> p (k n)"), pT[:, j % 2, 0:D]).then_inc(yT_ready, 1)
                act.wait_ge(gap_ready, 1)
                nc.scalar.activation(best[:, :], best[:, :], ACT.Exp).then_inc(gap_done, 1)

            @block.tensor
            def _(pe):
                with pe.Fori(0, TRIPS) as i:
                    for j in range(U):
                        t = i * U + j
                        pe.wait_ge(part_ready, t + 1)
                        after(pe, x1_ready, i * U + max(j - 1, 0))
                        for kk in range(DK):
                            last = nc.tensor.transpose(pT[:, j % 2, kk * P:(kk + 1) * P], part[:, j % 2, kk, :], k["ident"][:, :])
                        last.then_inc(turned, 1)
                pe.wait_ge(loads_in, 48)

                def turn(i, t, j):
                    pe.wait_ge(y_ready, t + 1)
                    if j >= 2:
                        pe.wait_ge(yT_ready, t - 1)
                    for kk in range(DK):
                        last = nc.tensor.transpose(pT[:, j % 2, kk * P:(kk + 1) * P], ycur[:, j % 2, kk * P:(kk + 1) * P],
                                                   k["ident"][:, :])
                    last.then_inc(y_turned, 1)

                with pe.Fori(0, TRIPS) as i:
                    turn(i, i * U, 0)
                    for j in range(U):
                        t = i * U + j
                        if j + 1 < U:
                            turn(i, t + 1, j + 1)
                        pe.wait_ge(yT_ready, t + 1)
                        after(pe, logits_ready, i * U + max(j - 1, 0))
                        for kk in range(DK):
                            last = nc.tensor.matmul(pG[:, j % 2, 0:NEXP], yT[:, j % 2, kk, :], wg[:, kk, :],
                                                    start=(kk == 0), stop=(kk == 1))
                        last.then_inc(gated, 1)
                pe.wait_ge(tri_ready, 1)
                pe.wait_ge(chosen, 1)
                nc.tensor.matmul(pB[:, 0:NT * NEXP], tri[:, :], work[:, :, :].rearrange("p t e -> p (t e)"), start=True, stop=True)
                nc.tensor.matmul(pC[:, 0:NT * NEXP], k["ones"][:, :], work[:, :, :].rearrange("p t e -> p (t e)"),
                                 start=True, stop=True).then_inc(counted, 1)

            @block.vector
            def _(dve):
                nc.vector.memset(eps[:, :], EPS)
                nc.vector.memset(ones_row[:, :], 1.0)
                with dve.Fori(0, TRIPS) as i:
                    dve.wait_ge(base_in, 16 * (i + 1))
                    for j in range(U):
                        t = i * U + j
                        after(dve, turned, t + 1)
                        nc.vector.scalar_tensor_tensor(out=x1[:, t, :], in0=pT[:, j % 2, 0:D], scalar=k["rdenom"][:, t, 0:1],
                                                       in1=basein[:, j, :], op0=ALU.mult, op1=ALU.add).then_inc(x1_ready, 1)
                dve.drain()
                with dve.Fori(0, NT) as t:
                    nc.vector.bn_stats(stats[:, t, :], x1[:, t, :])
                dve.drain()
                nc.vector.tensor_tensor(mean[:, :], stats[:, :, 1], stats[:, :, 4], ALU.add)
                nc.vector.tensor_tensor(half[:, :], stats[:, :, 1], stats[:, :, 4], ALU.subtract)
                nc.vector.tensor_tensor(var[:, :], stats[:, :, 2], stats[:, :, 5], ALU.add)
                dve.drain()
                nc.vector.tensor_scalar(mean[:, :], mean[:, :], 0.5, None, ALU.mult)
                nc.vector.tensor_tensor(half[:, :], half[:, :], half[:, :], ALU.mult)
                nc.vector.tensor_scalar(var[:, :], var[:, :], 1.0 / D, None, ALU.mult)
                dve.drain()
                nc.vector.scalar_tensor_tensor(out=var[:, :], in0=half[:, :], scalar=0.25, in1=var[:, :],
                                               op0=ALU.mult, op1=ALU.add).then_inc(stats_done, 1)
                dve.wait_ge(root_done, 1)
                newton(nc, dve, rstd, half, var)
                dve.wait_ge(loads_in, 48)

                def norm(i, t, j):
                    after(dve, y_turned, i * U + max(j - 1, 0))
                    after(dve, y_kept, i * U + max(j - 1, 0))
                    nc.vector.tensor_scalar(ycur[:, j % 2, :], x1[:, t, :], mean[:, bass.ds(t, 1)], rstd[:, bass.ds(t, 1)],
                                            ALU.subtract, ALU.mult).then_inc(y_ready, 1)

                with dve.Fori(0, TRIPS) as i:
                    norm(i, i * U, 0)
                    norm(i, i * U + 1, 1)
                    for j in range(U):
                        t = i * U + j
                        if j + 2 < U:
                            norm(i, t + 2, j + 2)
                        after(dve, gated, t + 1)
                        nc.vector.tensor_tensor(logits[:, t, :], pG[:, j % 2, 0:NEXP], bg[:, :], ALU.add).then_inc(logits_ready, 1)
                dve.drain()
                nc.vector.tensor_scalar(rank8[:, :], k["count"][:, 0:NEXP], -1.0, float(NEXP), ALU.mult, ALU.add)
                dve.drain()
                for s, to in enumerate((first, second)):
                    nc.vector.tensor_reduce(top[:, s, :], logits[:, :, :], AX_X, ALU.max)
                    dve.drain()
                    nc.vector.tensor_tensor(code[:, :, :], logits[:, :, :], spread(top[:, s, :], 2, NEXP), ALU.is_equal)
                    dve.drain()
                    nc.vector.tensor_tensor(code[:, :, :], code[:, :, :], spread(rank8[:, :], 1, NT), ALU.mult)
                    dve.drain()
                    nc.vector.tensor_reduce(best[:, :], code[:, :, :], AX_X, ALU.max)
                    dve.drain()
                    nc.vector.tensor_tensor(to[:, :, :], code[:, :, :], spread(best[:, :], 2, NEXP), ALU.is_equal)
                    dve.drain()
                    if s == 0:
                        nc.vector.scalar_tensor_tensor(out=logits[:, :, :], in0=to[:, :, :], scalar=-BIG, in1=logits[:, :, :],
                                                       op0=ALU.mult, op1=ALU.add)
                        dve.drain()
                nc.vector.tensor_tensor(best[:, :], top[:, 1, :], top[:, 0, :], ALU.subtract).then_inc(gap_ready, 1)
                nc.vector.tensor_tensor(work[:, :, :], first[:, :, :], second[:, :, :], ALU.add)
                dve.drain()
                nc.vector.tensor_tensor(work[:, :, :], work[:, :, :], spread(valid[:, :], 2, NEXP), ALU.mult).then_inc(chosen, 1)
                dve.wait_ge(gap_done, 1)
                nc.vector.tensor_scalar(half[:, :], best[:, :], 1.0, None, ALU.add)
                dve.drain()
                nc.vector.reciprocal(k["mix_weight"][:, 0, :], half[:, :])
                dve.drain()
                nc.vector.tensor_tensor(k["mix_weight"][:, 1, :], k["mix_weight"][:, 0, :], best[:, :], ALU.mult)
                dve.wait_ge(counted, 1)
                nc.vector.tensor_copy(code[:, :, :].rearrange("p t e -> p (t e)"), pC[:, 0:NT * NEXP])
                nc.vector.tensor_copy(before[:, :, :].rearrange("p t e -> p (t e)"), pB[:, 0:NT * NEXP])
                dve.drain()
                for e in range(NEXP):
                    nc.vector.tensor_tensor_scan(total[:, :, e], ones_row[:, :], code[:, :, e], 0.0, ALU.mult, ALU.add)
                dve.drain()
                nc.vector.tensor_scalar(tiles_f[:, :], total[:, NT - 1, :], float(P - 1), None, ALU.add)
                nc.vector.tensor_tensor(before[:, :, :], before[:, :, :], total[:, :, :], ALU.add)
                dve.drain()
                nc.vector.tensor_tensor(before[:, :, :], before[:, :, :], code[:, :, :], ALU.subtract)
                nc.vector.tensor_copy(tiles_i[:, :], tiles_f[:, :])
                dve.drain()
                nc.vector.tensor_scalar(tiles_i[:, :], tiles_i[:, :], 7, None, ALU.arith_shift_right)
                dve.drain()
                nc.vector.tensor_copy(tiles_f[:, :], tiles_i[:, :])
                dve.drain()
                nc.vector.tensor_tensor_scan(tile_start[:, :], ones_row[:, 0:NEXP], tiles_f[:, :], 0.0, ALU.mult, ALU.add)
                dve.drain()
                nc.vector.tensor_tensor(tile_start[:, :], tile_start[:, :], tiles_f[:, :], ALU.subtract)
                dve.drain()
                nc.vector.scalar_tensor_tensor(out=before[:, :, :], in0=spread(tile_start[:, :], 1, NT), scalar=float(P),
                                               in1=before[:, :, :], op0=ALU.mult, op1=ALU.add)
                nc.vector.memset(expert[:, :], 0.0)
                nc.vector.tensor_scalar(half[:, :], valid[:, :], -float(OUT_OF_RANGE), float(OUT_OF_RANGE), ALU.mult, ALU.add)
                dve.drain()
                for s, of in enumerate((first, second)):
                    nc.vector.tensor_tensor(code[:, :, :], of[:, :, :], before[:, :, :], ALU.mult)
                    dve.drain()
                    nc.vector.tensor_reduce(mean[:, :], code[:, :, :], AX_X, ALU.add)
                    dve.drain()
                    nc.vector.tensor_tensor(mean[:, :], mean[:, :], half[:, :], ALU.add)
                    dve.drain()
                    nc.vector.tensor_copy(k["slot_out"][:, s, :], mean[:, :])
                    nc.vector.tensor_scalar(var[:, :], mean[:, :], float(SLOTS - 1), None, ALU.min)
                    dve.drain()
                    nc.vector.tensor_copy(k["slot_in"][:, s, :], var[:, :])
                dve.drain()
                dve.sem_inc(slots_ready, 1)
                for e in range(1, NEXP):
                    nc.vector.scalar_tensor_tensor(out=expert[:, :], in0=k["count"][0:1, 0:TT], scalar=tile_start[0:1, e:e + 1],
                                                   in1=expert[:, :], op0=ALU.is_ge, op1=ALU.add)
                    dve.drain()
                nc.vector.tensor_copy(k["expert"][:, :], expert[:, :])


def newton(nc, dve, rstd, root, var):
    nc.vector.reciprocal(rstd[:, :], root[:, :])
    nc.vector.tensor_scalar(var[:, :], var[:, :], EPS, None, ALU.add)
    dve.drain()
    nc.vector.tensor_tensor(root[:, :], rstd[:, :], rstd[:, :], ALU.mult)
    dve.drain()
    nc.vector.tensor_tensor(root[:, :], root[:, :], var[:, :], ALU.mult)
    dve.drain()
    nc.vector.tensor_scalar(root[:, :], root[:, :], -0.5, 1.5, ALU.mult, ALU.add)
    dve.drain()
    nc.vector.tensor_tensor(rstd[:, :], rstd[:, :], root[:, :], ALU.mult)
    dve.drain()


def expert_pass(nc, k, d):
    HC = HID // P
    RX = 3
    SX = 5
    UE = RX * SX
    ETRIPS = TT // UE
    assert ETRIPS * UE == TT
    with ExitStack() as ctx:
        m = Memory(nc, ctx, "expert")
        w1 = m.sb("w1", [P, NEXP, DK, HID])
        w2 = m.sb("w2", [P, NEXP, HC, D])
        b1 = m.sb("b1", [P, NEXP, HC])
        b2 = m.sb("b2", [P, NEXP, D])
        xin = m.sb("xin", [P, SX, D])
        xT = m.sb("xT", [P, RX, DK, P])
        pre = m.sb("pre", [P, HID])
        hT = m.sb("hT", [P, HC, P])
        out = m.sb("out", [P, SX, D])
        pX = m.ps("pX", [P, 512])
        pH = m.ps("pH", [P, 2, 512])
        pG = m.ps("pG", [P, HC, P])
        pO = m.ps("pO", [P, RX, 512])
        bias_in = m.sem("bias_in")
        weights_in = [m.swdge_sem("w1_in"), m.swdge_sem("w2_in")]
        experts_in = m.sem("experts_in")
        x_in = [m.sem(f"x_in{j}") for j in range(SX)]
        x_turned = m.sem("x_turned", starts=SX)
        xT_ready = m.sem("xT_ready", starts=1)
        up_done = m.sem("up_done", starts=RX)
        pre_ready = m.sem("pre_ready", starts=1)
        pre_turned = m.sem("pre_turned")
        h_ready = m.sem("h_ready")
        down_done = m.sem("down_done")
        out_ready = m.sem("out_ready", starts=RX)
        out_free = m.sem("out_free", starts=SX)
        out_stored = [m.swdge_sem(f"out_stored{j}") for j in range(SX)]

        def loop(eng, body):
            with eng.Fori(0, ETRIPS - 1) as i:
                for j in range(UE):
                    body(i, j)
            for j in range(UE):
                body(ETRIPS - 1, j)

        def later(i, j, n):
            i, j = i + (j + n) // UE, (j + n) % UE
            return None if isinstance(i, int) and i == ETRIPS else (i, j)

        m.clear_semaphores()
        with nc.Block() as block:

            @block.sync
            def _(sp):
                sp.dma_start(b1[:, :, :], d["fb1_t"]).then_inc(bias_in, 16)
                sp.dma_start(b2[:, :, :], d["fb2"].partition_broadcast(P)).then_inc(bias_in, 16)

                def load_tokens(i, j):
                    t = i * UE + j
                    sp.wait_ge(x_turned, t + 1)
                    sp.dma_start(xin[:, j % SX, :], d["xs"][bass.ds(t * P, P), :]).then_inc(x_in[j % SX], 16)

                loop(sp, load_tokens)

            @block.scalar
            def _(act):
                act.wait_ge(bias_in, 32)

                def gelu(i, j):
                    t = i * UE + j
                    e = act.value_load(k["expert"][0:1, bass.ds(t, 1)], min_val=0, max_val=NEXP - 1)
                    act.wait_ge(pre_turned, t + 1)
                    for c in range(HC):
                        nc.scalar.activation(hT[:, c, :], pG[:, c, :], ACT.Gelu, bias=b1[:, e, c:c + 1]).then_inc(h_ready, 1)

                loop(act, gelu)

            @block.vector
            def _(dve):
                dve.wait_ge(bias_in, 32)

                def copy_tokens(i, j):
                    t = i * UE + j
                    dve.wait_ge(x_turned, t + 1 + SX)
                    dve.wait_ge(up_done, t + 1)
                    nc.vector.tensor_copy(xT[:, j % RX, :, :].rearrange("p k n -> p (k n)"), pX[:, 0:D]).then_inc(xT_ready, 1)

                def copy_pre(i, j):
                    t = i * UE + j
                    dve.wait_ge(up_done, t + 1 + RX)
                    nc.vector.tensor_copy(pre[:, :], pH[:, :, :].rearrange("p a b -> p (a b)")).then_inc(pre_ready, 1)

                def take_out(i, j):
                    t = i * UE + j
                    e = dve.value_load(k["expert"][0:1, bass.ds(t, 1)], min_val=0, max_val=NEXP - 1)
                    dve.wait_ge(out_free, t + 1)
                    dve.wait_ge(down_done, t + 1)
                    nc.vector.tensor_tensor(out[:, j % SX, :], pO[:, j % RX, 0:D], b2[:, e, :], ALU.add).then_inc(out_ready, 1)

                def follow(i, j):
                    if later(i, j, 1):
                        copy_pre(*later(i, j, 1))
                    if later(i, j, 2):
                        copy_tokens(*later(i, j, 2))
                    take_out(i, j)

                copy_tokens(0, 0)
                copy_pre(0, 0)
                copy_tokens(0, 1)
                loop(dve, follow)

            @block.tensor
            def _(pe):
                def turn_tokens(i, j):
                    t = i * UE + j
                    pe.wait_ge(x_in[j % SX], 16 * (i * RX + j // SX + 1))
                    after(pe, xT_ready, t)
                    for kk in range(DK):
                        last = nc.tensor.transpose(pX[:, kk * P:(kk + 1) * P], xin[:, j % SX, kk * P:(kk + 1) * P], k["ident"][:, :])
                    last.then_inc(x_turned, 1)

                def up(i, j):
                    t = i * UE + j
                    e = pe.value_load(k["expert"][0:1, bass.ds(t, 1)], min_val=0, max_val=NEXP - 1)
                    pe.wait_ge(experts_in, e + 1)
                    after(pe, xT_ready, t + 1)
                    after(pe, pre_ready, t)
                    for a in range(2):
                        for kk in range(DK):
                            last = nc.tensor.matmul(pH[:, a, :], xT[:, j % RX, kk, :], w1[:, e, kk, a * 512:(a + 1) * 512],
                                                    start=(kk == 0), stop=(kk == 1))
                    last.then_inc(up_done, 1)

                def turn(i, j):
                    after(pe, pre_ready, i * UE + j + 1)
                    for c in range(HC):
                        last = nc.tensor.transpose(pG[:, c, :], pre[:, c * P:(c + 1) * P], k["ident"][:, :])
                    last.then_inc(pre_turned, 1)

                def down(i, j):
                    t = i * UE + j
                    e = pe.value_load(k["expert"][0:1, bass.ds(t, 1)], min_val=0, max_val=NEXP - 1)
                    pe.wait_ge(out_ready, t + 1)
                    for c in range(HC):
                        pe.wait_ge(h_ready, t * HC + c + 1)
                        last = nc.tensor.matmul(pO[:, j % RX, 0:D], hT[:, c, :], w2[:, e, c, :], start=(c == 0), stop=(c == HC - 1))
                    last.then_inc(down_done, 1)

                def tile(i, j):
                    if later(i, j, 1):
                        up(*later(i, j, 1))
                    if later(i, j, 2):
                        turn_tokens(*later(i, j, 2))
                    down(i, j)
                    if later(i, j, 1):
                        turn(*later(i, j, 1))

                turn_tokens(0, 0)
                up(0, 0)
                turn_tokens(0, 1)
                turn(0, 0)
                loop(pe, tile)

            @block.gpsimd
            def _(pool):
                for e in range(NEXP):
                    pool.dma_start(w1[:, e, :, :], d["fw1"][e].rearrange("(k p) h -> p k h", p=P)).then_inc(weights_in[0], 16)
                    pool.dma_start(w2[:, e, :, :], d["fw2"][e].rearrange("(c p) o -> p c o", p=P)).then_inc(weights_in[1], 16)
                    pool.wait_ge(weights_in[0], 16 * (e + 1))
                    pool.wait_ge(weights_in[1], 16 * (e + 1))
                    pool.sem_inc(experts_in, 1)

                def store_rows(i, j):
                    t = i * UE + j
                    pool.wait_ge(out_ready, t + 1 + RX)
                    pool.dma_start(d["ys"][bass.ds(t * P, P), :], out[:, j % SX, :]).then_inc(out_stored[j % SX], 16)
                    pool.wait_ge(out_stored[j % SX], 16 * (i * RX + j // SX + 1))
                    pool.sem_inc(out_free, 1)

                loop(pool, store_rows)
                for j in range(SX):
                    pool.wait_ge(out_stored[j], 16 * ETRIPS * RX)


def combine_pass(nc, k, d):
    with ExitStack() as ctx:
        m = Memory(nc, ctx, "combine")
        x1 = m.sb("x1", [P, 2, U, D])
        rows = m.sb("rows", [P, 2, 2, U, D])
        x_in = [m.sem("x_in0"), m.sem("x_in1")]
        rows_in = [m.swdge_sem("rows_in0"), m.swdge_sem("rows_in1")]
        out_ready = m.sem("out_ready")
        out_stored = [m.sem("out_stored0"), m.sem("out_stored1")]
        m.clear_semaphores()
        with nc.Block() as block:

            @block.gpsimd
            def _(pool):
                for i in range(TRIPS):
                    if i >= 2:
                        pool.wait_ge(out_ready, i - 1)
                    for j in range(U):
                        for s in range(2):
                            pool.indirect_dma_start(rows[:, i % 2, s, j, :], None, d["ys"],
                                                    bass.IndirectOffsetOnAxis(ap=k["slot_in"][:, s, i * U + j:i * U + j + 1], axis=0)
                                                    ).then_inc(rows_in[i % 2], 16)

            @block.sync
            def _(sp):
                for i in range(TRIPS):
                    if i >= 2:
                        sp.wait_ge(out_stored[i % 2], 16 * (i // 2) if i < TRIPS else 0)
                    sp.dma_start(x1[:, i % 2, :, :], d["x1"].rearrange("(t p) c -> p t c", p=P)[:, i * U:(i + 1) * U, :]).then_inc(x_in[i % 2], 16)

            @block.scalar
            def _(act):
                for i in range(TRIPS):
                    act.wait_ge(out_ready, i + 1)
                    if i < TRIPS - 1:
                        act.dma_start(d["out"][i * U * P:(i + 1) * U * P, :].rearrange("(t p) c -> p t c", p=P),
                                      x1[:, i % 2, :, :]).then_inc(out_stored[i % 2], 16)
                    else:
                        act.dma_start(d["out"][i * U * P:(NT - 1) * P, :].rearrange("(t p) c -> p t c", p=P),
                                      x1[:, i % 2, 0:U - 1, :]).then_inc(out_stored[i % 2], 16)
                        act.dma_start(d["out"][(NT - 1) * P:N, :], x1[0:LAST, i % 2, U - 1, :]).then_inc(out_stored[i % 2], 16)
                act.wait_ge(out_stored[0], 16 * 5)
                act.wait_ge(out_stored[1], 16 * 3)

            @block.vector
            def _(dve):
                for i in range(TRIPS):
                    dve.wait_ge(x_in[i % 2], 16 * (i // 2 + 1))
                    dve.wait_ge(rows_in[i % 2], 16 * 2 * U * (i // 2 + 1))
                    for s in range(2):
                        for j in range(U):
                            t = i * U + j
                            last = nc.vector.scalar_tensor_tensor(out=x1[:, i % 2, j, :], in0=rows[:, i % 2, s, j, :],
                                                                  scalar=k["mix_weight"][:, s, t:t + 1], in1=x1[:, i % 2, j, :],
                                                                  op0=ALU.mult, op1=ALU.add)
                        dve.drain()
                    dve.sem_inc(out_ready, 1)


def build_program(nc, d, until=99):
    with ExitStack() as ctx:
        Memory.program = ctx
        m = Memory(nc, ctx, "all")
        k = dict(
            ident=m.sb("ident", [P, P]), ones=m.sb("ones", [P, P]), node_i=m.sb("node_i", [P, NT], I32),
            count_i=m.sb("count_i", [P, P], I32), node=m.sb("node", [P, NT]), count=m.sb("count", [P, P]),
            attn1=m.sb("attn1", [P, NT, 2 * HEADS1]), attn2=m.sb("attn2", [P, NT, 2]),
            tiles_leq=m.sb("tiles_leq", [P, NT]), no_edges=m.sb("no_edges", [P, NT]), last_i=m.sb("last_i", [P, NT], I32),
            start_i=m.sb("start_i", [P, NT], I32), etile_i=m.sb("etile_i", [P, SJ], I32),
            offset=m.sb("offset", [1, SP], I32), src_step=m.sb("src_step", [P, SP, TPS], I32),
            place=m.sb("place", [P, SP, TPS]), self_weight=m.sb("self_weight", [P, NT, HEADS1]),
            rdenom=m.sb("rdenom", [P, NT, HEADS1]), slot_out=m.sb("slot_out", [P, 2, NT], I32),
            slot_in=m.sb("slot_in", [P, 2, NT], I32), mix_weight=m.sb("mix_weight", [P, 2, NT]),
            expert=m.sb("expert", [1, TT], I32))

        def scratch(name, shape, dt=F32):
            return nc.dram_tensor(f"s_{name}", shape, dt, kind="Internal").ap()

        d["h1"] = scratch("h1", [NP, F1])
        d["base"] = scratch("base", [NP, D])
        constants(nc, k)
        d["offsets"] = scratch("offsets", [SP], I32)
        if until != 2:
            node_pass(nc, k, d)
        edge_pass(nc, k, d)
        d["spread"], d["scanned"], d["weights"], d["sums"], d["step_weights"] = {}, {}, {}, {}, {}
        d["terms"] = scratch("terms", [NP, HEADS1])
        for H in (HEADS1, 1):
            d["spread"][H] = scratch(f"spread{H}", [EP, 2 * H])
            d["scanned"][H] = scratch(f"scanned{H}", [EP, H])
            d["weights"][H] = scratch(f"weights{H}", [EP, H])
            d["sums"][H] = scratch(f"sums{H}", [EP, H])
            d["step_weights"][H] = scratch(f"step_weights{H}", [P, SP * TPS * H])
        d["h2"] = scratch("h2", [NP, D])
        d["xs"] = scratch("xs", [SLOTS, D])
        attention_pass(nc, k, d, 1, HEADS1, k["attn1"])
        weight_table(nc, k, d, 1, HEADS1)
        with nc.sbuf_tensor("acc1", [P, F1 // P, NP], F32) as acc:
            self_messages(nc, k, d, 1, HEADS1, F1, acc, d["h1"])
            message_pass(nc, k, d, 1, HEADS1, F1, acc, d["h1"])
            finish_layer1(nc, k, d, acc)
        attention_pass(nc, k, d, 2, 1, k["attn2"])
        weight_table(nc, k, d, 2, 1)
        d["x1"] = scratch("x1", [NP, D])
        d["ys"] = scratch("ys", [SLOTS, D])
        with nc.sbuf_tensor("acc2", [P, DK, NP], F32) as acc:
            self_messages(nc, k, d, 2, 1, D, acc, d["h2"])
            message_pass(nc, k, d, 2, 1, D, acc, d["h2"])
            finish_layer2(nc, k, d, acc)
        expert_pass(nc, k, d)
        combine_pass(nc, k, d)


def lay_out(inputs):
    import numpy as np

    g = {n: np.asarray(v) for n, v in inputs.items()}
    dst, src = g["dst"].astype(np.int32, copy=False), g["src"].astype(np.int32, copy=False)
    pad = EP - EDGES
    dst_ext = np.concatenate([np.full(1, -1, np.int32), dst, np.full(pad, N, np.int32)])
    src_pad = np.concatenate([src, np.zeros(pad, np.int32)])
    valid = np.ones((P, NT), np.float32)
    valid[LAST:, NT - 1] = 0.0
    c = np.ascontiguousarray
    return {
        "x": np.concatenate([g["x"], np.zeros((NP - N, D), np.float32)]),
        "src": c(src_pad), "dst": c(dst_ext[1:]), "dst_ext": c(dst_ext), "valid": valid,
        "w1": c(g["L0_gnn_W1"]), "a_src1": c(g["L0_gnn_a_src1"]), "a_dst1": c(g["L0_gnn_a_dst1"]),
        "b1": c(g["L0_gnn_b1"]), "prelu_w": c(g["L0_gnn_prelu_w"].reshape(1)), "w2": c(g["L0_gnn_W2"]),
        "a_src2": c(g["L0_gnn_a_src2"]), "a_dst2": c(g["L0_gnn_a_dst2"]), "b2": c(g["L0_gnn_b2"]),
        "wq": c(g["L0_mix_wq"]), "wk_t": c(g["L0_mix_wk"].T), "wv_t": c(g["L0_mix_wv"].T),
        "wo_t": c(g["L0_mix_wo"].T), "bo": c(g["L0_mix_bo"]),
        "ln_k_g": c(g["L0_mix_ln_k_g"]), "ln_k_b": c(g["L0_mix_ln_k_b"]),
        "ln_v_g": c(g["L0_mix_ln_v_g"]), "ln_v_b": c(g["L0_mix_ln_v_b"]),
        "wg": c(g["L0_ffn_Wg"]), "bg": c(g["L0_ffn_bg"]), "fw1": c(g["L0_ffn_W1"]), "fb1_t": c(g["L0_ffn_b1"].reshape(NEXP, HID // P, P).transpose(2, 0, 1)),
        "fw2": c(g["L0_ffn_W2"]), "fb2": c(g["L0_ffn_b2"]),
    }


def kernel(**inputs):
    import numpy as np
    import concourse.bacc as bacc
    from concourse.bass_utils import run_bass_kernel_spmd

    nc = bacc.Bacc("TRN2", target_bir_lowering=False, num_devices=1)
    arrays = {f"in_{n}_dram": a for n, a in lay_out(inputs).items()}
    d = {n[3:-5]: nc.dram_tensor(n, a.shape, mybir.dt.from_np(a.dtype), kind="ExternalInput").ap()
         for n, a in arrays.items()}
    d["out"] = nc.dram_tensor("out_dram", (N, D), F32, kind="ExternalOutput").ap()
    build_program(nc, d)
    return np.asarray(run_bass_kernel_spmd(nc, [arrays], core_ids=[0]).results[0]["out_dram"])
```
